# Optimizing a Trainium2 kernel written in Bass

```python
import numpy as np
import jax
import jax.numpy as jnp

def _softmax(x, axis=-1):
    return jax.nn.softmax(x, axis=axis)

def _gelu(x):
    return jax.nn.gelu(x, approximate=True)

def _silu(x):
    return jax.nn.silu(x)

def _sigmoid(x):
    return jax.nn.sigmoid(x)

def _layernorm(x, axis=-1, eps=1e-05):
    m = jnp.mean(x, axis=axis, keepdims=True)
    v = jnp.var(x, axis=axis, keepdims=True)
    return (x - m) / jnp.sqrt(v + eps)

def _scatter_add(tgt, idx, src, axis=0):
    return tgt.at[idx].add(src)

def _segment_sum(src, seg, n):
    return jax.ops.segment_sum(src, seg, n)
kernel_name = 'mk_hybrid_d1_jaxref_r8_a8eea0'

def setup_inputs(seed: int=0):
    np.random.seed(seed)
    _w = jnp.asarray

    def _L0_attn_a_setup():
        import jax, jax.numpy as jnp
        import numpy as np
        DIM = 128
        N_HEADS = 16
        HEAD_DIM = DIM // N_HEADS

        def apply_rope(x):
            T, D = (x.shape[-2], x.shape[-1])
            half = D // 2
            theta = 10000.0 ** (-jnp.arange(half, dtype=jnp.float32) / half)
            pos = jnp.arange(T, dtype=jnp.float32)
            freqs = pos[:, None] * theta[None, :]
            cos, sin = (jnp.cos(freqs), jnp.sin(freqs))
            x1 = x[..., :half]
            q = half // 2
            rot = jnp.concatenate([-x1[..., q:], x1[..., :q]], axis=-1)
            x_rot = x1 * cos + rot * sin
            return jnp.concatenate([x_rot, x[..., half:]], axis=-1)
        key = jax.random.key(seed)
        ks = jax.random.split(key, 9)
        B, T = (2, 256)
        s = 0.02
        return {'x': jax.random.normal(ks[0], (B, T, DIM), dtype=jnp.float32), 'Wq': jax.random.normal(ks[1], (DIM, DIM), dtype=jnp.float32) * s, 'bq': jnp.zeros((DIM,), dtype=jnp.float32), 'Wk': jax.random.normal(ks[2], (DIM, HEAD_DIM), dtype=jnp.float32) * s, 'bk': jnp.zeros((HEAD_DIM,), dtype=jnp.float32), 'Wv': jax.random.normal(ks[3], (DIM, HEAD_DIM), dtype=jnp.float32) * s, 'bv': jnp.zeros((HEAD_DIM,), dtype=jnp.float32), 'Wo': jax.random.normal(ks[4], (DIM, DIM), dtype=jnp.float32) * s, 'bo': jnp.zeros((DIM,), dtype=jnp.float32)}
    _L0_attn_a_in = _L0_attn_a_setup()

    def _L0_attn_b_setup():
        import jax, jax.numpy as jnp
        import numpy as np
        B, T, D, P, ALPHA, PR = (4, 512, 128, 64, 4, 64)
        key = jax.random.key(seed)
        ks = jax.random.split(key, 9)
        g = lambda k, shape, scale: jax.random.normal(k, shape, jnp.float32) * scale
        return {'x': jax.random.normal(ks[0], (B, T, D), jnp.float32), 'W_toP': g(ks[1], (D, P), D ** (-0.5)), 'W_U': g(ks[2], (D, P, ALPHA), D ** (-0.5)), 'W_F': g(ks[3], (D, P), D ** (-0.5)), 'W_V': g(ks[4], (P, ALPHA), 1.0), 'W_lam': g(ks[5], (P, PR), P ** (-0.5)), 'B_mat': g(ks[6], (P, PR), P ** (-0.5)), 'C_mat': g(ks[7], (PR, P), PR ** (-0.5)), 'W_fromP': g(ks[8], (P, D), P ** (-0.5))}
    _L0_attn_b_in = _L0_attn_b_setup()

    def _L0_ffn_setup():
        import jax, jax.numpy as jnp
        import numpy as np
        import math
        HID, HD, E, MIN_E = (128, 128, 16, 2)
        B, T = (4, 256)
        IS_CAUSAL = True

        def _l2norm(x, axis):
            return x / jnp.sqrt(jnp.sum(x * x, axis=axis, keepdims=True) + 1e-12)

        def _gating(hidden_states, sim_matrix, gates):
            b, t, c = hidden_states.shape
            flat = hidden_states.reshape(b * t, c)
            logits = _l2norm(flat, -1) @ _l2norm(sim_matrix, 0) - jax.nn.sigmoid(gates)
            gated = jax.nn.relu(logits)
            mask = (gated > 0).astype(gated.dtype)
            inactive = jnp.sum(mask, axis=1) == 0
            _, top_idx = jax.lax.top_k(logits, MIN_E)
            fb = jnp.sum(jax.nn.one_hot(top_idx, E, dtype=mask.dtype), axis=1)
            mask = mask + inactive[:, None].astype(mask.dtype) * fb
            masked = jnp.where(mask > 0, gated, -jnp.inf)
            probs = jax.nn.softmax(masked, axis=-1)
            return probs
        key = jax.random.key(seed)
        ks = jax.random.split(key, 6)
        a_qkv = math.sqrt(6.0 / (HID + HD))
        a_o = math.sqrt(6.0 / (HD + HID))
        return {'hidden_states': jax.random.normal(ks[0], (B, T, HID), jnp.float32), 'sim_matrix': jax.random.normal(ks[1], (HID, E), jnp.float32), 'gates': jnp.zeros((E,), jnp.float32), 'q_proj': jax.random.uniform(ks[2], (E, HID, HD), jnp.float32, -a_qkv, a_qkv), 'k_proj': jax.random.uniform(ks[3], (E, HID, HD), jnp.float32, -a_qkv, a_qkv), 'v_proj': jax.random.uniform(ks[4], (E, HID, HD), jnp.float32, -a_qkv, a_qkv), 'o_proj': jax.random.uniform(ks[5], (E, HD, HID), jnp.float32, -a_o, a_o)}
    _L0_ffn_in = _L0_ffn_setup()
    _d = {'L0_attn_a_x': _L0_attn_a_in['x'], 'L0_attn_a_Wq': _L0_attn_a_in['Wq'], 'L0_attn_a_bq': _L0_attn_a_in['bq'], 'L0_attn_a_Wk': _L0_attn_a_in['Wk'], 'L0_attn_a_bk': _L0_attn_a_in['bk'], 'L0_attn_a_Wv': _L0_attn_a_in['Wv'], 'L0_attn_a_bv': _L0_attn_a_in['bv'], 'L0_attn_a_Wo': _L0_attn_a_in['Wo'], 'L0_attn_a_bo': _L0_attn_a_in['bo'], 'L0_attn_b_W_toP': _L0_attn_b_in['W_toP'], 'L0_attn_b_W_U': _L0_attn_b_in['W_U'], 'L0_attn_b_W_F': _L0_attn_b_in['W_F'], 'L0_attn_b_W_V': _L0_attn_b_in['W_V'], 'L0_attn_b_W_lam': _L0_attn_b_in['W_lam'], 'L0_attn_b_B_mat': _L0_attn_b_in['B_mat'], 'L0_attn_b_C_mat': _L0_attn_b_in['C_mat'], 'L0_attn_b_W_fromP': _L0_attn_b_in['W_fromP'], 'L0_ffn_sim_matrix': _L0_ffn_in['sim_matrix'], 'L0_ffn_gates': _L0_ffn_in['gates'], 'L0_ffn_q_proj': _L0_ffn_in['q_proj'], 'L0_ffn_k_proj': _L0_ffn_in['k_proj'], 'L0_ffn_v_proj': _L0_ffn_in['v_proj'], 'L0_ffn_o_proj': _L0_ffn_in['o_proj']}
    _x0 = _d['L0_attn_a_x']
    _d['L0_attn_a_x'] = jax.random.normal(jax.random.fold_in(jax.random.key(seed), 1), (1, 2048, 128), dtype=_x0.dtype)
    del _x0
    return _d

def reference(L0_attn_a_x, L0_attn_a_Wq, L0_attn_a_bq, L0_attn_a_Wk, L0_attn_a_bk, L0_attn_a_Wv, L0_attn_a_bv, L0_attn_a_Wo, L0_attn_a_bo, L0_attn_b_W_toP, L0_attn_b_W_U, L0_attn_b_W_F, L0_attn_b_W_V, L0_attn_b_W_lam, L0_attn_b_B_mat, L0_attn_b_C_mat, L0_attn_b_W_fromP, L0_ffn_sim_matrix, L0_ffn_gates, L0_ffn_q_proj, L0_ffn_k_proj, L0_ffn_v_proj, L0_ffn_o_proj):

    def _L0_attn_a_ref(x, Wq, bq, Wk, bk, Wv, bv, Wo, bo):
        import jax, jax.numpy as jnp
        import numpy as np
        DIM = 128
        N_HEADS = 16
        HEAD_DIM = DIM // N_HEADS

        def apply_rope(x):
            T, D = (x.shape[-2], x.shape[-1])
            half = D // 2
            theta = 10000.0 ** (-jnp.arange(half, dtype=jnp.float32) / half)
            pos = jnp.arange(T, dtype=jnp.float32)
            freqs = pos[:, None] * theta[None, :]
            cos, sin = (jnp.cos(freqs), jnp.sin(freqs))
            x1 = x[..., :half]
            q = half // 2
            rot = jnp.concatenate([-x1[..., q:], x1[..., :q]], axis=-1)
            x_rot = x1 * cos + rot * sin
            return jnp.concatenate([x_rot, x[..., half:]], axis=-1)
        B, T, C = x.shape
        H, D = (N_HEADS, HEAD_DIM)
        q = (x @ Wq + bq).reshape(B, T, H, D).transpose(0, 2, 1, 3)
        k = x @ Wk + bk
        v = x @ Wv + bv
        q = apply_rope(q)
        k = apply_rope(k)
        att = jnp.einsum('bhqd,bkd->bhqk', q, k) / jnp.sqrt(jnp.float32(D))
        causal = jnp.tril(jnp.ones((T, T), dtype=bool))
        att = jnp.where(causal[None, None], att, jnp.float32(-jnp.inf))
        att = jax.nn.softmax(att, axis=-1)
        out = jnp.einsum('bhqk,bkd->bhqd', att, v)
        out = out.transpose(0, 2, 1, 3).reshape(B, T, C)
        return out @ Wo + bo

    def _L0_attn_b_ref(x, W_toP, W_U, W_F, W_V, W_lam, B_mat, C_mat, W_fromP):
        import jax, jax.numpy as jnp
        import numpy as np
        B, T, D, P, ALPHA, PR = (4, 512, 128, 64, 4, 64)
        pre = jnp.einsum('btd,dp->btp', x, W_toP)
        U = jnp.einsum('btd,dpa->btpa', x, W_U)
        Fg = jax.nn.sigmoid(jnp.einsum('btd,dp->btp', x, W_F))
        Y = U * W_V
        t = Y.sum(-1) + pre
        lam = jax.nn.sigmoid(jnp.einsum('btp,pr->btr', Fg, W_lam))
        u_in = jnp.einsum('btp,pr->btr', t, B_mat)

        def step(s, inp):
            l, u = inp
            s = l * s + u
            return (s, s)
        s0 = jnp.zeros((x.shape[0], PR), x.dtype)
        _, s_seq = jax.lax.scan(step, s0, (lam.transpose(1, 0, 2), u_in.transpose(1, 0, 2)))
        s_seq = s_seq.transpose(1, 0, 2)
        t_tilde = t + jnp.einsum('btr,rp->btp', s_seq, C_mat)
        h = jnp.einsum('btp,pd->btd', t_tilde, W_fromP)
        return h

    def _L0_ffn_ref(hidden_states, sim_matrix, gates, q_proj, k_proj, v_proj, o_proj):
        import jax, jax.numpy as jnp
        import numpy as np
        import math
        HID, HD, E, MIN_E = (128, 128, 16, 2)
        B, T = (4, 256)
        IS_CAUSAL = True

        def _l2norm(x, axis):
            return x / jnp.sqrt(jnp.sum(x * x, axis=axis, keepdims=True) + 1e-12)

        def _gating(hidden_states, sim_matrix, gates):
            b, t, c = hidden_states.shape
            flat = hidden_states.reshape(b * t, c)
            logits = _l2norm(flat, -1) @ _l2norm(sim_matrix, 0) - jax.nn.sigmoid(gates)
            gated = jax.nn.relu(logits)
            mask = (gated > 0).astype(gated.dtype)
            inactive = jnp.sum(mask, axis=1) == 0
            _, top_idx = jax.lax.top_k(logits, MIN_E)
            fb = jnp.sum(jax.nn.one_hot(top_idx, E, dtype=mask.dtype), axis=1)
            mask = mask + inactive[:, None].astype(mask.dtype) * fb
            masked = jnp.where(mask > 0, gated, -jnp.inf)
            probs = jax.nn.softmax(masked, axis=-1)
            return probs
        b, t, c = hidden_states.shape
        rw = _gating(hidden_states, sim_matrix, gates).reshape(b, t, E)
        q = jnp.einsum('btc,ech,bte->bth', hidden_states, q_proj, rw)
        k = jnp.einsum('btc,ech,bte->bth', hidden_states, k_proj, rw)
        v = jnp.einsum('btc,ech,bte->bth', hidden_states, v_proj, rw)
        scale = 1.0 / math.sqrt(HD)
        scores = jnp.einsum('bqh,bkh->bqk', q, k) * scale
        if IS_CAUSAL:
            causal = jnp.tril(jnp.ones((t, t), dtype=bool))
            scores = jnp.where(causal[None], scores, -jnp.inf)
        attn = jax.nn.softmax(scores, axis=-1)
        ao = jnp.einsum('bqk,bkh->bqh', attn, v)
        out = jnp.einsum('bth,ehc,bte->btc', ao, o_proj, rw)
        return out
    x = L0_attn_a_x
    x = x + _L0_attn_a_ref(_layernorm(x, axis=-1), L0_attn_a_Wq, L0_attn_a_bq, L0_attn_a_Wk, L0_attn_a_bk, L0_attn_a_Wv, L0_attn_a_bv, L0_attn_a_Wo, L0_attn_a_bo)
    x = x + _L0_ffn_ref(_layernorm(x, axis=-1), L0_ffn_sim_matrix, L0_ffn_gates, L0_ffn_q_proj, L0_ffn_k_proj, L0_ffn_v_proj, L0_ffn_o_proj)
    x = x + _L0_attn_b_ref(_layernorm(x, axis=-1), L0_attn_b_W_toP, L0_attn_b_W_U, L0_attn_b_W_F, L0_attn_b_W_V, L0_attn_b_W_lam, L0_attn_b_B_mat, L0_attn_b_C_mat, L0_attn_b_W_fromP)
    x = x + _L0_ffn_ref(_layernorm(x, axis=-1), L0_ffn_sim_matrix, L0_ffn_gates, L0_ffn_q_proj, L0_ffn_k_proj, L0_ffn_v_proj, L0_ffn_o_proj)
    return x

_drawn_inputs = setup_inputs


def setup_inputs(seed=0):
    import zlib

    import numpy as np

    out = dict(_drawn_inputs(seed))
    spreads = {'L0_attn_a_bq': (0.0, 0.8),
     'L0_attn_a_bk': (0.0, 0.8),
     'L0_attn_a_bv': (0.0, 0.1),
     'L0_attn_a_bo': (0.0, 0.1),
     'L0_ffn_gates': (0.0, 0.1)}
    factors = {'L0_attn_a_Wq': 8.0,
     'L0_attn_a_Wk': 8.0,
     'L0_attn_a_Wv': 8.0,
     'L0_ffn_q_proj': 3.395,
     'L0_ffn_k_proj': 3.399}
    for name, (base, spread) in spreads.items():
        noise = np.random.default_rng([zlib.crc32(name.encode()), seed]).standard_normal(out[name].shape)
        drawn = base * np.exp(spread * noise) if base else spread * noise
        out[name] = jnp.asarray(drawn.astype(out[name].dtype))
    for name, factor in factors.items():
        out[name] = (out[name] * factor).astype(out[name].dtype)
    return out
```

```python
from contextlib import ExitStack

import concourse.bass as bass
from concourse import mybir

F32 = mybir.dt.float32
BF16 = mybir.dt.bfloat16
U32 = mybir.dt.uint32
ALU = mybir.AluOpType
ACT = mybir.ActivationFunctionType
AX_X = mybir.AxisListType.X

P = 128
T = 2048
D = 128
NT = T // P
GT = 4
GN = GT * P
NG = NT // GT
H = 16
HD = D // H
HH = HD // 2
HB = 4
E = 16
PR = 64
ALPHA = 4
EPS = 1e-5
NORM_EPS = 1e-12
SCALE_A = float(HD) ** -0.5
SCALE_F = float(D) ** -0.5
MASKED = -1e30
PARTS = 3
QK_ROWS = PARTS * PARTS * HD
SHIFT_ROW = 96
QK_PAD = SHIFT_ROW
ST_ROWS = SHIFT_ROW + PARTS
MX_RING, ST_RING, P_RING, XS_RING, PT_RING = 3, 3, 8, 3, 4
STAGE_A, STAGE_F0, STAGE_B, STAGE_F1 = range(4)


class Uses:

    def __init__(self, keys, slots=1):
        self.at = {key: n for n, key in enumerate(keys)}
        self.keys = keys
        self.slots = slots

    def n(self, *key):
        return self.at[key]

    def before(self, *key):
        n = self.at[key] - self.slots
        return self.keys[n] if n >= 0 else None

    def slot(self, *key):
        return self.at[key] % self.slots


def max_units(i):
    nb = i + 1
    if nb <= GT:
        nh = GT // nb
        return [(h, min(nh, H - h), 0, nb) for h in range(0, H, nh)]
    pieces = -(-nb // GT)
    cuts = [nb * c // pieces for c in range(pieces + 1)]
    return [(h, 1, cuts[c], cuts[c + 1] - cuts[c]) for h in range(H) for c in range(pieces)]


def max_pieces(i):
    return max(1, -(-(i + 1) // GT))


def slot_plan(i):
    slots = HB * (i + 1)
    if i + 1 >= NT:
        return [[] for _ in range(slots)]
    units = max_units(i + 1)
    busy = max(1, (slots * 7) // 8)
    cuts = [min(len(units), -(-len(units) * k // busy)) for k in range(slots + 1)]
    return [list(range(cuts[k], cuts[k + 1])) for k in range(slots)]


def finish_slots(i):
    last = HB * (i + 1) - 1
    return [min(5, last), min(9, last), min(13, last)]


def misc_order():
    out = []

    def prep(g):
        out.extend([("xT", STAGE_A, g), ("proj", g, 0), ("proj", g, 1), ("kT", g)])

    prep(0)
    prep(1)
    out.extend([("sim",), ("qT", 0, 0), ("qT", 0, 1), ("shift", 0, 0), ("shift", 0, 1)])
    for i in range(NT):
        if i % GT == 0 and 0 < i // GT < NG - 1:
            prep(i // GT + 1)
        if i + 1 < NT:
            out.extend([("qT", i + 1, 0), ("qT", i + 1, 1)])
        if i > 0:
            out.extend([("oT", i - 1), ("attT", i - 1), ("wo", i - 1)])
        if i + 1 < NT:
            out.extend([("shift", i + 1, 0), ("shift", i + 1, 1)])
    out.extend([("oT", NT - 1), ("attT", NT - 1), ("wo", NT - 1)])
    for s in (STAGE_F0, STAGE_B, STAGE_F1):
        if s == STAGE_B:
            for g in range(NG):
                out.extend([("xT", s, g), ("h", g)])
            continue
        for g in range(NG):
            out.extend([("xT", s, g), ("logit", s, g), ("rT", s, g), ("v", s, g)])
        for g in range(NG):
            for i in range(GT * g, GT * g + GT):
                out.append(("aoT", s, i))
            out.append(("ffn", s, g))
    return out


def pair_order():
    out = []
    for s in (STAGE_F0, STAGE_F1):
        for g in range(NG):
            for i in range(GT * g, GT * g + GT):
                out.extend(("pT", s, i, c) for c in range(i // GT + 1))
            out.extend(("rb", s, g, e) for e in range(E))
    return out


def hybrid_block_kernel(nc, x, Wq, bq, Wk, bk, Wv, bv, Wo, bo, W_toP, W_U, W_F, W_V, W_lam, B_mat,
                        C_mat, W_fromP, sim, gates, q_proj, k_proj, v_proj, o_proj, cos, sin, out):
    MISC = Uses(misc_order())
    PAIR = Uses(pair_order(), 2)
    BASE = [i * (i + 1) // 2 for i in range(NT + 1)]
    MX_BASE = [sum(len(max_units(a)) for a in range(i)) for i in range(NT + 1)]

    def st_n(i, slot):
        return HB * BASE[i] + slot

    def xs_n(layer, out_side, g, e):
        return ((layer * 2 + out_side) * NG + g) * E + e

    def pT_n(layer, i, c):
        before = [a // GT + 1 for a in range(NT)]
        return sum(before) * layer + sum(before[:i]) + c

    def weighed(layer, i):
        return pT_n(layer, i, i // GT) + 1

    def x_new_n(stage, g):
        return GT * (g + 1) if stage == STAGE_A else NT + NG * (stage - 1) + g + 1

    with ExitStack() as ctx:
        def sb(name, shape, dt=F32):
            return ctx.enter_context(nc.sbuf_tensor(name, shape, dt))

        def sem(name):
            return ctx.enter_context(nc.semaphore(name))

        X = sb("X", [P, NT, D])
        xn = sb("xn", [P, NT, D])
        xnT = sb("xnT", [P, T])
        stats = sb("stats", [P, GT, 6])
        mean_var = sb("mean_var", [P, NT, 2])
        var_eps = sb("var_eps", [P, NT])
        rstd = sb("rstd", [P, NT])
        minus_half = sb("minus_half", [P, E])
        w_qkv = sb("w_qkv", [P, D + 2 * HD])
        b_qkv = sb("b_qkv", [P, D + 2 * HD])
        w_o = sb("w_o", [P, D])
        b_o = sb("b_o", [P, D])
        cos_t = sb("cos_t", [P, NT, HH])
        sin_t = sb("sin_t", [P, NT, HH])
        qkv = sb("qkv", [P, GT, D + 2 * HD])
        turn_c = sb("turn_c", [P, GT, H + 1, HH])
        turn_s = sb("turn_s", [P, GT, H + 1, HH])
        rest = sb("rest", [P, GT, H + 1, HD])
        q_parts = sb("q_parts", [P, 2 * GT, H, QK_PAD], BF16)
        k_parts = sb("k_parts", [P, GT, P], BF16)
        v_ones = sb("v_ones", [P, NT, 32])
        kT = sb("kT", [P, T], BF16)
        qT = sb("qT", [P, 2, H * P], BF16)
        m_part = sb("m_part", [P, H, GT])
        m = sb("m", [P, H])
        m_rest = sb("m_rest", [P, 2, H])
        m_parts = sb("m_parts", [P, 2, H, 4], BF16)
        probs = sb("probs", [P, P_RING, GN])
        o_sb = sb("o_sb", [P, GN])
        den = sb("den", [P, HB, HB])
        att = sb("att", [P, 2, D])
        attT = sb("attT", [P, D])
        wo_out = sb("wo_out", [P, D])
        fw = {name: sb(f"w_expert_{name}", [P, E, D]) for name in "qkvo"}
        sim_sb = sb("sim_sb", [P, E])
        sim_sq = sb("sim_sq", [P, E])
        sim_n = sb("sim_n", [P, E])
        gate_sig = sb("gate_sig", [P, E])
        expert_no = sb("expert_no", [P, E])
        sq_sum = sb("sq_sum", [P, NT])
        sq_junk = sb("sq_junk", [P, GT, D])
        x_inv = sb("x_inv", [P, NT])
        logits = sb("logits", [P, GT, E])
        top = sb("top", [P, GT, 8])
        top_no = sb("top_no", [P, GT, 8], U32)
        top_nof = sb("top_nof", [P, GT, 2])
        pick = sb("pick", [P, 2, GT, E])
        on = sb("on", [P, GT, E])
        gtmp = sb("gtmp", [P, GT, E])
        gexp = sb("gexp", [P, GT, E])
        gcol = sb("gcol", [P, 3, GT])
        rw = sb("rw", [P, GT, E])
        rw_rest = sb("rw_rest", [P, GT, E])
        rw_parts = sb("rw_parts", [P, GT, PARTS, E], BF16)
        rwT = sb("rwT", [PARTS * E, T], BF16)
        spread = sb("spread", [PARTS * E, E, P], BF16)
        xs = sb("xs", [P, XS_RING, GN])
        fqT = sb("fqT", [P, T])
        fkT = sb("fkT", [P, T])
        fvT = sb("fvT", [P, GN])
        fv = sb("fv", [P, NT, D])
        fm = sb("fm", [P, NT])
        f_shift = sb("f_shift", [P, NT])
        f_sum = sb("f_sum", [P, NT])
        f_inv = sb("f_inv", [P, NT])
        fp = probs[:, :, :].rearrange("p (a b) n -> p a (b n)", a=2)
        pT = sb("pT", [P, PT_RING, GN])
        ao = sb("ao", [P, 2, D])
        aoT = sb("aoT", [P, T])
        outT = sb("outT", [P, GN])
        w_tf = sb("w_tf", [P, P])
        w_u = sb("w_u", [P, PR, ALPHA])
        w_v = sb("w_v", [P, PR, ALPHA])
        w_uv = sb("w_uv", [P, PR])
        w_lam = sb("w_lam", [P, PR])
        w_b = sb("w_b", [PR, PR])
        w_c = sb("w_c", [PR, PR])
        w_p = sb("w_p", [PR, D])
        tT = sb("tT", [PR, GN])
        fg = sb("fg", [P, 2, GN])
        lam = sb("lam", [PR, 2, GN])
        s_seq = aoT[0:PR, :]
        tt = outT[0:PR, :]
        ident = sb("ident", [P, P])
        ident_b = sb("ident_b", [P, P], BF16)
        mask_b = sb("mask_b", [P, P], BF16)
        ones = sb("ones", [P, P])
        psum = ctx.enter_context(nc.psum_tensor("psum", [P, 8 * GN], F32))

        def bank(n):
            return psum[:, GN * n:GN * n + GN]

        def mx_bank(n):
            return bank(n % MX_RING)

        def st_bank(n):
            return bank(MX_RING + n % ST_RING)

        def pair_bank(key):
            return bank(4 + PAIR.slot(*key))

        misc = bank(7)
        misc_b = misc.bitcast(BF16)

        x_loaded = [sem(f"x_loaded{g}") for g in range(NG)]
        tab_loaded, a_loaded, b_loaded = sem("tab_loaded"), sem("a_loaded"), sem("b_loaded")
        f_loaded = sem("f_loaded")
        consts = sem("consts")
        pool_step, dve_step = sem("pool_step"), sem("dve_step")
        x_new = sem("x_new")
        var_ready, rstd_ready, xn_ready, xnT_ready = (
            sem(n) for n in ("var_ready", "rstd_ready", "xn_ready", "xnT_ready"))
        sq_ready, x_inv_ready = sem("sq_ready"), sem("x_inv_ready")
        misc_ready = sem("misc_ready")
        sim_sq_ready, sim_var, sim_pow, sim_ready = (
            sem(n) for n in ("sim_sq_ready", "sim_var", "sim_pow", "sim_ready"))
        gates_exp = sem("gates_exp")
        proj_copied, kparts_ready, kT_ready, qparts_ready, qT_ready = (
            sem(n) for n in ("proj_copied", "kparts_ready", "kT_ready", "qparts_ready", "qT_ready"))
        mx_ready, mx_free, m_ready = sem("mx_ready"), sem("mx_free"), sem("m_ready")
        shift_set = [sem(f"shift_set{half}") for half in range(2)]
        st_ready, probs_ready, pv_done, o_copied = (
            sem(n) for n in ("st_ready", "probs_ready", "pv_done", "o_copied"))
        att_ready, attT_ready, wo_copied = sem("att_ready"), sem("attT_ready"), sem("wo_copied")
        logit_copied, gate_arg, gate_exp, rparts_ready, rwT_ready = (
            sem(n) for n in ("logit_copied", "gate_arg", "gate_exp", "rparts_ready", "rwT_ready"))
        rb_ready, xs_ready, xs_used = sem("rb_ready"), sem("xs_ready"), sem("xs_used")
        fqkv_copied, fv_ready = sem("fqkv_copied"), sem("fv_ready")
        fs_ready, fshift_ready, fprobs_ready = (
            sem(n) for n in ("fs_ready", "fshift_ready", "fprobs_ready"))
        pT_filled = sem("pT_filled")
        pT_copied = [sem(f"pT_copied{n}") for n in range(2)]
        pT_used = sem("pT_used")
        ao_ready, aoT_ready, outT_ready = sem("ao_ready"), sem("aoT_ready"), sem("outT_ready")
        wtf_ready, tf_ready, fg_exp, fg_ready, t_ready = (
            sem(n) for n in ("wtf_ready", "tf_ready", "fg_exp", "fg_ready", "t_ready"))
        lu_ready, lam_exp, s_ready, c_ready, tt_ready = (
            sem(n) for n in ("lu_ready", "lam_exp", "s_ready", "c_ready", "tt_ready"))
        stored = sem("stored")

        def misc_copied(kind, *at):
            if kind == "sim":
                return sim_var, 1
            if kind == "xT":
                return xnT_ready, NG * at[0] + at[1] + 1
            if kind == "proj":
                return proj_copied, 2 * at[0] + at[1] + 1
            if kind == "kT":
                return kT_ready, at[0] + 1
            if kind == "qT":
                return qT_ready, 2 * at[0] + at[1] + 1
            if kind == "shift":
                return shift_set[at[1]], at[0] + 1
            if kind == "oT":
                return att_ready, at[0] + 1
            if kind == "attT":
                return attT_ready, at[0] + 1
            if kind == "wo":
                return wo_copied, at[0] + 1
            if kind == "h":
                return x_new, x_new_n(STAGE_B, at[0])
            layer = int(at[0] == STAGE_F1)
            if kind == "ffn":
                return x_new, x_new_n(at[0], at[1])
            if kind == "aoT":
                return aoT_ready, NT * layer + at[1] + 1
            by_group = {"logit": logit_copied, "rT": rwT_ready, "v": fv_ready}
            return by_group[kind], NG * layer + at[1] + 1

        def pT_copies(key):
            own = PAIR.keys[PAIR.slot(*key)::2][:PAIR.n(*key) // 2 + 1]
            return sum(k[0] == "pT" for k in own)

        block = ctx.enter_context(nc.Block())

        @block.sync
        def _(sp):
            xv = x.rearrange("b (n p) d -> p (b n) d", p=P)
            ov = out.rearrange("b (n p) d -> p (b n) d", p=P)
            for g in range(NG):
                sp.dma_start(X[:, GT * g:GT * g + GT, :], xv[:, GT * g:GT * g + GT, :]).then_inc(x_loaded[g], 16)
            for w, src in (("q", q_proj), ("k", k_proj), ("v", v_proj), ("o", o_proj)):
                sp.dma_start(fw[w][:, :, :], src.rearrange("e c h -> c e h")).then_inc(f_loaded, 16)
            for g in range(NG):
                sp.wait_ge(x_new, x_new_n(STAGE_F1, g))
                sp.dma_start(ov[:, GT * g:GT * g + GT, :], X[:, GT * g:GT * g + GT, :]).then_inc(stored, 16)
            sp.wait_ge(stored, 16 * NG)

        @block.gpsimd
        def _(pool):
            steps = [0]

            def after(ins):
                steps[0] += 1
                ins.then_inc(pool_step, 1)
                pool.wait_ge(pool_step, steps[0])

            after(pool.memset(ident[:, :], 0.0))
            after(pool.affine_select(out=ident[:, :], in_=ident[:, :], compare_op=ALU.not_equal, fill=1.0,
                                     base=0, pattern=[[-1, P]], channel_multiplier=1))
            pool.tensor_copy(ident_b[:, :], ident[:, :]).then_inc(consts, 1)
            after(pool.memset(minus_half[:, :], -0.5))

            def inverse_roots(stage, g):
                a, b = GT * g, GT * g + GT
                pool.wait_ge(var_ready, NG * stage + g + 1)
                pool.tensor_tensor(rstd[:, a:b], var_eps[:, a:b], minus_half[:, 0:GT], ALU.pow).then_inc(rstd_ready, 1)
                if stage in (STAGE_F0, STAGE_F1):
                    n = g + (NG if stage == STAGE_F1 else 0)
                    pool.wait_ge(sq_ready, n + 1)
                    pool.tensor_tensor(x_inv[:, a:b], sq_sum[:, a:b], minus_half[:, 0:GT], ALU.pow).then_inc(x_inv_ready, 1)

            inverse_roots(STAGE_A, 0)
            pool.memset(ones[:, :], 1.0).then_inc(consts, 1)
            after(pool.memset(mask_b[:, :], 0.0))
            pool.affine_select(out=mask_b[:, :], in_=mask_b[:, :], compare_op=ALU.is_ge, fill=MASKED,
                               base=0, pattern=[[-1, P]], channel_multiplier=1).then_inc(consts, 1)
            inverse_roots(STAGE_A, 1)
            pool.dma_start(w_tf[:, 0:PR], W_toP).then_inc(b_loaded, 16)
            pool.dma_start(w_tf[:, PR:P], W_F).then_inc(b_loaded, 16)
            pool.dma_start(w_u[:, :, :], W_U).then_inc(b_loaded, 16)
            pool.dma_start(w_v[:, :, :], W_V.rearrange("(o p) a -> o p a", o=1).broadcast_to([P, PR, ALPHA])).then_inc(b_loaded, 16)
            pool.dma_start(w_lam[PR:P, :], W_lam).then_inc(b_loaded, 16)
            pool.dma_start(w_b[:, :], B_mat).then_inc(b_loaded, 16)
            pool.dma_start(w_c[:, :], C_mat).then_inc(b_loaded, 16)
            pool.dma_start(w_p[:, :], W_fromP).then_inc(b_loaded, 16)
            pool.iota(expert_no[:, :], pattern=[[1, E]], base=0, channel_multiplier=0,
                      allow_small_or_imprecise_dtypes=True).then_inc(consts, 1)
            after(pool.memset(spread[:, :, :], 0.0))
            for part in range(PARTS):
                after(pool.affine_select(out=spread[:, :, :], in_=spread[:, :, :], compare_op=ALU.not_equal,
                                         fill=1.0, base=-E * part, pattern=[[-1, E], [0, P]],
                                         channel_multiplier=1))
            pool.wait_ge(sim_var, 1)
            pool.tensor_tensor(sim_sq[:, :], sim_sq[:, :], minus_half[:, :], ALU.pow).then_inc(sim_pow, 1)
            for g in range(2, NG):
                inverse_roots(STAGE_A, g)
            for stage in (STAGE_F0, STAGE_B, STAGE_F1):
                for g in range(NG):
                    inverse_roots(stage, g)

        @block.scalar
        def _(act):
            act.dma_start(w_qkv[:, 0:D], Wq).then_inc(a_loaded, 16)
            act.dma_start(w_qkv[:, D:D + HD], Wk).then_inc(a_loaded, 16)
            act.dma_start(w_qkv[:, D + HD:D + 2 * HD], Wv).then_inc(a_loaded, 16)
            for lo, n, b in ((0, D, bq), (D, HD, bk), (D + HD, HD, bv)):
                act.dma_start(b_qkv[:, lo:lo + n], b.rearrange("(o n) -> o n", o=1).broadcast_to([P, n])).then_inc(tab_loaded, 16)
            act.dma_start(cos_t[:, :, :], cos.rearrange("(n p) c -> p n c", p=P)).then_inc(tab_loaded, 16)
            act.dma_start(sin_t[:, :, :], sin.rearrange("(n p) c -> p n c", p=P)).then_inc(tab_loaded, 16)
            act.dma_start(b_o[:, :], bo.rearrange("(o n) -> o n", o=1).broadcast_to([P, D])).then_inc(tab_loaded, 16)
            act.dma_start(sim_sb[:, :], sim).then_inc(tab_loaded, 16)
            act.dma_start(gate_sig[:, :], gates.rearrange("(o n) -> o n", o=1).broadcast_to([P, E])).then_inc(tab_loaded, 16)
            act.dma_start(w_o[:, :], Wo).then_inc(a_loaded, 16)

            def take(*key):
                act.wait_ge(misc_ready, MISC.n(*key) + 1)

            def xT_copy(stage, g):
                take("xT", stage, g)
                act.activation(xnT[:, GN * g:GN * g + GN], misc, ACT.Copy).then_inc(xnT_ready, 1)

            def prep(g):
                xT_copy(STAGE_A, g)
                take("kT", g)
                act.activation(kT[0:ST_ROWS, GN * g:GN * g + GN], misc_b[0:ST_ROWS, 0:GN], ACT.Copy).then_inc(kT_ready, 1)

            def q_copies(i):
                if i >= 2:
                    act.wait_ge(st_ready, st_n(i - 1, 0))
                for half in range(2):
                    take("qT", i, half)
                    act.activation(qT[0:QK_PAD, i % 2, 1024 * half:1024 * half + 1024], misc_b[0:QK_PAD, :],
                                   ACT.Copy).then_inc(qT_ready, 1)

            def shift_copy(i):
                take("shift", i, 0)
                act.activation(qT[SHIFT_ROW:ST_ROWS, i % 2, 0:1024], misc_b[SHIFT_ROW:ST_ROWS, :],
                               ACT.Copy).then_inc(shift_set[0], 1)

            def exp_a(i, slot):
                n = st_n(i, slot)
                act.wait_ge(st_ready, n + 1)
                if n >= P_RING:
                    act.wait_ge(pv_done, (n - P_RING) // HB + 1)
                act.activation(probs[:, n % P_RING, :], st_bank(n), ACT.Exp, scale=SCALE_A).then_inc(probs_ready, 1)

            def sums_copy(i):
                act.wait_ge(pv_done, BASE[i + 1])
                act.activation(o_sb[:, :], bank(6), ACT.Copy).then_inc(o_copied, 1)

            def attT_copy(i):
                take("attT", i)
                act.activation(attT[:, :], misc[:, 0:D], ACT.Copy).then_inc(attT_ready, 1)

            act.wait_ge(tab_loaded, 16 * 8)
            act.activation(gate_sig[:, :], gate_sig[:, :], ACT.Exp, scale=-1.0).then_inc(gates_exp, 1)
            prep(0)
            prep(1)
            q_copies(0)
            shift_copy(0)
            for i in range(NT):
                if i % GT == 0 and 0 < i // GT < NG - 1:
                    prep(i // GT + 1)
                if i + 1 < NT:
                    q_copies(i + 1)
                for slot in range(HB * (i + 1)):
                    exp_a(i, slot)
                    if i > 0 and slot == HB - 1:
                        sums_copy(i - 1)
                    if i > 0 and slot == finish_slots(i)[1]:
                        attT_copy(i - 1)
                if i + 1 < NT:
                    shift_copy(i + 1)
            sums_copy(NT - 1)
            attT_copy(NT - 1)

            def gate_and_project(stage, layer, g):
                n = NG * layer + g
                xT_copy(stage, g)
                act.wait_ge(gate_arg, n + 1)
                act.activation(gexp[:, :, :], gtmp[:, :, :], ACT.Exp).then_inc(gate_exp, 1)
                take("rT", stage, g)
                act.activation(rwT[:, GN * g:GN * g + GN], misc_b[0:PARTS * E, 0:GN], ACT.Copy).then_inc(rwT_ready, 1)
                act.wait_ge(xs_used, xs_n(layer, 0, g, E - 1) + 1)
                act.activation(fvT[:, :], bank(5), ACT.Copy).then_inc(fqkv_copied, 1)
                act.activation(fqT[:, GN * g:GN * g + GN], bank(3), ACT.Copy).then_inc(fqkv_copied, 1)
                act.activation(fkT[:, GN * g:GN * g + GN], bank(4), ACT.Copy).then_inc(fqkv_copied, 1)
                take("v", stage, g)
                act.activation(fv[:, GT * g:GT * g + GT, :].rearrange("p a b -> p (a b)"), misc,
                               ACT.Copy).then_inc(fv_ready, 1)

            def exp_f(layer, i):
                n = NT * layer + i
                act.wait_ge(fshift_ready, n + 1)
                if n >= 2:
                    act.wait_ge(pT_used, weighed((n - 2) // NT, (n - 2) % NT))
                act.activation(fp[:, i % 2, 0:P * (i + 1)], psum[:, 0:P * (i + 1)], ACT.Exp,
                               bias=f_shift[:, i:i + 1], scale=SCALE_F, accum_out=f_sum[:, i:i + 1])\
                    .then_inc(fprobs_ready, 1)

            def pT_copy(stage, layer, i, c):
                n, key = pT_n(layer, i, c), ("pT", stage, i, c)
                w = P * min(GT, i + 1 - GT * c)
                act.wait_ge(pT_filled, n + 1)
                if n >= PT_RING:
                    act.wait_ge(pT_used, n - PT_RING + 1)
                act.activation(pT[:, n % PT_RING, 0:w], pair_bank(key)[:, 0:w], ACT.Copy)\
                    .then_inc(pT_copied[PAIR.slot(*key)], 1)

            def expert_attention(stage, layer):
                for g in range(NG):
                    gate_and_project(stage, layer, g)
                exp_f(layer, 0)
                for g in range(NG):
                    for i in range(GT * g, GT * g + GT):
                        if i + 1 < NT:
                            exp_f(layer, i + 1)
                        for c in range(1, i // GT + 1, 2):
                            pT_copy(stage, layer, i, c)
                        take("aoT", stage, i)
                        act.activation(aoT[:, P * i:P * i + P], misc[:, 0:P], ACT.Copy).then_inc(aoT_ready, 1)
                    act.wait_ge(xs_used, xs_n(layer, 1, g, E - 1) + 1)
                    act.activation(outT[:, :], bank(6), ACT.Copy).then_inc(outT_ready, 1)

            def scan(g):
                xT_copy(STAGE_B, g)
                act.wait_ge(tf_ready, g + 1)
                act.activation(fg[PR:P, 0, :], bank(0)[PR:P, :], ACT.Exp, scale=-1.0).then_inc(fg_exp, 1)
                act.activation(tT[:, :], bank(0)[0:PR, :], ACT.Copy).then_inc(t_ready, 1)
                act.wait_ge(lu_ready, g + 1)
                act.activation(lam[:, 0, :], bank(1)[0:PR, :], ACT.Exp, scale=-1.0).then_inc(lam_exp, 1)

            expert_attention(STAGE_F0, 0)
            for g in range(NG):
                scan(g)
            expert_attention(STAGE_F1, 1)

        @block.tensor
        def _(pe):
            def fill(*key):
                last = MISC.before(*key)
                if last:
                    pe.wait_ge(*misc_copied(*last))

            def transposes(key, into, pieces, identity):
                fill(*key)
                for o, src in zip(into, pieces):
                    last = pe.transpose(o, src, identity)
                last.then_inc(misc_ready, 1)

            def xT(stage, g):
                pe.wait_ge(xn_ready, NG * stage + g + 1)
                transposes(("xT", stage, g), [misc[:, P * a:P * a + P] for a in range(GT)],
                           [xn[:, GT * g + a, :] for a in range(GT)], ident[:, :])

            def prep(g):
                xT(STAGE_A, g)
                pe.wait_ge(xnT_ready, g + 1)
                w = D + 2 * HD
                for half in range(2):
                    fill("proj", g, half)
                    for a in range(2):
                        t = GT * g + 2 * half + a
                        last = pe.matmul(misc[:, w * a:w * a + w], xnT[:, P * t:P * t + P], w_qkv[:, :],
                                         start=True, stop=True)
                    last.then_inc(misc_ready, 1)
                pe.wait_ge(kparts_ready, g + 1)
                transposes(("kT", g), [misc_b[0:ST_ROWS, P * a:P * a + P] for a in range(GT)],
                           [k_parts[:, a, 0:ST_ROWS] for a in range(GT)], ident_b[:, :])

            def q_transposes(i):
                pe.wait_ge(qparts_ready, i // GT + 1)
                for half in range(2):
                    transposes(("qT", i, half), [misc_b[0:QK_PAD, P * a:P * a + P] for a in range(8)],
                               [q_parts[:, i % (2 * GT), 8 * half + a, :] for a in range(8)], ident_b[:, :])

            def max_scores(i, u):
                h0, nh, k0, nk = max_units(i)[u]
                n = MX_BASE[i] + u
                w = nk * P
                if u == 0:
                    pe.wait_ge(qT_ready, 2 * (i + 1))
                    pe.wait_ge(kT_ready, i // GT + 1)
                if n >= MX_RING:
                    pe.wait_ge(mx_free, n - MX_RING + 1)
                diagonal = k0 + nk == i + 1
                for a in range(nh):
                    h = h0 + a
                    last = pe.matmul(mx_bank(n)[:, w * a:w * a + w], qT[0:QK_PAD, i % 2, P * h:P * h + P],
                                     kT[0:QK_PAD, P * k0:P * k0 + w], start=True, stop=True)
                    if diagonal:
                        last = pe.matmul(mx_bank(n)[:, w * a + w - P:w * a + w], ident_b[:, :], mask_b[:, :],
                                         start=False, stop=True, skip_group_check=True)
                last.then_inc(mx_ready, 1)

            def shift_rows(i):
                pe.wait_ge(m_ready, i + 1)
                for half in range(2):
                    fill("shift", i, half)
                    for a in range(8):
                        last = pe.transpose(misc_b[SHIFT_ROW:ST_ROWS, P * a:P * a + P],
                                            m_parts[:, i % 2, 8 * half + a, 0:PARTS], ident_b[:, :],
                                            tile_position=(0, SHIFT_ROW))
                    last.then_inc(misc_ready, 1)

            def scores(i, slot):
                j, c = slot // HB, slot % HB
                n = st_n(i, slot)
                w = HB * P
                if slot == 0:
                    for half in range(2):
                        pe.wait_ge(shift_set[half], i + 1)
                if n >= ST_RING:
                    pe.wait_ge(probs_ready, n - ST_RING + 1)
                last = pe.matmul(st_bank(n), kT[0:ST_ROWS, P * j:P * j + P],
                                 qT[0:ST_ROWS, i % 2, w * c:w * c + w], start=True, stop=j < i)
                if j == i:
                    last = pe.matmul(st_bank(n).rearrange("p (a b) -> p a b", a=HB), mask_b[:, :],
                                     ident_b[:, :].rearrange("p (o b) -> p o b", o=1).broadcast_to([P, HB, P]),
                                     start=False, stop=True)
                last.then_inc(st_ready, 1)

            def weigh_values(i, j):
                n = st_n(i, HB * j)
                pe.wait_ge(probs_ready, n + HB)
                if j == 0 and i > 0:
                    pe.wait_ge(o_copied, i)
                for c in range(HB):
                    last = pe.matmul(bank(6)[32 * c:32 * c + 32, :], v_ones[:, j, :], probs[:, (n + c) % P_RING, :],
                                     start=j == 0, stop=j == i, tile_position=(0, 32 * c), skip_group_check=True)
                last.then_inc(pv_done, 1)

            def finish_a(i, step):
                if step == 0:
                    pe.wait_ge(o_copied, i + 1)
                    transposes(("oT", i), [misc[:, P * a:P * a + P] for a in range(HB)],
                               [o_sb[:, P * a:P * a + P] for a in range(HB)], ident[:, :])
                elif step == 1:
                    pe.wait_ge(att_ready, i + 1)
                    transposes(("attT", i), [misc[:, 0:P]], [att[:, i % 2, :]], ident[:, :])
                else:
                    pe.wait_ge(attT_ready, i + 1)
                    fill("wo", i)
                    pe.matmul(misc[:, 0:D], attT[:, :], w_o[:, :], start=True, stop=True).then_inc(misc_ready, 1)

            pe.wait_ge(consts, 1)
            pe.wait_ge(a_loaded, 16 * 4)
            prep(0)
            prep(1)
            pe.wait_ge(consts, 3)
            pe.wait_ge(sim_sq_ready, 1)
            fill("sim")
            pe.matmul(misc[:, 0:E], ones[:, :], sim_sq[:, :], start=True, stop=True).then_inc(misc_ready, 1)
            q_transposes(0)
            for u in range(len(max_units(0))):
                max_scores(0, u)
            shift_rows(0)
            for i in range(NT):
                if i % GT == 0 and 0 < i // GT < NG - 1:
                    prep(i // GT + 1)
                if i + 1 < NT:
                    q_transposes(i + 1)
                plan = slot_plan(i)
                for slot in range(HB * (i + 1)):
                    scores(i, slot)
                    for u in plan[slot]:
                        max_scores(i + 1, u)
                    if slot % HB == HB - 1:
                        if slot >= HB:
                            weigh_values(i, slot // HB - 1)
                        elif i > 0:
                            weigh_values(i - 1, i - 1)
                    if i > 0:
                        for step in range(3):
                            if slot == finish_slots(i)[step]:
                                finish_a(i - 1, step)
                if i + 1 < NT:
                    shift_rows(i + 1)
            weigh_values(NT - 1, NT - 1)
            for step in range(3):
                finish_a(NT - 1, step)

            def spread_weight(ps, g, e):
                pe.matmul(ps, spread[:, e, :], rwT[:, GN * g:GN * g + GN], start=True, stop=True).then_inc(rb_ready, 1)

            def gate_and_project(stage, layer, g):
                n = NG * layer + g
                xT(stage, g)
                pe.wait_ge(xnT_ready, NG * stage + g + 1)
                if n == 0:
                    pe.wait_ge(sim_ready, 1)
                    pe.wait_ge(f_loaded, 16 * 4)
                fill("logit", stage, g)
                for a in range(GT):
                    t = GT * g + a
                    last = pe.matmul(misc[:, E * a:E * a + E], xnT[:, P * t:P * t + P], sim_n[:, :],
                                     start=True, stop=True)
                last.then_inc(misc_ready, 1)
                pe.wait_ge(rparts_ready, n + 1)
                transposes(("rT", stage, g), [misc_b[0:PARTS * E, P * a:P * a + P] for a in range(GT)],
                           [rw_parts[:, a, :, :].rearrange("p a b -> p (a b)") for a in range(GT)], ident_b[:, :])
                pe.wait_ge(rwT_ready, n + 1)
                for e in range(E + 2):
                    if e < E:
                        k = xs_n(layer, 0, g, e)
                        if k >= 3:
                            pe.wait_ge(xs_ready, k - 2)
                        spread_weight(bank(k % 3), g, e)
                    if e > 1:
                        k = xs_n(layer, 0, g, e - 2)
                        pe.wait_ge(xs_ready, k + 1)
                        if e == 2 and n > 0:
                            pe.wait_ge(fqkv_copied, 3 * n)
                        for w, b in zip("qkv", (3, 4, 5)):
                            last = pe.matmul(bank(b), fw[w][:, e - 2, :], xs[:, k % XS_RING, :],
                                             start=e == 2, stop=e == E + 1)
                        last.then_inc(xs_used, 1)
                pe.wait_ge(fqkv_copied, 3 * n + 1)
                transposes(("v", stage, g), [misc[:, P * a:P * a + P] for a in range(GT)],
                           [fvT[:, P * a:P * a + P] for a in range(GT)], ident[:, :])

            def scores_f(layer, i):
                n, L = NT * layer + i, P * (i + 1)
                if i % GT == 0:
                    pe.wait_ge(fqkv_copied, 3 * (NG * layer + i // GT + 1))
                if i:
                    pe.wait_ge(fprobs_ready, n)
                for k0 in range(0, L, GN):
                    w = min(GN, L - k0)
                    pe.matmul(psum[:, k0:k0 + w], fqT[:, P * i:P * i + P], fkT[:, k0:k0 + w],
                              start=True, stop=True)
                pe.matmul(psum[:, L - P:L], ident_b[:, :], mask_b[:, :], start=False, stop=True,
                          skip_group_check=True).then_inc(fs_ready, 1)

            def pair_fill(*key):
                last = PAIR.before(*key)
                if last and last[0] == "pT":
                    pe.wait_ge(pT_copied[PAIR.slot(*key)], pT_copies(last))
                elif last:
                    pe.wait_ge(xs_ready, xs_n(int(last[1] == STAGE_F1), 1, last[2], last[3]) + 1)

            def transpose_probs(stage, layer, i, c):
                key = ("pT", stage, i, c)
                if c == 0:
                    pe.wait_ge(fprobs_ready, NT * layer + i + 1)
                pair_fill(*key)
                for a in range(min(GT, i + 1 - GT * c)):
                    k0 = P * (GT * c + a)
                    last = pe.transpose(pair_bank(key)[:, P * a:P * a + P], fp[:, i % 2, k0:k0 + P], ident[:, :])
                last.then_inc(pT_filled, 1)

            def weigh_f(stage, layer, i, c):
                n, key = pT_n(layer, i, c), ("pT", stage, i, c)
                pe.wait_ge(pT_copied[PAIR.slot(*key)], pT_copies(key))
                if c == 0:
                    pe.wait_ge(fv_ready, NG * layer + i // GT + 1)
                    if i:
                        pe.wait_ge(ao_ready, NT * layer + i)
                for a in range(min(GT, i + 1 - GT * c)):
                    j = GT * c + a
                    last = pe.matmul(bank(6)[:, 0:D], pT[:, n % PT_RING, P * a:P * a + P], fv[:, j, :],
                                     start=j == 0, stop=j == i)
                last.then_inc(pT_used, 1)

            def output_side(stage, layer, g):
                for e in range(E + 2):
                    if e < E:
                        pair_fill("rb", stage, g, e)
                        spread_weight(pair_bank(("rb", stage, g, e)), g, e)
                    if e > 1:
                        k = xs_n(layer, 1, g, e - 2)
                        pe.wait_ge(xs_ready, k + 1)
                        last = pe.matmul(bank(6), fw["o"][:, e - 2, :], xs[:, k % XS_RING, :],
                                         start=e == 2, stop=e == E + 1)
                        last.then_inc(xs_used, 1)
                pe.wait_ge(outT_ready, NG * layer + g + 1)
                transposes(("ffn", stage, g), [misc[:, P * a:P * a + P] for a in range(GT)],
                           [outT[:, P * a:P * a + P] for a in range(GT)], ident[:, :])

            def expert_attention(stage, layer):
                for g in range(NG):
                    gate_and_project(stage, layer, g)
                scores_f(layer, 0)
                for g in range(NG):
                    for i in range(GT * g, GT * g + GT):
                        if i + 1 < NT:
                            scores_f(layer, i + 1)
                        last_c = i // GT
                        for c in range(last_c + 2):
                            if c <= last_c:
                                transpose_probs(stage, layer, i, c)
                            if c:
                                weigh_f(stage, layer, i, c - 1)
                        pe.wait_ge(ao_ready, NT * layer + i + 1)
                        transposes(("aoT", stage, i), [misc[:, 0:P]], [ao[:, i % 2, :]], ident[:, :])
                    output_side(stage, layer, g)

            def scan(g):
                xT(STAGE_B, g)
                pe.wait_ge(xnT_ready, NG * STAGE_B + g + 1)
                if g == 0:
                    pe.wait_ge(wtf_ready, 1)
                pe.matmul(bank(0), w_tf[:, :], xnT[:, GN * g:GN * g + GN], start=True, stop=True).then_inc(tf_ready, 1)
                pe.wait_ge(fg_ready, g + 1)
                pe.matmul(bank(1)[0:PR, :], w_lam[PR:P, :], fg[PR:P, 0, :], start=True, stop=True,
                          tile_position=(PR, 0))
                pe.wait_ge(t_ready, g + 1)
                pe.matmul(bank(2)[0:PR, :], w_b[:, :], tT[:, :], start=True, stop=True).then_inc(lu_ready, 1)
                pe.wait_ge(s_ready, g + 1)
                pe.matmul(bank(3)[0:PR, :], w_c[:, :], s_seq[:, GN * g:GN * g + GN], start=True,
                          stop=True).then_inc(c_ready, 1)
                pe.wait_ge(tt_ready, g + 1)
                fill("h", g)
                for a in range(GT):
                    last = pe.matmul(misc[:, P * a:P * a + P], tt[:, P * a:P * a + P], w_p[:, :],
                                     start=True, stop=True)
                last.then_inc(misc_ready, 1)

            expert_attention(STAGE_F0, 0)
            for g in range(NG):
                scan(g)
            expert_attention(STAGE_F1, 1)

        @block.vector
        def _(dve):
            steps = [0]

            def after(ins):
                steps[0] += 1
                ins.then_inc(dve_step, 1)
                dve.wait_ge(dve_step, steps[0])

            def take(*key):
                dve.wait_ge(misc_ready, MISC.n(*key) + 1)

            def wide(col, shape):
                return col.broadcast_to(shape)

            def layer_norm(stage, g):
                tiles = range(GT * g, GT * g + GT)
                a, b = GT * g, GT * g + GT
                if stage == STAGE_A:
                    dve.wait_ge(x_loaded[g], 16)
                else:
                    dve.wait_ge(x_new, x_new_n(stage - 1, g))
                for t in tiles:
                    last = dve.bn_stats(stats[:, t - a, :], X[:, t, :])
                after(last)
                for t in tiles:
                    last = dve.bn_aggr(mean_var[:, t, :], stats[:, t - a, :])
                after(last)
                dve.tensor_scalar(var_eps[:, a:b], mean_var[:, a:b, 1], EPS, None, ALU.add).then_inc(var_ready, 1)
                dve.wait_ge(rstd_ready, NG * stage + g + 1)
                for t in tiles:
                    last = dve.tensor_scalar(xn[:, t, :], X[:, t, :], mean_var[:, t, 0:1], rstd[:, t:t + 1],
                                             ALU.subtract, ALU.mult)
                last.then_inc(xn_ready, 1)

            def split(src, parts, rests):
                for part in range(PARTS):
                    for o, v in parts(part, src):
                        last = dve.tensor_copy(o, v)
                    if part == PARTS - 1:
                        return last
                    after(last)
                    o, first = rests(part)
                    after(dve.tensor_tensor(o, src, first, ALU.subtract))
                    src = o

            def prep(g):
                a, b = GT * g, GT * g + GT
                s = a % (2 * GT)
                layer_norm(STAGE_A, g)
                for half in range(2):
                    take("proj", g, half)
                    w = D + 2 * HD
                    dve.tensor_tensor(qkv[:, 2 * half:2 * half + 2, :],
                                      misc[:, 0:2 * w].rearrange("p (a b) -> p a b", a=2),
                                      b_qkv[:, :].rearrange("p (o b) -> p o b", o=1).broadcast_to([P, 2, w]),
                                      ALU.add).then_inc(proj_copied, 1)
                dve.wait_ge(proj_copied, 2 * (g + 1))
                qk = qkv[:, :, 0:D + HD].rearrange("p t (h d) -> p t h d", d=HD)
                hs = [P, GT, H + 1, HH // 2]
                c = cos_t[:, a:b, :].rearrange("p t (o d) -> p t o d", o=1)
                sn = sin_t[:, a:b, :].rearrange("p t (o d) -> p t o d", o=1)
                dve.tensor_tensor(turn_c[:, :, :, :], qk[:, :, :, 0:HH], c.broadcast_to([P, GT, H + 1, HH]), ALU.mult)
                q2 = HH // 2
                dve.tensor_tensor(turn_s[:, :, :, 0:q2], qk[:, :, :, q2:HH], sn[:, :, :, 0:q2].broadcast_to(hs), ALU.mult)
                after(dve.tensor_tensor(turn_s[:, :, :, q2:HH], qk[:, :, :, 0:q2], sn[:, :, :, q2:HH].broadcast_to(hs), ALU.mult))
                dve.tensor_copy(v_ones[:, a:b, 0:HD], qkv[:, :, D + HD:D + 2 * HD])
                after(dve.tensor_tensor(qk[:, :, :, 0:HH], turn_c[:, :, :, :], turn_s[:, :, :, :], ALU.add))

                if g:
                    dve.wait_ge(misc_ready, MISC.n("kT", g - 1) + 1)
                kp = k_parts[:, :, 0:QK_ROWS].rearrange("p t (a b d) -> p t a b d", a=PARTS, b=PARTS)
                k32 = qkv[:, :, D:D + HD]

                def k_cols(part, src):
                    return [(kp[:, :, :, part, :],
                             src.rearrange("p t (o d) -> p t o d", o=1).broadcast_to([P, GT, PARTS, HD]))]

                split(k32, k_cols, lambda part: (rest[:, :, H, :], kp[:, :, 0, part, :])).then_inc(kparts_ready, 1)

                if g >= 2:
                    dve.wait_ge(misc_ready, MISC.n("qT", GT * (g - 1) - 1, 1) + 1)
                qp = q_parts[:, s:s + GT, :, 0:QK_ROWS].rearrange("p t h (a b d) -> p t h a b d", a=PARTS, b=PARTS)
                q32 = qkv[:, :, 0:D].rearrange("p t (h d) -> p t h d", d=HD)

                def q_cols(part, src):
                    return [(qp[:, t, :, part, :, :],
                             src[:, t, :, :].rearrange("p h (o d) -> p h o d", o=1).broadcast_to([P, H, PARTS, HD]))
                            for t in range(GT)]

                split(q32, q_cols, lambda part: (rest[:, :, 0:H, :], qp[:, :, :, part, 0, :])).then_inc(qparts_ready, 1)

            def max_reduce(i, u):
                h0, nh, k0, nk = max_units(i)[u]
                n, pieces = MX_BASE[i] + u, max_pieces(i)
                o = m[:, h0:h0 + nh] if pieces == 1 else m_part[:, h0, u % pieces:u % pieces + 1]
                dve.wait_ge(mx_ready, n + 1)
                dve.tensor_reduce(o, mx_bank(n)[:, 0:nh * nk * P].rearrange("p (a b) -> p a b", a=nh),
                                  AX_X, ALU.max).then_inc(mx_free, 1)

            def shift_parts(i):
                dve.wait_ge(mx_free, MX_BASE[i + 1])
                if max_pieces(i) > 1:
                    after(dve.tensor_reduce(m[:, :], m_part[:, :, 0:max_pieces(i)], AX_X, ALU.max))
                mp = m_parts[:, i % 2, :, :]
                after(dve.tensor_scalar(mp[:, :, 0], m[:, :], -1.0, None, ALU.mult))
                after(dve.scalar_tensor_tensor(out=m_rest[:, 0, :], in0=m[:, :], scalar=-1.0, in1=mp[:, :, 0],
                                               op0=ALU.mult, op1=ALU.subtract))
                after(dve.tensor_copy(mp[:, :, 1], m_rest[:, 0, :]))
                after(dve.tensor_tensor(m_rest[:, 1, :], m_rest[:, 0, :], mp[:, :, 1], ALU.subtract))
                dve.tensor_copy(mp[:, :, 2], m_rest[:, 1, :]).then_inc(m_ready, 1)

            def shift_copy(i):
                take("shift", i, 1)
                dve.tensor_copy(qT[SHIFT_ROW:ST_ROWS, i % 2, 1024:2048], misc_b[SHIFT_ROW:ST_ROWS, :])\
                    .then_inc(shift_set[1], 1)

            def finish_a(i, step):
                if step == 0:
                    take("oT", i)
                    o = misc.rearrange("p (a c d) -> p a c d", a=HB, c=HB)
                    after(dve.reciprocal(den[:, :, :], o[:, :, :, HD]))
                    dve.tensor_tensor(att[:, i % 2, :].rearrange("p (c a d) -> p a c d", c=HB, a=HB),
                                      o[:, :, :, 0:HD],
                                      den[:, :, :].rearrange("p a (c o) -> p a c o", o=1).broadcast_to([P, HB, HB, HD]),
                                      ALU.mult).then_inc(att_ready, 1)
                elif step == 2:
                    take("wo", i)
                    dve.tensor_tensor(wo_out[:, :], misc[:, 0:D], b_o[:, :], ALU.add).then_inc(wo_copied, 1)
                    dve.wait_ge(wo_copied, i + 1)
                    dve.tensor_tensor(X[:, i, :], X[:, i, :], wo_out[:, :], ALU.add).then_inc(x_new, 1)

            dve.memset(q_parts[:, :, :, QK_ROWS:QK_PAD], 0.0)
            dve.memset(k_parts[:, :, QK_ROWS:QK_PAD], 0.0)
            dve.memset(k_parts[:, :, SHIFT_ROW:ST_ROWS], 1.0)
            dve.memset(v_ones[:, :, HD:HD + 1], 1.0)
            after(dve.memset(v_ones[:, :, HD + 1:32], 0.0))
            dve.wait_ge(tab_loaded, 16 * 8)
            dve.tensor_tensor(sim_sq[:, :], sim_sb[:, :], sim_sb[:, :], ALU.mult).then_inc(sim_sq_ready, 1)
            prep(0)
            prep(1)
            take("sim")
            dve.tensor_scalar(sim_sq[:, :], misc[:, 0:E], NORM_EPS, None, ALU.add).then_inc(sim_var, 1)
            for u in range(len(max_units(0))):
                max_reduce(0, u)
            shift_parts(0)
            shift_copy(0)
            for i in range(NT):
                if i % GT == 0 and 0 < i // GT < NG - 1:
                    prep(i // GT + 1)
                plan = slot_plan(i)
                for slot in range(HB * (i + 1)):
                    for u in plan[slot]:
                        max_reduce(i + 1, u)
                    if i > 0:
                        for step in (0, 2):
                            if slot == finish_slots(i)[step]:
                                finish_a(i - 1, step)
                if i + 1 < NT:
                    shift_parts(i + 1)
                    shift_copy(i + 1)
            finish_a(NT - 1, 0)
            finish_a(NT - 1, 2)

            def gates_of(layer, g):
                n = NG * layer + g
                eg = [P, GT, E]
                stage = (STAGE_F0, STAGE_F1)[layer]
                a, b = GT * g, GT * g + GT
                take("logit", stage, g)
                dve.wait_ge(x_inv_ready, n + 1)
                dve.tensor_tensor(logits[:, :, :], misc[:, 0:GT * E].rearrange("p (t e) -> p t e", t=GT),
                                  x_inv[:, a:b].rearrange("p (t o) -> p t o", o=1).broadcast_to(eg),
                                  ALU.mult).then_inc(logit_copied, 1)
                dve.wait_ge(logit_copied, n + 1)
                after(dve.tensor_tensor(logits[:, :, :], logits[:, :, :],
                                        gate_sig[:, :].rearrange("p (o e) -> p o e", o=1).broadcast_to(eg), ALU.subtract))
                for t in range(GT):
                    last = dve.max(top[:, t, :], logits[:, t, :])
                after(last)
                for t in range(GT):
                    last = dve.max_index(top_no[:, t, :], top[:, t, :], logits[:, t, :])
                after(last)
                after(dve.tensor_copy(top_nof[:, :, :], top_no[:, :, 0:2]))
                numbers = expert_no[:, :].rearrange("p (o e) -> p o e", o=1).broadcast_to(eg)
                dve.tensor_tensor(pick[:, 0, :, :], numbers, top_nof[:, :, 0:1].broadcast_to(eg), ALU.is_equal)
                after(dve.tensor_tensor(pick[:, 1, :, :], numbers, top_nof[:, :, 1:2].broadcast_to(eg), ALU.is_equal))
                dve.tensor_tensor(pick[:, 0, :, :], pick[:, 0, :, :], pick[:, 1, :, :], ALU.add)
                dve.tensor_scalar(gcol[:, 0, :], top[:, :, 0], 0.0, None, ALU.is_le)
                after(dve.tensor_scalar(gcol[:, 1, :], top[:, :, 0], 0.0, None, ALU.max))
                dve.tensor_scalar(on[:, :, :], logits[:, :, :], 0.0, None, ALU.is_gt)
                dve.tensor_scalar(gtmp[:, :, :], logits[:, :, :], 0.0, None, ALU.max)
                col = lambda c: gcol[:, c, :].rearrange("p (t o) -> p t o", o=1).broadcast_to(eg)
                after(dve.tensor_tensor(pick[:, 0, :, :], pick[:, 0, :, :], col(0), ALU.mult))
                after(dve.tensor_tensor(on[:, :, :], on[:, :, :], pick[:, 0, :, :], ALU.add))
                dve.tensor_tensor(gtmp[:, :, :], gtmp[:, :, :], col(1), ALU.subtract).then_inc(gate_arg, 1)
                dve.wait_ge(gate_exp, n + 1)
                after(dve.tensor_tensor(rw[:, :, :], gexp[:, :, :], on[:, :, :], ALU.mult))
                after(dve.tensor_reduce(gcol[:, 2, :], rw[:, :, :], AX_X, ALU.add))
                after(dve.reciprocal(gcol[:, 0, :], gcol[:, 2, :]))
                after(dve.tensor_tensor(rw[:, :, :], rw[:, :, :], col(0), ALU.mult))
                split(rw[:, :, :], lambda part, src: [(rw_parts[:, :, part, :], src)],
                      lambda part: (rw_rest[:, :, :], rw_parts[:, :, part, :])).then_inc(rparts_ready, 1)

            def scale_tile(k, weights, src):
                dve.wait_ge(rb_ready, k + 1)
                if k >= XS_RING:
                    dve.wait_ge(xs_used, k - XS_RING + 1)
                dve.tensor_tensor(xs[:, k % XS_RING, :], weights, src, ALU.mult).then_inc(xs_ready, 1)

            def gate_and_project(stage, layer, g):
                a, b = GT * g, GT * g + GT
                layer_norm(stage, g)
                dve.wait_ge(xn_ready, NG * stage + g + 1)
                for t in range(a, b):
                    last = dve.tensor_tensor_reduce(sq_junk[:, t - a, :], xn[:, t, :], xn[:, t, :], 1.0, 0.0,
                                                    ALU.mult, ALU.add, sq_sum[:, t:t + 1])
                after(last)
                dve.tensor_scalar(sq_sum[:, a:b], sq_sum[:, a:b], NORM_EPS, None, ALU.add).then_inc(sq_ready, 1)
                gates_of(layer, g)
                dve.wait_ge(xnT_ready, NG * stage + g + 1)
                for e in range(E):
                    k = xs_n(layer, 0, g, e)
                    scale_tile(k, bank(k % 3), xnT[:, GN * g:GN * g + GN])

            def max_f(layer, i):
                dve.wait_ge(fs_ready, NT * layer + i + 1)
                after(dve.tensor_reduce(fm[:, i:i + 1], psum[:, 0:P * (i + 1)], AX_X, ALU.max))
                dve.tensor_scalar(f_shift[:, i:i + 1], fm[:, i:i + 1], -SCALE_F, None, ALU.mult).then_inc(fshift_ready, 1)

            def attend_f(stage, layer, i):
                n = NT * layer + i
                dve.wait_ge(fprobs_ready, n + 1)
                after(dve.reciprocal(f_inv[:, i:i + 1], f_sum[:, i:i + 1]))
                for c in range(0, i // GT + 1, 2):
                    u, key = pT_n(layer, i, c), ("pT", stage, i, c)
                    w = P * min(GT, i + 1 - GT * c)
                    dve.wait_ge(pT_filled, u + 1)
                    if u >= PT_RING:
                        dve.wait_ge(pT_used, u - PT_RING + 1)
                    dve.tensor_copy(pT[:, u % PT_RING, 0:w], pair_bank(key)[:, 0:w]).then_inc(pT_copied[PAIR.slot(*key)], 1)
                dve.wait_ge(pT_used, weighed(layer, i))
                dve.tensor_scalar(ao[:, i % 2, :], bank(6)[:, 0:D], f_inv[:, i:i + 1], None, ALU.mult).then_inc(ao_ready, 1)

            def add_to_x(g):
                a, b = GT * g, GT * g + GT
                dve.tensor_tensor(X[:, a:b, :], X[:, a:b, :], misc.rearrange("p (t d) -> p t d", t=GT),
                                  ALU.add).then_inc(x_new, 1)

            def expert_attention(stage, layer):
                for g in range(NG):
                    gate_and_project(stage, layer, g)
                max_f(layer, 0)
                for g in range(NG):
                    for i in range(GT * g, GT * g + GT):
                        if i + 1 < NT:
                            max_f(layer, i + 1)
                        attend_f(stage, layer, i)
                    dve.wait_ge(aoT_ready, NT * layer + GT * (g + 1))
                    for e in range(E):
                        scale_tile(xs_n(layer, 1, g, e), pair_bank(("rb", stage, g, e)), aoT[:, GN * g:GN * g + GN])
                    take("ffn", stage, g)
                    add_to_x(g)

            def scan(g):
                layer_norm(STAGE_B, g)
                dve.wait_ge(fg_exp, g + 1)
                after(dve.tensor_scalar(fg[PR:P, 1, :], fg[PR:P, 0, :], 1.0, None, ALU.add))
                dve.reciprocal(fg[PR:P, 0, :], fg[PR:P, 1, :]).then_inc(fg_ready, 1)
                dve.wait_ge(lam_exp, g + 1)
                after(dve.tensor_scalar(lam[:, 1, :], lam[:, 0, :], 1.0, None, ALU.add))
                after(dve.reciprocal(lam[:, 0, :], lam[:, 1, :]))
                dve.tensor_tensor_scan(s_seq[:, GN * g:GN * g + GN], lam[:, 0, :], bank(2)[0:PR, :],
                                       s_seq[:, GN * g - 1:GN * g] if g else 0.0, ALU.mult, ALU.add).then_inc(s_ready, 1)
                dve.wait_ge(c_ready, g + 1)
                dve.tensor_tensor(tt[:, :], bank(3)[0:PR, :], tT[:, :], ALU.add).then_inc(tt_ready, 1)
                take("h", g)
                add_to_x(g)

            dve.wait_ge(sim_pow, 1)
            dve.tensor_tensor(sim_n[:, :], sim_sb[:, :], sim_sq[:, :], ALU.mult).then_inc(sim_ready, 1)
            dve.wait_ge(gates_exp, 1)
            after(dve.tensor_scalar(gate_sig[:, :], gate_sig[:, :], 1.0, None, ALU.add))
            after(dve.reciprocal(gate_sig[:, :], gate_sig[:, :]))
            dve.wait_ge(b_loaded, 16 * 8)
            after(dve.tensor_tensor(w_u[:, :, :], w_u[:, :, :], w_v[:, :, :], ALU.mult))
            after(dve.tensor_reduce(w_uv[:, :], w_u[:, :, :], AX_X, ALU.add))
            dve.tensor_tensor(w_tf[:, 0:PR], w_tf[:, 0:PR], w_uv[:, :], ALU.add).then_inc(wtf_ready, 1)
            dve.wait_ge(consts, 4)
            expert_attention(STAGE_F0, 0)
            for g in range(NG):
                scan(g)
            expert_attention(STAGE_F1, 1)


_INS = ["L0_attn_a_x", "L0_attn_a_Wq", "L0_attn_a_bq", "L0_attn_a_Wk", "L0_attn_a_bk", "L0_attn_a_Wv",
        "L0_attn_a_bv", "L0_attn_a_Wo", "L0_attn_a_bo", "L0_attn_b_W_toP", "L0_attn_b_W_U", "L0_attn_b_W_F",
        "L0_attn_b_W_V", "L0_attn_b_W_lam", "L0_attn_b_B_mat", "L0_attn_b_C_mat", "L0_attn_b_W_fromP",
        "L0_ffn_sim_matrix", "L0_ffn_gates", "L0_ffn_q_proj", "L0_ffn_k_proj", "L0_ffn_v_proj",
        "L0_ffn_o_proj"]
_OUTS = [((1, 2048, 128), "float32")]


def _rotation_tables():
    import numpy as np
    theta = np.float32(10000.0) ** (-np.arange(HH, dtype=np.float32) / np.float32(HH))
    angle = np.arange(T, dtype=np.float32)[:, None] * theta[None, :].astype(np.float32)
    sign = np.where(np.arange(HH) < HH // 2, -1.0, 1.0).astype(np.float32)
    return np.cos(angle).astype(np.float32), (np.sin(angle) * sign).astype(np.float32)


def kernel(**inputs):
    import numpy as _np
    import concourse.bacc as _bacc
    from concourse import mybir as _mybir
    from concourse.bass_utils import run_bass_kernel_spmd as _run

    nc = _bacc.Bacc("TRN2", target_bir_lowering=False, num_devices=1)
    cos, sin = _rotation_tables()
    named = [(name, inputs[name]) for name in _INS] + [("cos", cos), ("sin", sin)]
    arrays, args = {}, []
    for name, value in named:
        a = _np.ascontiguousarray(value)
        arrays[f"in_{name}_dram"] = a
        args.append(nc.dram_tensor(f"in_{name}_dram", a.shape, _mybir.dt.from_np(a.dtype), kind="ExternalInput").ap())
    for i, (shape, dtype) in enumerate(_OUTS):
        dt = _mybir.dt.from_np(_np.dtype(dtype))
        args.append(nc.dram_tensor(f"out_{i}_dram", shape, dt, kind="ExternalOutput").ap())
    hybrid_block_kernel(nc, *args)
    r = _run(nc, [arrays], core_ids=[0])
    return r.results[0]["out_0_dram"]
```

```python
from contextlib import ExitStack

import concourse.bass as bass
from concourse import mybir

F32 = mybir.dt.float32
BF16 = mybir.dt.bfloat16
U32 = mybir.dt.uint32
ALU = mybir.AluOpType
ACT = mybir.ActivationFunctionType
AX_X = mybir.AxisListType.X

P = 128
T = 2048
D = 128
NT = T // P
GT = 4
GN = GT * P
NG = NT // GT
H = 16
HD = D // H
HH = HD // 2
HB = 4
E = 16
PR = 64
ALPHA = 4
EPS = 1e-5
NORM_EPS = 1e-12
SCALE_A = float(HD) ** -0.5
SCALE_F = float(D) ** -0.5
MASKED = -1e30
PARTS = 3
QK_ROWS = PARTS * PARTS * HD
SHIFT_ROW = 96
QK_PAD = SHIFT_ROW
ST_ROWS = SHIFT_ROW + PARTS
MX_RING, ST_RING, P_RING, XS_RING, PT_RING = 3, 3, 8, 3, 4
STAGE_A, STAGE_F0, STAGE_B, STAGE_F1 = range(4)
LEAD = 12
PREP_STEPS = 10
OE = 4
LAG = 2
Q_RING = 3


class Uses:

    def __init__(self, keys, slots=1):
        self.at = {key: n for n, key in enumerate(keys)}
        self.keys = keys
        self.slots = slots

    def n(self, *key):
        return self.at[key]

    def before(self, *key):
        n = self.at[key] - self.slots
        return self.keys[n] if n >= 0 else None

    def slot(self, *key):
        return self.at[key] % self.slots


def max_units(i):
    nb = i + 1
    if nb <= GT:
        nh = GT // nb
        return [(h, min(nh, H - h), 0, nb) for h in range(0, H, nh)]
    pieces = -(-nb // GT)
    cuts = [nb * c // pieces for c in range(pieces + 1)]
    return [(h, 1, cuts[c], cuts[c + 1] - cuts[c]) for h in range(H) for c in range(pieces)]


def max_pieces(i):
    return max(1, -(-(i + 1) // GT))


def first_slot(i):
    return HB * (i * (i + 1) // 2)


def lead(i):
    return min(LEAD, i + 1)


def max_window(i):
    return 0 if i == 1 else first_slot(i - 1) - lead(i - 1), first_slot(i) - lead(i)


def max_plan():
    plan = [[] for _ in range(first_slot(NT))]
    for i in range(1, NT):
        (lo, hi), n = max_window(i), len(max_units(i))
        for u in range(n):
            plan[lo + u * (hi - lo) // n].append((i, u))
    return plan


def side_plan():
    plan = {}

    def put(chain, at, places):
        for step, place in enumerate(places):
            plan.setdefault(place, []).append((chain, at, step))

    for i in range(1, NT):
        lo, s, last = max_window(i)[0], first_slot(i), first_slot(i + 1) - 1
        q = max(lo - 6, first_slot(i - Q_RING + 1) if i >= Q_RING else 0)
        put("q", (i,), [("A", q), ("A", min(max(lo - 3, q), lo))])
        put("shift", (i,), [("A", s - max(2, 2 * lead(i) // 3)), ("A", s - max(1, lead(i) // 3))])
        put("finish", (i - 1,), [("A", s + 3), ("A", min(s + 5, last)), ("A", min(s + 9, last)), ("A", min(s + 13, last))])
    put("finish", (NT - 1,), [("P", 0, 0, e) for e in (0, 1, 3, 5)])
    for g, first in ((1, 0), (2, 62), (3, 184)):
        steps = (0, 1, 3, 5, 6, 8, 9, 10, 11, 13) if g == 1 else (0, 2, 4, 6, 8, 10, 12, 14, 16, 18)
        put("prep", (g,), [("A", first + n) for n in steps])
    put("sim", (), [("A", n) for n in (24, 28, 32, 36)])
    for g, first in ((0, 90), (1, 210), (2, 340)):
        put("gate", (0, g), [("A", first + n) for n in (0, 3, 7, 11, 15, 20)])
    put("gate", (0, 3), [("P", 0, 0, e) for e in (7, 8, 9, 11, 13, 15)])
    for g in range(1, NG):
        at = [("T", 0, GT * g + k, n) for k in range(GT) for n in range(GT)]
        put("scan", (g - 1,), at[5:15])
        if g > 1:
            put("gate", (1, g - 2), at[2:14:2])
    put("scan", (NG - 1,), [("P", 1, 0, e) for e in (0, 1, 2, 3, 5, 7, 9, 11, 13, 15)])
    put("gate", (1, NG - 2), [("P", 1, 0, e) for e in (4, 5, 6, 8, 10, 14)])
    put("gate", (1, NG - 1), [("P", 1, 1, e) for e in (1, 2, 4, 7, 9, 13)])
    return plan


def places():
    for slot in range(first_slot(NT)):
        yield ("A", slot)
    for layer in range(2):
        for g in range(NG):
            for e in range(E + LAG):
                yield ("P", layer, g, e)
            yield ("v", layer, g)
        for g in range(NG):
            for i in range(GT * g, GT * g + GT):
                yield ("T", layer, i, 0)
                if i:
                    yield ("aoT", layer, i - 1)
                for n in range(1, GT):
                    yield ("T", layer, i, n)
                    if i and i % GT == 0 and n == 2:
                        yield ("ffn", layer, g - 1)
        yield ("aoT", layer, NT - 1)
        yield ("ffn", layer, NG - 1)


def row_steps(i):
    last = i // GT if i < NT else -1
    steps = []
    if i < NT:
        steps += [("pT", c) for c in range(min(2, last + 1))]
    for c in range(GT):
        if i:
            steps.append(("out", c))
        if c < 2 and i < NT:
            steps.append(("at", c + 1))
        if c and c + 1 <= last:
            steps.append(("pT", c + 1))
        if c <= last:
            steps.append(("av", c))
    return steps + [("at", 3)] if i < NT else steps


FFN_STAGE = (STAGE_F0, STAGE_F1)
SIDE = side_plan()


def misc_order():
    def of_step(chain, at, step):
        if chain == "q":
            return [("qT", *at, step)]
        if chain == "shift":
            return [("shift", *at, step)]
        if chain == "finish":
            return [(("oT", "attT", "wo")[step - 1], *at)] if step else []
        if chain == "prep":
            return {2: [("xT", STAGE_A, *at)], 3: [("proj", *at, 0)], 4: [("proj", *at, 1)], 9: [("kT", *at)]}.get(step, [])
        if chain == "sim":
            return [("sim",)] if step == 1 else []
        if chain == "gate":
            stage = FFN_STAGE[at[0]]
            kind = {2: "xT", 3: "logit", 5: "rT"}.get(step)
            return [(kind, stage, at[1])] if kind else []
        if chain == "scan":
            if step == 2:
                return [("xT", STAGE_B, *at)]
            kind = {3: "tf", 5: "lam", 7: "u", 8: "c", 9: "h"}.get(step)
            return [(kind, *at)] if kind else []

    out = [use for step in range(PREP_STEPS) for use in of_step("prep", (0,), step)]
    out += of_step("q", (0,), 0) + of_step("q", (0,), 1) + of_step("shift", (0,), 0) + of_step("shift", (0,), 1)
    for place in places():
        if place[0] in ("v", "aoT"):
            out.append((place[0], FFN_STAGE[place[1]], place[2]))
        for at in SIDE.get(place, ()):
            out += of_step(*at)
    return out


def norm_order():
    stage_of = {"prep": lambda at: (STAGE_A, at[0]), "gate": lambda at: (FFN_STAGE[at[0]], at[1]),
                "scan": lambda at: (STAGE_B, at[0])}
    return [(STAGE_A, 0)] + [stage_of[chain](at) for place in places() for chain, at, step in SIDE.get(place, ())
                             if chain in stage_of and step == 0]


def update_order():
    out = []
    for place in places():
        out += [(STAGE_B, at[0]) for chain, at, step in SIDE.get(place, ()) if (chain, step) == ("scan", 9)]
        if place[0] == "ffn":
            out.append((FFN_STAGE[place[1]], place[2]))
    return out


def pair_order():
    out = []
    for s in (STAGE_F0, STAGE_F1):
        for i in range(NT + 1):
            for kind, c in row_steps(i):
                if kind == "pT":
                    out.append(("pT", s, i, c))
                elif kind == "out":
                    out.append(("out", s, i - 1, c))
    return out


def hybrid_block_kernel(nc, x, Wq, bq, Wk, bk, Wv, bv, Wo, bo, W_toP, W_U, W_F, W_V, W_lam, B_mat,
                        C_mat, W_fromP, sim, gates, q_proj, k_proj, v_proj, o_proj, cos, sin, out):
    MISC = Uses(misc_order())
    PAIR = Uses(pair_order(), 2)
    BASE = [i * (i + 1) // 2 for i in range(NT + 1)]
    NORM, UPDATE = Uses(norm_order()), Uses(update_order())
    MAX_PLAN = max_plan()
    MX_BASE = [sum(len(max_units(a)) for a in range(i)) for i in range(NT + 1)]

    def st_n(i, slot):
        return HB * BASE[i] + slot

    def xs_n(layer, g, e):
        return (layer * NG + g) * E + e

    def scaled_n(layer, i, e):
        return (NT * layer + i) * E + e

    def pT_n(layer, i, c):
        before = [a // GT + 1 for a in range(NT)]
        return sum(before) * layer + sum(before[:i]) + c

    def weighed(layer, i):
        return pT_n(layer, i, i // GT) + 1

    def x_new_n(stage, g):
        return GT * (g + 1) if stage == STAGE_A else NT + UPDATE.n(stage, g) + 1

    with ExitStack() as ctx:
        def sb(name, shape, dt=F32):
            return ctx.enter_context(nc.sbuf_tensor(name, shape, dt))

        def sem(name):
            return ctx.enter_context(nc.semaphore(name))

        X = sb("X", [P, NT, D])
        xn = sb("xn", [P, NT, D])
        xnT = sb("xnT", [P, T])
        stats = sb("stats", [P, GT, 6])
        mean_var = sb("mean_var", [P, NT, 2])
        var_eps = sb("var_eps", [P, NT])
        rstd = sb("rstd", [P, NT])
        minus_half = sb("minus_half", [P, E])
        w_qkv = sb("w_qkv", [P, D + 2 * HD])
        b_qkv = sb("b_qkv", [P, D + 2 * HD])
        w_o = sb("w_o", [P, D])
        b_o = sb("b_o", [P, D])
        cos_t = sb("cos_t", [P, NT, HH])
        sin_t = sb("sin_t", [P, NT, HH])
        qkv = sb("qkv", [P, GT, D + 2 * HD])
        turn_c = sb("turn_c", [P, GT, H + 1, HH])
        turn_s = sb("turn_s", [P, GT, H + 1, HH])
        rest = sb("rest", [P, GT, H + 1, HD])
        q_parts = sb("q_parts", [P, 2 * GT, H, QK_PAD], BF16)
        k_parts = sb("k_parts", [P, GT, P], BF16)
        v_ones = sb("v_ones", [P, NT, 32])
        kT = sb("kT", [P, T], BF16)
        qT = sb("qT", [P, Q_RING, H * P], BF16)
        m_part = sb("m_part", [P, H, GT])
        m = sb("m", [P, H])
        m_rest = sb("m_rest", [P, 2, H])
        m_parts = sb("m_parts", [P, 2, H, 4], BF16)
        probs = sb("probs", [P, P_RING, GN])
        o_sb = sb("o_sb", [P, GN])
        den = sb("den", [P, HB, HB])
        att = sb("att", [P, 2, D])
        attT = sb("attT", [P, D])
        wo_out = sb("wo_out", [P, D])
        fw = {name: sb(f"w_expert_{name}", [P, E, D]) for name in "qkvo"}
        sim_sb = sb("sim_sb", [P, E])
        sim_sq = sb("sim_sq", [P, E])
        sim_n = sb("sim_n", [P, E])
        gate_sig = sb("gate_sig", [P, E])
        expert_no = sb("expert_no", [P, E])
        sq_sum = sb("sq_sum", [P, NT])
        sq_junk = sb("sq_junk", [P, GT, D])
        x_inv = sb("x_inv", [P, NT])
        logits = sb("logits", [P, GT, E])
        top = sb("top", [P, GT, 8])
        top_no = sb("top_no", [P, GT, 8], U32)
        top_nof = sb("top_nof", [P, GT, 2])
        pick = sb("pick", [P, 2, GT, E])
        on = sb("on", [P, GT, E])
        gtmp = sb("gtmp", [P, GT, E])
        gexp = sb("gexp", [P, GT, E])
        gcol = sb("gcol", [P, 3, GT])
        rw = sb("rw", [P, NT, E])
        rw_rest = sb("rw_rest", [P, GT, E])
        rw_parts = sb("rw_parts", [P, GT, PARTS, E], BF16)
        rwT = sb("rwT", [PARTS * E, T], BF16)
        spread = sb("spread", [PARTS * E, E, P], BF16)
        xs = sb("xs", [P, XS_RING, GN])
        fqT = sb("fqT", [P, T])
        fkT = sb("fkT", [P, T])
        fvT = sb("fvT", [P, GN])
        after_a = q_parts[:, :, :, :].rearrange("p t h c -> p (t h c)").bitcast(F32)
        s_seq = after_a[0:PR, 0:T]
        tt = after_a[0:PR, T:T + GN]
        fv = after_a[:, T + GN:T + GN + NT * D].rearrange("p (t d) -> p t d", d=D)
        fm = sb("fm", [P, NT])
        f_shift = sb("f_shift", [P, NT])
        f_sum = sb("f_sum", [P, NT])
        f_inv = sb("f_inv", [P, NT])
        fp = probs[:, :, :].rearrange("p (a b) n -> p a (b n)", a=2)
        pT = sb("pT", [P, PT_RING, GN])
        ao = sb("ao", [P, 2, D])
        aoT = sb("aoT", [P, T])
        out_sum = sb("out_sum", [P, 2, D])
        w_tf = sb("w_tf", [P, P])
        w_u = sb("w_u", [P, PR, ALPHA])
        w_v = sb("w_v", [P, PR, ALPHA])
        w_uv = sb("w_uv", [P, PR])
        w_lam = sb("w_lam", [P, PR])
        w_b = sb("w_b", [PR, PR])
        w_c = sb("w_c", [PR, PR])
        w_p = sb("w_p", [PR, D])
        tT = sb("tT", [PR, GN])
        fg = sb("fg", [P, 2, GN])
        lam = sb("lam", [PR, 2, GN])
        ident = sb("ident", [P, P])
        ident_b = sb("ident_b", [P, P], BF16)
        mask_b = sb("mask_b", [P, P], BF16)
        ones = sb("ones", [P, P])
        psum = ctx.enter_context(nc.psum_tensor("psum", [P, 8 * GN], F32))

        def bank(n):
            return psum[:, GN * n:GN * n + GN]

        def mx_bank(n):
            return bank(n % MX_RING)

        def st_bank(n):
            return bank(MX_RING + n % ST_RING)

        def pair_bank(key):
            return bank(4 + PAIR.slot(*key))

        misc = bank(7)
        misc_b = misc.bitcast(BF16)

        x_loaded = [sem(f"x_loaded{g}") for g in range(NG)]
        rot_loaded, tab_loaded, a_loaded, wo_loaded, b_loaded = (
            sem(n) for n in ("rot_loaded", "tab_loaded", "a_loaded", "wo_loaded", "b_loaded"))
        f_loaded = sem("f_loaded")
        consts = sem("consts")
        pool_step, dve_step = sem("pool_step"), sem("dve_step")
        x_new = sem("x_new")
        var_ready, rstd_ready, xn_ready, xnT_ready = (
            sem(n) for n in ("var_ready", "rstd_ready", "xn_ready", "xnT_ready"))
        sq_ready, x_inv_ready = sem("sq_ready"), sem("x_inv_ready")
        misc_ready = sem("misc_ready")
        sim_sq_ready, sim_var, sim_pow, sim_ready = (
            sem(n) for n in ("sim_sq_ready", "sim_var", "sim_pow", "sim_ready"))
        gates_exp = sem("gates_exp")
        proj_copied, kparts_ready, kT_ready, qparts_ready, qT_ready = (
            sem(n) for n in ("proj_copied", "kparts_ready", "kT_ready", "qparts_ready", "qT_ready"))
        mx_ready, mx_free, m_ready = sem("mx_ready"), sem("mx_free"), sem("m_ready")
        shift_set = [sem(f"shift_set{half}") for half in range(2)]
        st_ready, probs_ready, pv_done, o_copied = (
            sem(n) for n in ("st_ready", "probs_ready", "pv_done", "o_copied"))
        att_ready, attT_ready, wo_copied = sem("att_ready"), sem("attT_ready"), sem("wo_copied")
        logit_copied, gate_arg, gate_exp, rparts_ready, rwT_ready = (
            sem(n) for n in ("logit_copied", "gate_arg", "gate_exp", "rparts_ready", "rwT_ready"))
        rb_ready, xs_ready, xs_used = sem("rb_ready"), sem("xs_ready"), sem("xs_used")
        fqkv_copied, fv_ready = sem("fqkv_copied"), sem("fv_ready")
        fs_ready, fshift_ready, fprobs_ready = (
            sem(n) for n in ("fs_ready", "fshift_ready", "fprobs_ready"))
        pT_filled = sem("pT_filled")
        pT_copied = [sem(f"pT_copied{n}") for n in range(2)]
        pT_used = sem("pT_used")
        ao_ready, aoT_ready = sem("ao_ready"), sem("aoT_ready")
        out_filled, out_scaled = sem("out_filled"), sem("out_scaled")
        wtf_ready, fg_exp, fg_ready, t_ready = (
            sem(n) for n in ("wtf_ready", "fg_exp", "fg_ready", "t_ready"))
        lam_exp, s_ready, tt_ready = sem("lam_exp"), sem("s_ready"), sem("tt_ready")
        stored = sem("stored")

        def misc_copied(kind, *at):
            if kind == "sim":
                return sim_var, 1
            if kind == "xT":
                return xnT_ready, NORM.n(*at) + 1
            if kind == "proj":
                return proj_copied, 2 * at[0] + at[1] + 1
            if kind == "kT":
                return kT_ready, at[0] + 1
            if kind == "qT":
                return qT_ready, 2 * at[0] + at[1] + 1
            if kind == "shift":
                return shift_set[at[1]], at[0] + 1
            if kind == "oT":
                return att_ready, at[0] + 1
            if kind == "attT":
                return attT_ready, at[0] + 1
            if kind == "wo":
                return wo_copied, at[0] + 1
            if kind in ("tf", "lam", "u", "c"):
                return {"tf": t_ready, "lam": lam_exp, "u": s_ready, "c": tt_ready}[kind], at[0] + 1
            if kind == "h":
                return x_new, x_new_n(STAGE_B, at[0])
            layer = int(at[0] == STAGE_F1)
            if kind == "aoT":
                return aoT_ready, NT * layer + at[1] + 1
            by_group = {"logit": logit_copied, "rT": rwT_ready, "v": fv_ready}
            return by_group[kind], NG * layer + at[1] + 1

        def pT_copies(key):
            own = PAIR.keys[PAIR.slot(*key)::2][:PAIR.n(*key) // 2 + 1]
            return sum(k[0] == "pT" for k in own)

        block = ctx.enter_context(nc.Block())

        @block.sync
        def _(sp):
            sp.dma_start(X[:, 0:GT, :], x.rearrange("b (n p) d -> p (b n) d", p=P)[:, 0:GT, :]).then_inc(x_loaded[0], 16)
            sp.dma_start(cos_t[:, :, :], cos).then_inc(rot_loaded, 16)
            sp.dma_start(sin_t[:, :, :], sin).then_inc(rot_loaded, 16)
            xv = x.rearrange("b (n p) d -> p (b n) d", p=P)
            ov = out.rearrange("b (n p) d -> p (b n) d", p=P)
            for g in range(1, NG):
                sp.dma_start(X[:, GT * g:GT * g + GT, :], xv[:, GT * g:GT * g + GT, :]).then_inc(x_loaded[g], 16)
            for w, src in (("q", q_proj), ("k", k_proj), ("v", v_proj), ("o", o_proj)):
                sp.dma_start(fw[w][:, :, :], src.rearrange("e c h -> c e h")).then_inc(f_loaded, 16)
            for g in range(NG):
                sp.wait_ge(x_new, x_new_n(STAGE_F1, g))
                sp.dma_start(ov[:, GT * g:GT * g + GT, :], X[:, GT * g:GT * g + GT, :]).then_inc(stored, 16)
            sp.wait_ge(stored, 16 * NG)

        @block.gpsimd
        def _(pool):
            steps = [0]

            def after(ins):
                steps[0] += 1
                ins.then_inc(pool_step, 1)
                pool.wait_ge(pool_step, steps[0])

            after(pool.memset(ident[:, :], 0.0))
            after(pool.affine_select(out=ident[:, :], in_=ident[:, :], compare_op=ALU.not_equal, fill=1.0,
                                     base=0, pattern=[[-1, P]], channel_multiplier=1))
            pool.tensor_copy(ident_b[:, :], ident[:, :]).then_inc(consts, 1)
            after(pool.memset(minus_half[:, :], -0.5))

            def inverse_roots(stage, g):
                a, b = GT * g, GT * g + GT
                pool.wait_ge(var_ready, NORM.n(stage, g) + 1)
                pool.tensor_tensor(rstd[:, a:b], var_eps[:, a:b], minus_half[:, 0:GT], ALU.pow).then_inc(rstd_ready, 1)
                if stage in FFN_STAGE:
                    pool.wait_ge(sq_ready, NG * FFN_STAGE.index(stage) + g + 1)
                    pool.tensor_tensor(x_inv[:, a:b], sq_sum[:, a:b], minus_half[:, 0:GT], ALU.pow).then_inc(x_inv_ready, 1)

            inverse_roots(STAGE_A, 0)
            after(pool.memset(mask_b[:, :], 0.0))
            pool.affine_select(out=mask_b[:, :], in_=mask_b[:, :], compare_op=ALU.is_ge, fill=MASKED,
                               base=0, pattern=[[-1, P]], channel_multiplier=1).then_inc(consts, 1)
            pool.memset(ones[:, :], 1.0).then_inc(consts, 1)
            pool.dma_start(w_tf[:, 0:PR], W_toP).then_inc(b_loaded, 16)
            pool.dma_start(w_tf[:, PR:P], W_F).then_inc(b_loaded, 16)
            pool.dma_start(w_u[:, :, :], W_U).then_inc(b_loaded, 16)
            pool.dma_start(w_v[:, :, :], W_V.rearrange("(o p) a -> o p a", o=1).broadcast_to([P, PR, ALPHA])).then_inc(b_loaded, 16)
            pool.dma_start(w_lam[PR:P, :], W_lam).then_inc(b_loaded, 16)
            pool.dma_start(w_b[:, :], B_mat).then_inc(b_loaded, 16)
            pool.dma_start(w_c[:, :], C_mat).then_inc(b_loaded, 16)
            pool.dma_start(w_p[:, :], W_fromP).then_inc(b_loaded, 16)
            inverse_roots(STAGE_A, 1)
            pool.wait_ge(sim_var, 1)
            pool.tensor_tensor(sim_sq[:, :], sim_sq[:, :], minus_half[:, :], ALU.pow).then_inc(sim_pow, 1)
            pool.iota(expert_no[:, :], pattern=[[1, E]], base=0, channel_multiplier=0,
                      allow_small_or_imprecise_dtypes=True).then_inc(consts, 1)
            after(pool.memset(spread[:, :, :], 0.0))
            for part in range(PARTS):
                after(pool.affine_select(out=spread[:, :, :], in_=spread[:, :, :], compare_op=ALU.not_equal,
                                         fill=1.0, base=-E * part, pattern=[[-1, E], [0, P]],
                                         channel_multiplier=1))
            for stage, g in NORM.keys[2:]:
                inverse_roots(stage, g)

        @block.scalar
        def _(act):
            act.dma_start(w_qkv[:, 0:D], Wq).then_inc(a_loaded, 16)
            act.dma_start(w_qkv[:, D:D + HD], Wk).then_inc(a_loaded, 16)
            act.dma_start(w_qkv[:, D + HD:D + 2 * HD], Wv).then_inc(a_loaded, 16)
            for lo, n, b in ((0, D, bq), (D, HD, bk), (D + HD, HD, bv)):
                act.dma_start(b_qkv[:, lo:lo + n], b.rearrange("(o n) -> o n", o=1).broadcast_to([P, n])).then_inc(rot_loaded, 16)
            act.dma_start(b_o[:, :], bo.rearrange("(o n) -> o n", o=1).broadcast_to([P, D])).then_inc(tab_loaded, 16)
            act.dma_start(sim_sb[:, :], sim).then_inc(tab_loaded, 16)
            act.dma_start(gate_sig[:, :], gates.rearrange("(o n) -> o n", o=1).broadcast_to([P, E])).then_inc(tab_loaded, 16)
            act.dma_start(w_o[:, :], Wo).then_inc(wo_loaded, 16)

            def take(*key):
                act.wait_ge(misc_ready, MISC.n(*key) + 1)

            def xT_copy(stage, g):
                take("xT", stage, g)
                act.activation(xnT[:, GN * g:GN * g + GN], misc, ACT.Copy).then_inc(xnT_ready, 1)

            def prep(g, step):
                if step == 2:
                    xT_copy(STAGE_A, g)
                elif step == 9:
                    kT_copy(g)

            def kT_copy(g):
                take("kT", g)
                act.activation(kT[0:ST_ROWS, GN * g:GN * g + GN], misc_b[0:ST_ROWS, 0:GN], ACT.Copy).then_inc(kT_ready, 1)

            def q_copy(i, half):
                if i >= Q_RING:
                    act.wait_ge(st_ready, st_n(i - Q_RING + 1, 0))
                take("qT", i, half)
                act.activation(qT[0:QK_PAD, i % Q_RING, 1024 * half:1024 * half + 1024], misc_b[0:QK_PAD, :],
                               ACT.Copy).then_inc(qT_ready, 1)

            def shift_copy(i):
                take("shift", i, 0)
                act.activation(qT[SHIFT_ROW:ST_ROWS, i % Q_RING, 0:1024], misc_b[SHIFT_ROW:ST_ROWS, :],
                               ACT.Copy).then_inc(shift_set[0], 1)

            def exp_a(i, slot):
                n = st_n(i, slot)
                act.wait_ge(st_ready, n + 1)
                if n >= P_RING:
                    act.wait_ge(pv_done, (n - P_RING) // HB + 1)
                act.activation(probs[:, n % P_RING, :], st_bank(n), ACT.Exp, scale=SCALE_A).then_inc(probs_ready, 1)

            def sums_copy(i):
                act.wait_ge(pv_done, BASE[i + 1])
                act.activation(o_sb[:, :], bank(6), ACT.Copy).then_inc(o_copied, 1)

            def attT_copy(i):
                take("attT", i)
                act.activation(attT[:, :], misc[:, 0:D], ACT.Copy).then_inc(attT_ready, 1)

            def finish(i, step):
                if step == 0:
                    sums_copy(i)
                elif step == 2:
                    attT_copy(i)

            def gate(layer, g, step):
                n = NG * layer + g
                if step == 2:
                    xT_copy(FFN_STAGE[layer], g)
                elif step == 3:
                    act.wait_ge(gate_arg, n + 1)
                    act.activation(gexp[:, :, :], gtmp[:, :, :], ACT.Exp).then_inc(gate_exp, 1)
                elif step == 5:
                    take("rT", FFN_STAGE[layer], g)
                    act.activation(rwT[:, GN * g:GN * g + GN], misc_b[0:PARTS * E, 0:GN], ACT.Copy).then_inc(rwT_ready, 1)

            def scan(g, step):
                if step == 2:
                    xT_copy(STAGE_B, g)
                elif step == 3:
                    take("tf", g)
                    act.activation(fg[PR:P, 0, :], misc[PR:P, :], ACT.Exp, scale=-1.0).then_inc(fg_exp, 1)
                    act.activation(tT[:, :], misc[0:PR, :], ACT.Copy).then_inc(t_ready, 1)
                elif step == 5:
                    take("lam", g)
                    act.activation(lam[:, 0, :], misc[0:PR, :], ACT.Exp, scale=-1.0).then_inc(lam_exp, 1)

            def beside(*place):
                for chain, at, step in SIDE.get(place, ()):
                    if chain == "q":
                        q_copy(*at, step)
                    elif chain == "shift" and step == 0:
                        shift_copy(*at)
                    elif chain == "finish":
                        finish(*at, step)
                    elif chain == "prep":
                        prep(*at, step)
                    elif chain == "sim" and step == 1:
                        act.wait_ge(tab_loaded, 16 * 3)
                        act.activation(gate_sig[:, :], gate_sig[:, :], ACT.Exp, scale=-1.0).then_inc(gates_exp, 1)
                    elif chain == "gate":
                        gate(*at, step)
                    elif chain == "scan":
                        scan(*at, step)

            for step in range(PREP_STEPS):
                prep(0, step)
            q_copy(0, 0)
            q_copy(0, 1)
            shift_copy(0)
            for i in range(NT):
                for slot in range(HB * (i + 1)):
                    exp_a(i, slot)
                    beside("A", st_n(i, slot))

            def project(stage, layer, g):
                for e in range(E + LAG):
                    beside("P", layer, g, e)
                act.wait_ge(xs_used, xs_n(layer, g, E - 1) + 1)
                act.activation(fvT[:, :], bank(5), ACT.Copy).then_inc(fqkv_copied, 1)
                act.activation(fqT[:, GN * g:GN * g + GN], bank(3), ACT.Copy).then_inc(fqkv_copied, 1)
                act.activation(fkT[:, GN * g:GN * g + GN], bank(4), ACT.Copy).then_inc(fqkv_copied, 1)
                take("v", stage, g)
                act.activation(fv[:, GT * g:GT * g + GT, :].rearrange("p a b -> p (a b)"), misc,
                               ACT.Copy).then_inc(fv_ready, 1)

            def exp_f(layer, i):
                n = NT * layer + i
                act.wait_ge(fshift_ready, n + 1)
                if n >= 2:
                    act.wait_ge(pT_used, weighed((n - 2) // NT, (n - 2) % NT))
                act.activation(fp[:, i % 2, 0:P * (i + 1)], psum[:, 0:P * (i + 1)], ACT.Exp,
                               bias=f_shift[:, i:i + 1], scale=SCALE_F, accum_out=f_sum[:, i:i + 1])\
                    .then_inc(fprobs_ready, 1)

            def aoT_copy(stage, i):
                take("aoT", stage, i)
                act.activation(aoT[:, P * i:P * i + P], misc[:, 0:P], ACT.Copy).then_inc(aoT_ready, 1)

            def pT_copy(stage, layer, i, c):
                n, key = pT_n(layer, i, c), ("pT", stage, i, c)
                w = P * min(GT, i + 1 - GT * c)
                act.wait_ge(pT_filled, n + 1)
                if n >= PT_RING:
                    act.wait_ge(pT_used, n - PT_RING + 1)
                act.activation(pT[:, n % PT_RING, 0:w], pair_bank(key)[:, 0:w], ACT.Copy)\
                    .then_inc(pT_copied[PAIR.slot(*key)], 1)

            def expert_attention(stage, layer):
                for g in range(NG):
                    project(stage, layer, g)
                exp_f(layer, 0)
                for g in range(NG):
                    for i in range(GT * g, GT * g + GT):
                        beside("T", layer, i, 0)
                        if i:
                            aoT_copy(stage, i - 1)
                        for c in range(min(2, i // GT + 1)):
                            pT_copy(stage, layer, i, c)
                        beside("T", layer, i, 1)
                        if i + 1 < NT:
                            exp_f(layer, i + 1)
                        beside("T", layer, i, 2)
                        for c in range(2, i // GT + 1):
                            pT_copy(stage, layer, i, c)
                        beside("T", layer, i, 3)
                aoT_copy(stage, NT - 1)

            expert_attention(STAGE_F0, 0)
            expert_attention(STAGE_F1, 1)

        @block.tensor
        def _(pe):
            def fill(*key):
                last = MISC.before(*key)
                if last:
                    pe.wait_ge(*misc_copied(*last))

            def transposes(key, into, pieces, identity):
                fill(*key)
                for o, src in zip(into, pieces):
                    last = pe.transpose(o, src, identity)
                last.then_inc(misc_ready, 1)

            def xT(stage, g):
                pe.wait_ge(xn_ready, NORM.n(stage, g) + 1)
                transposes(("xT", stage, g), [misc[:, P * a:P * a + P] for a in range(GT)],
                           [xn[:, GT * g + a, :] for a in range(GT)], ident[:, :])

            def prep(g, step):
                if step == 2:
                    xT(STAGE_A, g)
                elif step in (3, 4):
                    qkv_of(g, step - 3)
                elif step == 9:
                    k_transposes(g)

            def qkv_of(g, half):
                pe.wait_ge(xnT_ready, NORM.n(STAGE_A, g) + 1)
                w = D + 2 * HD
                fill("proj", g, half)
                for a in range(2):
                    t = GT * g + 2 * half + a
                    last = pe.matmul(misc[:, w * a:w * a + w], xnT[:, P * t:P * t + P], w_qkv[:, :],
                                     start=True, stop=True)
                last.then_inc(misc_ready, 1)

            def k_transposes(g):
                pe.wait_ge(kparts_ready, g + 1)
                transposes(("kT", g), [misc_b[0:ST_ROWS, P * a:P * a + P] for a in range(GT)],
                           [k_parts[:, a, 0:ST_ROWS] for a in range(GT)], ident_b[:, :])

            def q_transposes(i, half):
                pe.wait_ge(qparts_ready, i // GT + 1)
                transposes(("qT", i, half), [misc_b[0:QK_PAD, P * a:P * a + P] for a in range(8)],
                           [q_parts[:, i % (2 * GT), 8 * half + a, :] for a in range(8)], ident_b[:, :])

            def max_scores(i, u):
                h0, nh, k0, nk = max_units(i)[u]
                n = MX_BASE[i] + u
                w = nk * P
                if u == 0:
                    pe.wait_ge(qT_ready, 2 * (i + 1))
                    pe.wait_ge(kT_ready, i // GT + 1)
                if n >= MX_RING:
                    pe.wait_ge(mx_free, n - MX_RING + 1)
                diagonal = k0 + nk == i + 1
                for a in range(nh):
                    h = h0 + a
                    last = pe.matmul(mx_bank(n)[:, w * a:w * a + w], qT[0:QK_PAD, i % Q_RING, P * h:P * h + P],
                                     kT[0:QK_PAD, P * k0:P * k0 + w], start=True, stop=True)
                    if diagonal:
                        last = pe.matmul(mx_bank(n)[:, w * a + w - P:w * a + w], ident_b[:, :], mask_b[:, :],
                                         start=False, stop=True, skip_group_check=True)
                last.then_inc(mx_ready, 1)

            def shift_rows(i, half):
                pe.wait_ge(m_ready, i + 1)
                fill("shift", i, half)
                for a in range(8):
                    last = pe.transpose(misc_b[SHIFT_ROW:ST_ROWS, P * a:P * a + P],
                                        m_parts[:, i % 2, 8 * half + a, 0:PARTS], ident_b[:, :],
                                        tile_position=(0, SHIFT_ROW))
                last.then_inc(misc_ready, 1)

            def scores(i, slot):
                j, c = slot // HB, slot % HB
                n = st_n(i, slot)
                w = HB * P
                if slot == 0:
                    for half in range(2):
                        pe.wait_ge(shift_set[half], i + 1)
                if n >= ST_RING:
                    pe.wait_ge(probs_ready, n - ST_RING + 1)
                last = pe.matmul(st_bank(n), kT[0:ST_ROWS, P * j:P * j + P],
                                 qT[0:ST_ROWS, i % Q_RING, w * c:w * c + w], start=True, stop=j < i)
                if j == i:
                    last = pe.matmul(st_bank(n).rearrange("p (a b) -> p a b", a=HB), mask_b[:, :],
                                     ident_b[:, :].rearrange("p (o b) -> p o b", o=1).broadcast_to([P, HB, P]),
                                     start=False, stop=True)
                last.then_inc(st_ready, 1)

            def weigh_values(i, j):
                n = st_n(i, HB * j)
                pe.wait_ge(probs_ready, n + HB)
                if j == 0 and i > 0:
                    pe.wait_ge(o_copied, i)
                for c in range(HB):
                    last = pe.matmul(bank(6)[32 * c:32 * c + 32, :], v_ones[:, j, :], probs[:, (n + c) % P_RING, :],
                                     start=j == 0, stop=j == i, tile_position=(0, 32 * c), skip_group_check=True)
                last.then_inc(pv_done, 1)

            def finish_a(i, step):
                if step == 0:
                    pe.wait_ge(o_copied, i + 1)
                    transposes(("oT", i), [misc[:, P * a:P * a + P] for a in range(HB)],
                               [o_sb[:, P * a:P * a + P] for a in range(HB)], ident[:, :])
                elif step == 1:
                    pe.wait_ge(att_ready, i + 1)
                    transposes(("attT", i), [misc[:, 0:P]], [att[:, i % 2, :]], ident[:, :])
                else:
                    pe.wait_ge(attT_ready, i + 1)
                    if i == 0:
                        pe.wait_ge(wo_loaded, 16)
                    fill("wo", i)
                    pe.matmul(misc[:, 0:D], attT[:, :], w_o[:, :], start=True, stop=True).then_inc(misc_ready, 1)

            def gate(layer, g, step):
                stage, n = FFN_STAGE[layer], NG * layer + g
                if step == 2:
                    xT(stage, g)
                elif step == 3:
                    pe.wait_ge(xnT_ready, NORM.n(stage, g) + 1)
                    if n == 0:
                        pe.wait_ge(sim_ready, 1)
                    fill("logit", stage, g)
                    for a in range(GT):
                        t = GT * g + a
                        last = pe.matmul(misc[:, E * a:E * a + E], xnT[:, P * t:P * t + P], sim_n[:, :],
                                         start=True, stop=True)
                    last.then_inc(misc_ready, 1)
                elif step == 5:
                    pe.wait_ge(rparts_ready, n + 1)
                    transposes(("rT", stage, g), [misc_b[0:PARTS * E, P * a:P * a + P] for a in range(GT)],
                               [rw_parts[:, a, :, :].rearrange("p a b -> p (a b)") for a in range(GT)], ident_b[:, :])

            def scan(g, step):
                if step == 2:
                    xT(STAGE_B, g)
                elif step == 3:
                    pe.wait_ge(xnT_ready, NORM.n(STAGE_B, g) + 1)
                    if g == 0:
                        pe.wait_ge(wtf_ready, 1)
                    fill("tf", g)
                    pe.matmul(misc, w_tf[:, :], xnT[:, GN * g:GN * g + GN], start=True, stop=True).then_inc(misc_ready, 1)
                elif step == 5:
                    pe.wait_ge(fg_ready, g + 1)
                    fill("lam", g)
                    pe.matmul(misc[0:PR, :], w_lam[PR:P, :], fg[PR:P, 0, :], start=True, stop=True,
                              tile_position=(PR, 0)).then_inc(misc_ready, 1)
                elif step == 7:
                    fill("u", g)
                    pe.matmul(misc[0:PR, :], w_b[:, :], tT[:, :], start=True, stop=True).then_inc(misc_ready, 1)
                elif step == 8:
                    fill("c", g)
                    pe.matmul(misc[0:PR, :], w_c[:, :], s_seq[:, GN * g:GN * g + GN], start=True,
                              stop=True).then_inc(misc_ready, 1)
                elif step == 9:
                    fill("h", g)
                    for a in range(GT):
                        last = pe.matmul(misc[:, P * a:P * a + P], tt[:, P * a:P * a + P], w_p[:, :],
                                         start=True, stop=True)
                    last.then_inc(misc_ready, 1)

            def beside(*place):
                for chain, at, step in SIDE.get(place, ()):
                    if chain == "q":
                        q_transposes(*at, step)
                    elif chain == "shift":
                        shift_rows(*at, step)
                    elif chain == "finish" and step > 0:
                        finish_a(*at, step - 1)
                    elif chain == "prep":
                        prep(*at, step)
                    elif chain == "sim" and step == 1:
                        pe.wait_ge(consts, 3)
                        pe.wait_ge(sim_sq_ready, 1)
                        fill("sim")
                        pe.matmul(misc[:, 0:E], ones[:, :], sim_sq[:, :], start=True, stop=True).then_inc(misc_ready, 1)
                    elif chain == "gate":
                        gate(*at, step)
                    elif chain == "scan":
                        scan(*at, step)

            pe.wait_ge(consts, 1)
            pe.wait_ge(a_loaded, 16 * 3)
            for step in range(PREP_STEPS):
                prep(0, step)
            q_transposes(0, 0)
            q_transposes(0, 1)
            pe.wait_ge(consts, 2)
            for u in range(len(max_units(0))):
                max_scores(0, u)
            shift_rows(0, 0)
            shift_rows(0, 1)
            for i in range(NT):
                for slot in range(HB * (i + 1)):
                    scores(i, slot)
                    if slot == HB - 1 and i > 0:
                        weigh_values(i - 1, i - 1)
                    beside("A", st_n(i, slot))
                    for unit in MAX_PLAN[st_n(i, slot)]:
                        max_scores(*unit)
                    if slot % HB == HB - 1 and slot >= HB:
                        weigh_values(i, slot // HB - 1)
            weigh_values(NT - 1, NT - 1)

            def spread_weight(ps, g, e):
                pe.matmul(ps, spread[:, e, :], rwT[:, GN * g:GN * g + GN], start=True, stop=True).then_inc(rb_ready, 1)

            def project(stage, layer, g):
                n = NG * layer + g
                if n == 0:
                    pe.wait_ge(f_loaded, 16 * 4)
                pe.wait_ge(rwT_ready, n + 1)
                for e in range(E + LAG):
                    beside("P", layer, g, e)
                    if e < E:
                        k = xs_n(layer, g, e)
                        if k >= 3:
                            pe.wait_ge(xs_ready, k - 2)
                        spread_weight(bank(k % 3), g, e)
                    if e >= LAG:
                        k = xs_n(layer, g, e - LAG)
                        pe.wait_ge(xs_ready, k + 1)
                        if e == LAG and n > 0:
                            pe.wait_ge(fqkv_copied, 3 * n)
                        for w, b in zip("qkv", (3, 4, 5)):
                            last = pe.matmul(bank(b), fw[w][:, e - LAG, :], xs[:, k % XS_RING, :],
                                             start=e == LAG, stop=e == E + LAG - 1)
                        last.then_inc(xs_used, 1)
                pe.wait_ge(fqkv_copied, 3 * n + 1)
                transposes(("v", stage, g), [misc[:, P * a:P * a + P] for a in range(GT)],
                           [fvT[:, P * a:P * a + P] for a in range(GT)], ident[:, :])

            def scores_f(layer, i):
                n, L = NT * layer + i, P * (i + 1)
                if i % GT == 0:
                    pe.wait_ge(fqkv_copied, 3 * (NG * layer + i // GT + 1))
                if i:
                    pe.wait_ge(fprobs_ready, n)
                for k0 in range(0, L, GN):
                    w = min(GN, L - k0)
                    pe.matmul(psum[:, k0:k0 + w], fqT[:, P * i:P * i + P], fkT[:, k0:k0 + w],
                              start=True, stop=True)
                pe.matmul(psum[:, L - P:L], ident_b[:, :], mask_b[:, :], start=False, stop=True,
                          skip_group_check=True).then_inc(fs_ready, 1)

            def pair_fill(*key):
                last = PAIR.before(*key)
                if last and last[0] == "pT":
                    pe.wait_ge(pT_copied[PAIR.slot(*key)], pT_copies(last))
                elif last:
                    pe.wait_ge(out_scaled, scaled_n(int(last[1] == STAGE_F1), last[2], OE * last[3] + OE))

            def transpose_probs(stage, layer, i, c):
                key = ("pT", stage, i, c)
                if c == 0:
                    pe.wait_ge(fprobs_ready, NT * layer + i + 1)
                pair_fill(*key)
                for a in range(min(GT, i + 1 - GT * c)):
                    k0 = P * (GT * c + a)
                    last = pe.transpose(pair_bank(key)[:, P * a:P * a + P], fp[:, i % 2, k0:k0 + P], ident[:, :])
                last.then_inc(pT_filled, 1)

            def weigh_f(stage, layer, i, c):
                n, key = pT_n(layer, i, c), ("pT", stage, i, c)
                pe.wait_ge(pT_copied[PAIR.slot(*key)], pT_copies(key))
                if c == 0:
                    pe.wait_ge(fv_ready, NG * layer + i // GT + 1)
                    if i:
                        pe.wait_ge(ao_ready, NT * layer + i)
                for a in range(min(GT, i + 1 - GT * c)):
                    j = GT * c + a
                    last = pe.matmul(bank(6)[:, 0:D], pT[:, n % PT_RING, P * a:P * a + P], fv[:, j, :],
                                     start=j == 0, stop=j == i)
                last.then_inc(pT_used, 1)

            def expert_outputs(stage, layer, i, c):
                if c == 0:
                    pe.wait_ge(aoT_ready, NT * layer + i + 1)
                pair_fill("out", stage, i, c)
                pe.matmul(pair_bank(("out", stage, i, c)), aoT[:, P * i:P * i + P],
                          fw["o"][:, OE * c:OE * c + OE, :].rearrange("p e d -> p (e d)"),
                          start=True, stop=True).then_inc(out_filled, 1)

            def turn_output(stage, layer, i):
                pe.wait_ge(ao_ready, NT * layer + i + 1)
                transposes(("aoT", stage, i), [misc[:, 0:P]], [ao[:, i % 2, :]], ident[:, :])

            def row(stage, layer, i):
                if i:
                    turn_output(stage, layer, i - 1)
                for kind, c in row_steps(i):
                    if kind == "pT":
                        transpose_probs(stage, layer, i, c)
                    elif kind == "av":
                        weigh_f(stage, layer, i, c)
                    elif kind == "out":
                        expert_outputs(stage, layer, i - 1, c)
                    else:
                        beside("T", layer, i, c)

            def expert_attention(stage, layer):
                for g in range(NG):
                    project(stage, layer, g)
                scores_f(layer, 0)
                for g in range(NG):
                    for i in range(GT * g, GT * g + GT):
                        beside("T", layer, i, 0)
                        if i + 1 < NT:
                            scores_f(layer, i + 1)
                        row(stage, layer, i)
                row(stage, layer, NT)

            expert_attention(STAGE_F0, 0)
            expert_attention(STAGE_F1, 1)

        @block.vector
        def _(dve):
            steps = [0]

            def after(ins):
                steps[0] += 1
                ins.then_inc(dve_step, 1)
                dve.wait_ge(dve_step, steps[0])

            def take(*key):
                dve.wait_ge(misc_ready, MISC.n(*key) + 1)

            def wide(col, shape):
                return col.broadcast_to(shape)

            def moments(stage, g):
                tiles = range(GT * g, GT * g + GT)
                a, b = GT * g, GT * g + GT
                if stage == STAGE_A:
                    dve.wait_ge(x_loaded[g], 16)
                else:
                    dve.wait_ge(x_new, x_new_n(stage - 1, g))
                for t in tiles:
                    last = dve.bn_stats(stats[:, t - a, :], X[:, t, :])
                after(last)
                for t in tiles:
                    last = dve.bn_aggr(mean_var[:, t, :], stats[:, t - a, :])
                after(last)
                dve.tensor_scalar(var_eps[:, a:b], mean_var[:, a:b, 1], EPS, None, ALU.add).then_inc(var_ready, 1)

            def normalise(stage, g):
                dve.wait_ge(rstd_ready, NORM.n(stage, g) + 1)
                for t in range(GT * g, GT * g + GT):
                    last = dve.tensor_scalar(xn[:, t, :], X[:, t, :], mean_var[:, t, 0:1], rstd[:, t:t + 1],
                                             ALU.subtract, ALU.mult)
                last.then_inc(xn_ready, 1)

            def split_part(part, src, outs, rest_out=None, first=None):
                for o, v in outs:
                    last = dve.tensor_copy(o, v)
                if rest_out is None:
                    return last
                after(last)
                after(dve.tensor_tensor(rest_out, src, first, ALU.subtract))

            def prep(g, step):
                a, b = GT * g, GT * g + GT
                if step == 0:
                    moments(STAGE_A, g)
                elif step == 1:
                    normalise(STAGE_A, g)
                elif step in (3, 4):
                    add_bias(g, step - 3)
                    if step == 4:
                        dve.wait_ge(proj_copied, 2 * (g + 1))
                        rotate(g)
                elif step == 5:
                    for part in range(PARTS):
                        k_part(g, part)
                elif step in (6, 7, 8):
                    q_part(g, step - 6)

            def add_bias(g, half):
                if g == 0 and half == 0:
                    dve.wait_ge(rot_loaded, 16 * 5)
                take("proj", g, half)
                w = D + 2 * HD
                dve.tensor_tensor(qkv[:, 2 * half:2 * half + 2, :],
                                  misc[:, 0:2 * w].rearrange("p (a b) -> p a b", a=2),
                                  b_qkv[:, :].rearrange("p (o b) -> p o b", o=1).broadcast_to([P, 2, w]),
                                  ALU.add).then_inc(proj_copied, 1)

            def rotate(g):
                a, b = GT * g, GT * g + GT
                qk = qkv[:, :, 0:D + HD].rearrange("p t (h d) -> p t h d", d=HD)
                q2 = HH // 2
                hs = [P, GT, H + 1, q2]
                c = cos_t[:, a:b, :].rearrange("p t (o d) -> p t o d", o=1)
                sn = sin_t[:, a:b, :].rearrange("p t (o d) -> p t o d", o=1)
                dve.tensor_tensor(turn_c[:, :, :, :], qk[:, :, :, 0:HH], c.broadcast_to([P, GT, H + 1, HH]), ALU.mult)
                dve.tensor_tensor(turn_s[:, :, :, 0:q2], qk[:, :, :, q2:HH], sn[:, :, :, 0:q2].broadcast_to(hs), ALU.mult)
                after(dve.tensor_tensor(turn_s[:, :, :, q2:HH], qk[:, :, :, 0:q2], sn[:, :, :, q2:HH].broadcast_to(hs), ALU.mult))
                dve.tensor_copy(v_ones[:, a:b, 0:HD], qkv[:, :, D + HD:D + 2 * HD])
                after(dve.tensor_tensor(qk[:, :, :, 0:HH], turn_c[:, :, :, :], turn_s[:, :, :, :], ALU.add))

            def k_part(g, part):
                if part == 0 and g:
                    dve.wait_ge(misc_ready, MISC.n("kT", g - 1) + 1)
                kp = k_parts[:, :, 0:QK_ROWS].rearrange("p t (a b d) -> p t a b d", a=PARTS, b=PARTS)
                src = rest[:, :, H, :] if part else qkv[:, :, D:D + HD]
                outs = [(kp[:, :, :, part, :],
                         src.rearrange("p t (o d) -> p t o d", o=1).broadcast_to([P, GT, PARTS, HD]))]
                if part < PARTS - 1:
                    split_part(part, src, outs, rest[:, :, H, :], kp[:, :, 0, part, :])
                else:
                    split_part(part, src, outs).then_inc(kparts_ready, 1)

            def q_part(g, part):
                if part == 0 and g >= 2:
                    dve.wait_ge(misc_ready, MISC.n("qT", GT * (g - 1) - 1, 1) + 1)
                s = GT * g % (2 * GT)
                qp = q_parts[:, s:s + GT, :, 0:QK_ROWS].rearrange("p t h (a b d) -> p t h a b d", a=PARTS, b=PARTS)
                src = rest[:, :, 0:H, :] if part else qkv[:, :, 0:D].rearrange("p t (h d) -> p t h d", d=HD)
                outs = [(qp[:, t, :, part, :, :],
                         src[:, t, :, :].rearrange("p h (o d) -> p h o d", o=1).broadcast_to([P, H, PARTS, HD]))
                        for t in range(GT)]
                if part < PARTS - 1:
                    split_part(part, src, outs, rest[:, :, 0:H, :], qp[:, :, :, part, 0, :])
                else:
                    split_part(part, src, outs).then_inc(qparts_ready, 1)

            def max_reduce(i, u):
                h0, nh, k0, nk = max_units(i)[u]
                n, pieces = MX_BASE[i] + u, max_pieces(i)
                o = m[:, h0:h0 + nh] if pieces == 1 else m_part[:, h0, u % pieces:u % pieces + 1]
                dve.wait_ge(mx_ready, n + 1)
                dve.tensor_reduce(o, mx_bank(n)[:, 0:nh * nk * P].rearrange("p (a b) -> p a b", a=nh),
                                  AX_X, ALU.max).then_inc(mx_free, 1)

            def shift_parts(i):
                dve.wait_ge(mx_free, MX_BASE[i + 1])
                if max_pieces(i) > 1:
                    after(dve.tensor_reduce(m[:, :], m_part[:, :, 0:max_pieces(i)], AX_X, ALU.max))
                mp = m_parts[:, i % 2, :, :]
                after(dve.tensor_scalar(mp[:, :, 0], m[:, :], -1.0, None, ALU.mult))
                after(dve.scalar_tensor_tensor(out=m_rest[:, 0, :], in0=m[:, :], scalar=-1.0, in1=mp[:, :, 0],
                                               op0=ALU.mult, op1=ALU.subtract))
                after(dve.tensor_copy(mp[:, :, 1], m_rest[:, 0, :]))
                after(dve.tensor_tensor(m_rest[:, 1, :], m_rest[:, 0, :], mp[:, :, 1], ALU.subtract))
                dve.tensor_copy(mp[:, :, 2], m_rest[:, 1, :]).then_inc(m_ready, 1)

            def shift_copy(i):
                take("shift", i, 1)
                dve.tensor_copy(qT[SHIFT_ROW:ST_ROWS, i % Q_RING, 1024:2048], misc_b[SHIFT_ROW:ST_ROWS, :])\
                    .then_inc(shift_set[1], 1)

            def finish_a(i, step):
                if step == 0:
                    take("oT", i)
                    o = misc.rearrange("p (a c d) -> p a c d", a=HB, c=HB)
                    after(dve.reciprocal(den[:, :, :], o[:, :, :, HD]))
                    dve.tensor_tensor(att[:, i % 2, :].rearrange("p (c a d) -> p a c d", c=HB, a=HB),
                                      o[:, :, :, 0:HD],
                                      den[:, :, :].rearrange("p a (c o) -> p a c o", o=1).broadcast_to([P, HB, HB, HD]),
                                      ALU.mult).then_inc(att_ready, 1)
                elif step == 2:
                    take("wo", i)
                    dve.tensor_tensor(wo_out[:, :], misc[:, 0:D], b_o[:, :], ALU.add).then_inc(wo_copied, 1)
                    dve.wait_ge(wo_copied, i + 1)
                    dve.tensor_tensor(X[:, i, :], X[:, i, :], wo_out[:, :], ALU.add).then_inc(x_new, 1)

            dve.memset(q_parts[:, :, :, QK_ROWS:QK_PAD], 0.0)
            dve.memset(k_parts[:, :, QK_ROWS:QK_PAD], 0.0)
            dve.memset(k_parts[:, :, SHIFT_ROW:ST_ROWS], 1.0)
            dve.memset(v_ones[:, :, HD:HD + 1], 1.0)
            after(dve.memset(v_ones[:, :, HD + 1:32], 0.0))
            def sim_step(step):
                if step == 0:
                    dve.wait_ge(tab_loaded, 16 * 3)
                    dve.tensor_tensor(sim_sq[:, :], sim_sb[:, :], sim_sb[:, :], ALU.mult).then_inc(sim_sq_ready, 1)
                elif step == 1:
                    take("sim")
                    dve.tensor_scalar(sim_sq[:, :], misc[:, 0:E], NORM_EPS, None, ALU.add).then_inc(sim_var, 1)
                elif step == 2:
                    dve.wait_ge(gates_exp, 1)
                    after(dve.tensor_scalar(gate_sig[:, :], gate_sig[:, :], 1.0, None, ALU.add))
                    after(dve.reciprocal(gate_sig[:, :], gate_sig[:, :]))
                    dve.wait_ge(sim_pow, 1)
                    dve.tensor_tensor(sim_n[:, :], sim_sb[:, :], sim_sq[:, :], ALU.mult).then_inc(sim_ready, 1)
                elif step == 3:
                    dve.wait_ge(b_loaded, 16 * 8)
                    after(dve.tensor_tensor(w_u[:, :, :], w_u[:, :, :], w_v[:, :, :], ALU.mult))
                    after(dve.tensor_reduce(w_uv[:, :], w_u[:, :, :], AX_X, ALU.add))
                    dve.tensor_tensor(w_tf[:, 0:PR], w_tf[:, 0:PR], w_uv[:, :], ALU.add).then_inc(wtf_ready, 1)

            def gates_of(layer, g):
                n = NG * layer + g
                eg = [P, GT, E]
                stage = FFN_STAGE[layer]
                if n == 0:
                    dve.wait_ge(consts, 4)
                a, b = GT * g, GT * g + GT
                take("logit", stage, g)
                dve.wait_ge(x_inv_ready, n + 1)
                dve.tensor_tensor(logits[:, :, :], misc[:, 0:GT * E].rearrange("p (t e) -> p t e", t=GT),
                                  x_inv[:, a:b].rearrange("p (t o) -> p t o", o=1).broadcast_to(eg),
                                  ALU.mult).then_inc(logit_copied, 1)
                dve.wait_ge(logit_copied, n + 1)
                after(dve.tensor_tensor(logits[:, :, :], logits[:, :, :],
                                        gate_sig[:, :].rearrange("p (o e) -> p o e", o=1).broadcast_to(eg), ALU.subtract))
                for t in range(GT):
                    last = dve.max(top[:, t, :], logits[:, t, :])
                after(last)
                for t in range(GT):
                    last = dve.max_index(top_no[:, t, :], top[:, t, :], logits[:, t, :])
                after(last)
                after(dve.tensor_copy(top_nof[:, :, :], top_no[:, :, 0:2]))
                numbers = expert_no[:, :].rearrange("p (o e) -> p o e", o=1).broadcast_to(eg)
                dve.tensor_tensor(pick[:, 0, :, :], numbers, top_nof[:, :, 0:1].broadcast_to(eg), ALU.is_equal)
                after(dve.tensor_tensor(pick[:, 1, :, :], numbers, top_nof[:, :, 1:2].broadcast_to(eg), ALU.is_equal))
                dve.tensor_tensor(pick[:, 0, :, :], pick[:, 0, :, :], pick[:, 1, :, :], ALU.add)
                dve.tensor_scalar(gcol[:, 0, :], top[:, :, 0], 0.0, None, ALU.is_le)
                after(dve.tensor_scalar(gcol[:, 1, :], top[:, :, 0], 0.0, None, ALU.max))
                dve.tensor_scalar(on[:, :, :], logits[:, :, :], 0.0, None, ALU.is_gt)
                dve.tensor_scalar(gtmp[:, :, :], logits[:, :, :], 0.0, None, ALU.max)
                col = lambda c: gcol[:, c, :].rearrange("p (t o) -> p t o", o=1).broadcast_to(eg)
                after(dve.tensor_tensor(pick[:, 0, :, :], pick[:, 0, :, :], col(0), ALU.mult))
                after(dve.tensor_tensor(on[:, :, :], on[:, :, :], pick[:, 0, :, :], ALU.add))
                dve.tensor_tensor(gtmp[:, :, :], gtmp[:, :, :], col(1), ALU.subtract).then_inc(gate_arg, 1)

            def gate_softmax(layer, g):
                n = NG * layer + g
                col = lambda c: gcol[:, c, :].rearrange("p (t o) -> p t o", o=1).broadcast_to([P, GT, E])
                dve.wait_ge(gate_exp, n + 1)
                w = rw[:, GT * g:GT * g + GT, :]
                after(dve.tensor_tensor(w, gexp[:, :, :], on[:, :, :], ALU.mult))
                after(dve.tensor_reduce(gcol[:, 2, :], w, AX_X, ALU.add))
                after(dve.reciprocal(gcol[:, 0, :], gcol[:, 2, :]))
                after(dve.tensor_tensor(w, w, col(0), ALU.mult))
                if n:
                    dve.wait_ge(misc_ready, MISC.n("rT", FFN_STAGE[(n - 1) // NG], (n - 1) % NG) + 1)
                for part in range(PARTS):
                    src = rw_rest[:, :, :] if part else w
                    o = rw_parts[:, :, part, :]
                    if part < PARTS - 1:
                        split_part(part, src, [(o, src)], rw_rest[:, :, :], o)
                    else:
                        split_part(part, src, [(o, src)]).then_inc(rparts_ready, 1)

            def scale_tile(k, weights, src):
                dve.wait_ge(rb_ready, k + 1)
                if k >= XS_RING:
                    dve.wait_ge(xs_used, k - XS_RING + 1)
                dve.tensor_tensor(xs[:, k % XS_RING, :], weights, src, ALU.mult).then_inc(xs_ready, 1)

            def gate(layer, g, step):
                a, b = GT * g, GT * g + GT
                stage = FFN_STAGE[layer]
                if step == 0:
                    moments(stage, g)
                elif step == 1:
                    normalise(stage, g)
                    dve.wait_ge(xn_ready, NORM.n(stage, g) + 1)
                    for t in range(a, b):
                        last = dve.tensor_tensor_reduce(sq_junk[:, t - a, :], xn[:, t, :], xn[:, t, :], 1.0, 0.0,
                                                        ALU.mult, ALU.add, sq_sum[:, t:t + 1])
                    after(last)
                    dve.tensor_scalar(sq_sum[:, a:b], sq_sum[:, a:b], NORM_EPS, None, ALU.add).then_inc(sq_ready, 1)
                elif step == 3:
                    gates_of(layer, g)
                elif step == 4:
                    gate_softmax(layer, g)

            def add_to_x(g):
                a, b = GT * g, GT * g + GT
                dve.tensor_tensor(X[:, a:b, :], X[:, a:b, :], misc.rearrange("p (t d) -> p t d", t=GT),
                                  ALU.add).then_inc(x_new, 1)

            def scan(g, step):
                if step == 0:
                    moments(STAGE_B, g)
                elif step == 1:
                    normalise(STAGE_B, g)
                elif step == 4:
                    dve.wait_ge(fg_exp, g + 1)
                    after(dve.tensor_scalar(fg[PR:P, 1, :], fg[PR:P, 0, :], 1.0, None, ALU.add))
                    dve.reciprocal(fg[PR:P, 0, :], fg[PR:P, 1, :]).then_inc(fg_ready, 1)
                elif step == 6:
                    dve.wait_ge(lam_exp, g + 1)
                    after(dve.tensor_scalar(lam[:, 1, :], lam[:, 0, :], 1.0, None, ALU.add))
                    after(dve.reciprocal(lam[:, 0, :], lam[:, 1, :]))
                elif step == 7:
                    take("u", g)
                    if g:
                        dve.wait_ge(s_ready, g)
                    dve.tensor_tensor_scan(s_seq[:, GN * g:GN * g + GN], lam[:, 0, :], misc[0:PR, :],
                                           s_seq[:, GN * g - 1:GN * g] if g else 0.0, ALU.mult, ALU.add)\
                        .then_inc(s_ready, 1)
                elif step == 8:
                    take("c", g)
                    dve.tensor_tensor(tt[:, :], misc[0:PR, :], tT[:, :], ALU.add).then_inc(tt_ready, 1)
                elif step == 9:
                    take("h", g)
                    add_to_x(g)

            def beside(*place):
                for chain, at, step in SIDE.get(place, ()):
                    if chain == "shift" and step == 1:
                        shift_copy(*at)
                    elif chain == "finish" and step > 0:
                        finish_a(*at, step - 1)
                    elif chain == "prep":
                        prep(*at, step)
                    elif chain == "sim":
                        sim_step(step)
                    elif chain == "gate":
                        gate(*at, step)
                    elif chain == "scan":
                        scan(*at, step)

            for step in range(PREP_STEPS):
                prep(0, step)
            for u in range(len(max_units(0))):
                max_reduce(0, u)
            shift_parts(0)
            shift_copy(0)
            for slot in range(first_slot(NT)):
                beside("A", slot)
                for unit in MAX_PLAN[slot]:
                    max_reduce(*unit)
                for i in range(1, NT):
                    if slot == max_window(i)[1] - 1:
                        shift_parts(i)

            def project(stage, layer, g):
                dve.wait_ge(xnT_ready, NORM.n(stage, g) + 1)
                for e in range(E + LAG):
                    beside("P", layer, g, e)
                    if e < E:
                        k = xs_n(layer, g, e)
                        scale_tile(k, bank(k % 3), xnT[:, GN * g:GN * g + GN])

            def max_f(layer, i):
                dve.wait_ge(fs_ready, NT * layer + i + 1)
                after(dve.tensor_reduce(fm[:, i:i + 1], psum[:, 0:P * (i + 1)], AX_X, ALU.max))
                dve.tensor_scalar(f_shift[:, i:i + 1], fm[:, i:i + 1], -SCALE_F, None, ALU.mult).then_inc(fshift_ready, 1)

            def sum_experts(stage, layer, i, c):
                dve.wait_ge(out_filled, (NT * layer + i) * GT + c + 1)
                ps = pair_bank(("out", stage, i, c))
                for e in range(OE * c, OE * c + OE):
                    n = scaled_n(layer, i, e)
                    o, src = out_sum[:, e % 2, :], ps[:, D * (e % OE):D * (e % OE) + D]
                    if e < 2:
                        dve.tensor_scalar(o, src, rw[:, i, e:e + 1], None, ALU.mult).then_inc(out_scaled, 1)
                    else:
                        dve.wait_ge(out_scaled, n - 1)
                        dve.scalar_tensor_tensor(out=o, in0=src, scalar=rw[:, i, e:e + 1], in1=o,
                                                 op0=ALU.mult, op1=ALU.add).then_inc(out_scaled, 1)
                if c == GT - 1:
                    dve.wait_ge(out_scaled, scaled_n(layer, i, E))
                    after(dve.tensor_tensor(out_sum[:, 0, :], out_sum[:, 0, :], out_sum[:, 1, :], ALU.add))
                    last = dve.tensor_tensor(X[:, i, :], X[:, i, :], out_sum[:, 0, :], ALU.add)
                    if i % GT == GT - 1:
                        last.then_inc(x_new, 1)

            def attend_f(layer, i):
                n = NT * layer + i
                dve.wait_ge(fprobs_ready, n + 1)
                after(dve.reciprocal(f_inv[:, i:i + 1], f_sum[:, i:i + 1]))
                dve.wait_ge(pT_used, weighed(layer, i))
                dve.tensor_scalar(ao[:, i % 2, :], bank(6)[:, 0:D], f_inv[:, i:i + 1], None, ALU.mult).then_inc(ao_ready, 1)

            def expert_attention(stage, layer):
                for g in range(NG):
                    project(stage, layer, g)
                max_f(layer, 0)
                for g in range(NG):
                    for i in range(GT * g, GT * g + GT):
                        beside("T", layer, i, 0)
                        if i + 1 < NT:
                            max_f(layer, i + 1)
                        if i:
                            sum_experts(stage, layer, i - 1, 0)
                        beside("T", layer, i, 1)
                        if i:
                            sum_experts(stage, layer, i - 1, 1)
                        beside("T", layer, i, 2)
                        if i:
                            sum_experts(stage, layer, i - 1, 2)
                            sum_experts(stage, layer, i - 1, 3)
                        attend_f(layer, i)
                        beside("T", layer, i, 3)
                for c in range(GT):
                    sum_experts(stage, layer, NT - 1, c)

            expert_attention(STAGE_F0, 0)
            expert_attention(STAGE_F1, 1)


_INS = ["L0_attn_a_x", "L0_attn_a_Wq", "L0_attn_a_bq", "L0_attn_a_Wk", "L0_attn_a_bk", "L0_attn_a_Wv",
        "L0_attn_a_bv", "L0_attn_a_Wo", "L0_attn_a_bo", "L0_attn_b_W_toP", "L0_attn_b_W_U", "L0_attn_b_W_F",
        "L0_attn_b_W_V", "L0_attn_b_W_lam", "L0_attn_b_B_mat", "L0_attn_b_C_mat", "L0_attn_b_W_fromP",
        "L0_ffn_sim_matrix", "L0_ffn_gates", "L0_ffn_q_proj", "L0_ffn_k_proj", "L0_ffn_v_proj",
        "L0_ffn_o_proj"]
_OUTS = [((1, 2048, 128), "float32")]


def _rotation_tables():
    import numpy as np
    theta = np.float32(10000.0) ** (-np.arange(HH, dtype=np.float32) / np.float32(HH))
    angle = np.arange(T, dtype=np.float32)[:, None] * theta[None, :].astype(np.float32)
    sign = np.where(np.arange(HH) < HH // 2, -1.0, 1.0).astype(np.float32)
    tables = np.cos(angle).astype(np.float32), (np.sin(angle) * sign).astype(np.float32)
    return [np.ascontiguousarray(a.reshape(NT, P, HH).transpose(1, 0, 2)) for a in tables]


def kernel(**inputs):
    import numpy as _np
    import concourse.bacc as _bacc
    from concourse import mybir as _mybir
    from concourse.bass_utils import run_bass_kernel_spmd as _run

    nc = _bacc.Bacc("TRN2", target_bir_lowering=False, num_devices=1)
    cos, sin = _rotation_tables()
    named = [(name, inputs[name]) for name in _INS] + [("cos", cos), ("sin", sin)]
    arrays, args = {}, []
    for name, value in named:
        a = _np.ascontiguousarray(value)
        arrays[f"in_{name}_dram"] = a
        args.append(nc.dram_tensor(f"in_{name}_dram", a.shape, _mybir.dt.from_np(a.dtype), kind="ExternalInput").ap())
    for i, (shape, dtype) in enumerate(_OUTS):
        dt = _mybir.dt.from_np(_np.dtype(dtype))
        args.append(nc.dram_tensor(f"out_{i}_dram", shape, dt, kind="ExternalOutput").ap())
    hybrid_block_kernel(nc, *args)
    r = _run(nc, [arrays], core_ids=[0])
    return r.results[0]["out_0_dram"]
```

```python
from contextlib import ExitStack

import concourse.bass as bass
from concourse import mybir

F32 = mybir.dt.float32
BF16 = mybir.dt.bfloat16
F32R = mybir.dt.float32r
U32 = mybir.dt.uint32
ALU = mybir.AluOpType
ACT = mybir.ActivationFunctionType
AX_X = mybir.AxisListType.X

P = 128
T = 2048
D = 128
NT = T // P
GT = 4
GN = GT * P
NG = NT // GT
H = 16
HD = D // H
HH = HD // 2
HB = 4
E = 16
PR = 64
ALPHA = 4
EPS = 1e-5
NORM_EPS = 1e-12
SCALE_A = float(HD) ** -0.5
SCALE_F = float(D) ** -0.5
MASKED = -1e30
PARTS = 3
QK_ROWS = PARTS * PARTS * HD
SHIFT_ROW = 96
QK_PAD = SHIFT_ROW
ST_ROWS = SHIFT_ROW + PARTS
MX_RING, ST_RING, P_RING, PT_RING = 3, 3, 8, 4
XS_RING, XS_HALVES_RING = 2, 3
HI, LO = range(2)
STAGE_A, STAGE_F0, STAGE_B, STAGE_F1 = range(4)
SHARE = 1.0
LEAD = 12
PREP_STEPS = 10
OE = 4
SHARES = 2
LAG = 2
V_TURN = LAG + 1
Q_RING = 3


class Uses:

    def __init__(self, keys, slots=1):
        self.at = {key: n for n, key in enumerate(keys)}
        self.keys = keys
        self.slots = slots

    def n(self, *key):
        return self.at[key]

    def before(self, *key):
        n = self.at[key] - self.slots
        return self.keys[n] if n >= 0 else None

    def slot(self, *key):
        return self.at[key] % self.slots


def max_units(i):
    nb = i + 1
    if nb <= GT:
        nh = GT // nb
        return [(h, min(nh, H - h), 0, nb) for h in range(0, H, nh)]
    pieces = -(-nb // GT)
    cuts = [nb * c // pieces for c in range(pieces + 1)]
    return [(h, 1, cuts[c], cuts[c + 1] - cuts[c]) for h in range(H) for c in range(pieces)]


def max_pieces(i):
    return max(1, -(-(i + 1) // GT))


def first_slot(i):
    return HB * (i * (i + 1) // 2)


def lead(i):
    return min(LEAD, 3 * i // 2 + 1)


def max_window(i):
    return 0 if i == 1 else first_slot(i - 1) - lead(i - 1), first_slot(i) - lead(i)


STEP_WORK = {"prep": (1.3, 1.2, 0, .6, 2.5, 1.4, 2.2, 2.2, 1.4, 0), "gate": (1.3, 2.2, 0, 3.5, 2, 0),
             "finish": (0, .4, 0, .5), "sim": (.2, .2, .5, 1)}


def max_plan(share=SHARE):
    free, backlog = [], 0.0
    for slot in range(first_slot(NT)):
        backlog += sum(STEP_WORK[chain][step] for chain, at, step in SIDE.get(("A", slot), ()) if chain in STEP_WORK)
        now = min(backlog, share)
        backlog -= now
        free.append(1.0 - now)
    plan = [[] for _ in range(first_slot(NT))]
    for i in range(1, NT):
        (lo, hi), n = max_window(i), len(max_units(i))
        total, done, u = sum(free[lo:hi]), 0.0, 0
        for slot in range(lo, hi):
            while u < n and u * total / n < done + free[slot] or (u < n and slot == hi - 1):
                plan[slot].append((i, u))
                u += 1
            done += free[slot]
    return plan


def side_plan():
    plan = {}

    def put(chain, at, places):
        for step, place in enumerate(places):
            plan.setdefault(place, []).append((chain, at, step))

    for i in range(1, NT):
        lo, s, last = max_window(i)[0], first_slot(i), first_slot(i + 1) - 1
        q = max(lo - 6, first_slot(i - Q_RING + 1) if i >= Q_RING else 0)
        put("q", (i,), [("A", q), ("A", min(max(lo - 3, q), lo))])
        put("shift", (i,), [("A", s - max(2, 2 * lead(i) // 3)), ("A", s - max(1, lead(i) // 3))])
        put("finish", (i - 1,), [("A", s + 3), ("A", min(s + 5, last)), ("A", min(s + 9, last)), ("A", min(s + 13, last))])
    put("finish", (NT - 1,), [("P", 0, 0, e) for e in (0, 1, 3, 5)])
    for g, first in ((1, 0), (2, 62), (3, 184)):
        steps = (0, 1, 3, 5, 6, 8, 9, 10, 11, 13) if g == 1 else (0, 3, 6, 8, 10, 13, 16, 19, 22, 25)
        put("prep", (g,), [("A", first + n) for n in steps])
    put("sim", (), [("A", n) for n in (24, 28, 32, 36)])
    for g, first in ((0, 90), (1, 210), (2, 340)):
        put("gate", (0, g), [("A", first + n) for n in (0, 3, 7, 11, 15, 20)])
    put("gate", (0, 3), [("P", 0, 0, e) for e in (7, 8, 9, 11, 13, 15)])
    for g in range(1, NG):
        at = [("T", 0, GT * g + k, n) for k in range(GT) for n in range(GT)]
        put("scan", (g - 1,), [at[n] for n in (5, 6, 7, 8, 8, 10, 11, 13, 14, 15)])
        if g > 1:
            put("gate", (1, g - 2), at[2:14:2])
    put("scan", (NG - 1,), [("P", 1, 0, e) for e in (4, 5, 6, 8, 10, 11, 12, 13, 14, 15)])
    put("gate", (1, NG - 2), [("P", 1, 0, e) for e in (0, 3, 4, 7, 9, 11)])
    put("gate", (1, NG - 1), [("P", 1, 1, e) for e in (1, 2, 4, 7, 9, 13)])
    return plan


def places():
    for slot in range(first_slot(NT)):
        yield ("A", slot)
    for layer in range(2):
        for g in range(NG):
            for e in range(E):
                yield ("P", layer, g, e)
                if g and e == V_TURN:
                    yield ("v", layer, g - 1)
        yield ("v", layer, NG - 1)
        for g in range(NG):
            for i in range(GT * g, GT * g + GT):
                yield ("T", layer, i, 0)
                if i:
                    yield ("aoT", layer, i - 1)
                if i > 1:
                    yield ("ffn", layer, i - 2)
                for n in range(1, GT):
                    yield ("T", layer, i, n)
        yield ("aoT", layer, NT - 1)
        yield ("ffn", layer, NT - 2)
        yield ("ffn", layer, NT - 1)


def row_steps(i):
    last = i // GT if i < NT else -1
    steps = []
    if i < NT:
        steps += [("pT", c) for c in range(min(2, last + 1))]
    for c in range(GT):
        if i:
            steps.append(("out", c))
        if c < 2 and i < NT:
            steps.append(("at", c + 1))
        if c and c + 1 <= last:
            steps.append(("pT", c + 1))
        if c <= last:
            steps.append(("av", c))
    return steps + [("at", 3)] if i < NT else steps


FFN_STAGE = (STAGE_F0, STAGE_F1)
SIDE = side_plan()


def misc_order():
    def of_step(chain, at, step):
        if chain == "q":
            return [("qT", *at, step)]
        if chain == "shift":
            return [("shift", *at, step)]
        if chain == "finish":
            return [(("oT", "attT", "wo")[step - 1], *at)] if step else []
        if chain == "prep":
            return {2: [("xT", STAGE_A, *at)], 3: [("proj", *at, 0)], 4: [("proj", *at, 1)], 9: [("kT", *at)]}.get(step, [])
        if chain == "sim":
            return [("sim",)] if step == 1 else []
        if chain == "gate":
            stage = FFN_STAGE[at[0]]
            kind = {2: "xT", 3: "logit", 5: "rT"}.get(step)
            return [(kind, stage, at[1])] if kind else []
        if chain == "scan":
            if step == 2:
                return [("xT", STAGE_B, *at)]
            kind = {3: "tf", 5: "lam", 7: "u", 8: "c", 9: "h"}.get(step)
            return [(kind, *at)] if kind else []

    out = [use for step in range(PREP_STEPS) for use in of_step("prep", (0,), step)]
    out += of_step("q", (0,), 0) + of_step("q", (0,), 1) + of_step("shift", (0,), 0) + of_step("shift", (0,), 1)
    for place in places():
        if place[0] in ("v", "aoT"):
            out.append((place[0], FFN_STAGE[place[1]], place[2]))
        for at in SIDE.get(place, ()):
            out += of_step(*at)
    return out


def norm_order():
    stage_of = {"prep": lambda at: (STAGE_A, at[0]), "gate": lambda at: (FFN_STAGE[at[0]], at[1]),
                "scan": lambda at: (STAGE_B, at[0])}
    return [(STAGE_A, 0)] + [stage_of[chain](at) for place in places() for chain, at, step in SIDE.get(place, ())
                             if chain in stage_of and step == 0]


def update_order():
    out = []
    for place in places():
        out += [(STAGE_B, at[0]) for chain, at, step in SIDE.get(place, ()) if (chain, step) == ("scan", 9)]
        if place[0] == "ffn":
            out.append((FFN_STAGE[place[1]], place[2]))
    return out


def pair_order():
    out = []
    for s in (STAGE_F0, STAGE_F1):
        for i in range(NT + 1):
            for kind, c in row_steps(i):
                if kind == "pT":
                    out.append(("pT", s, i, c))
                elif kind == "out":
                    out.append(("out", s, i - 1, c))
    return out


def hybrid_block_kernel(nc, x, Wq, bq, Wk, bk, Wv, bv, Wo, bo, W_toP, W_U, W_F, W_V, W_lam, B_mat,
                        C_mat, W_fromP, sim, gates, q_proj, k_proj, v_proj, o_proj, cos, sin, out):
    MISC = Uses(misc_order())
    PAIR = Uses(pair_order(), 2)
    BASE = [i * (i + 1) // 2 for i in range(NT + 1)]
    NORM, UPDATE = Uses(norm_order()), Uses(update_order())
    MAX_PLAN = max_plan()
    MX_BASE = [sum(len(max_units(a)) for a in range(i)) for i in range(NT + 1)]

    def st_n(i, slot):
        return HB * BASE[i] + slot

    def xs_n(layer, g, e):
        return (layer * NG + g) * E + e

    def scaled_n(layer, i, e):
        return (NT * layer + i) * E // SHARES + e // OE // SHARES * OE + e % OE

    def pT_n(layer, i, c):
        before = [a // GT + 1 for a in range(NT)]
        return sum(before) * layer + sum(before[:i]) + c

    def weighed(layer, i):
        return pT_n(layer, i, i // GT) + 1

    def x_new_n(stage, g):
        return (GT * (g + 1) if stage == STAGE_A else
                NT + UPDATE.n(stage, GT * g + GT - 1 if stage in FFN_STAGE else g) + 1)

    with ExitStack() as ctx:
        def sb(name, shape, dt=F32):
            return ctx.enter_context(nc.sbuf_tensor(name, shape, dt))

        def sem(name):
            return ctx.enter_context(nc.semaphore(name))

        X = sb("X", [P, NT, D])
        xn = sb("xn", [P, 2 * GT, D])
        xnT = sb("xnT", [P, T])
        stats = sb("stats", [P, GT, 6])
        mean_var = sb("mean_var", [P, NT, 2])
        var_eps = sb("var_eps", [P, NT])
        rstd = sb("rstd", [P, NT])
        minus_half = sb("minus_half", [P, E])
        w_qkv = sb("w_qkv", [P, D + 2 * HD])
        b_qkv = sb("b_qkv", [P, D + 2 * HD])
        w_o = sb("w_o", [P, D])
        b_o = sb("b_o", [P, D])
        cos_t = sb("cos_t", [P, NT, HH])
        sin_t = sb("sin_t", [P, NT, HH])
        qkv = sb("qkv", [P, GT, D + 2 * HD])
        turn_c = sb("turn_c", [P, GT, H + 1, HH])
        turn_s = sb("turn_s", [P, GT, H + 1, HH])
        rest = sb("rest", [P, GT, H + 1, HD])
        q_parts = sb("q_parts", [P, 2 * GT, H, QK_PAD], BF16)
        k_parts = sb("k_parts", [P, GT, P], BF16)
        v_ones = sb("v_ones", [P, NT, 32])
        kT = sb("kT", [P, T], BF16)
        qT = sb("qT", [P, Q_RING, H * P], BF16)
        m_part = sb("m_part", [P, H, GT])
        m = sb("m", [P, H])
        m_rest = sb("m_rest", [P, 2, H])
        m_parts = sb("m_parts", [P, 2, H, 4], BF16)
        probs = sb("probs", [P, P_RING, GN])
        o_sb = sb("o_sb", [P, GN])
        den = sb("den", [P, HB, HB])
        att = sb("att", [P, 2, D])
        attT = sb("attT", [P, D])
        wo_out = sb("wo_out", [P, D])
        fw = {name: sb(f"w_expert_{name}", [P, 2, E, D], F32R) for name in "qkvo"}
        sim_sb = sb("sim_sb", [P, E])
        sim_sq = sb("sim_sq", [P, E])
        sim_n = sb("sim_n", [P, E])
        gate_sig = sb("gate_sig", [P, E])
        expert_no = sb("expert_no", [P, E])
        sq_sum = sb("sq_sum", [P, NT])
        sq_junk = sb("sq_junk", [P, GT, D])
        x_inv = sb("x_inv", [P, NT])
        logits = sb("logits", [P, GT, E])
        top = sb("top", [P, GT, 8])
        top_no = sb("top_no", [P, GT, 8], U32)
        top_nof = sb("top_nof", [P, GT, 2])
        pick = sb("pick", [P, 2, GT, E])
        on = sb("on", [P, GT, E])
        gtmp = sb("gtmp", [P, GT, E])
        gexp = sb("gexp", [P, GT, E])
        gcol = sb("gcol", [P, 3, GT])
        rw = sb("rw", [P, NT, E])
        rw_rest = sb("rw_rest", [P, GT, E])
        rw_parts = sb("rw_parts", [P, GT, PARTS, E], BF16)
        rwT = sb("rwT", [PARTS * E, T], BF16)
        spread = sb("spread", [PARTS * E, E, P], BF16)
        xs_halves = sb("xs_halves", [P, XS_HALVES_RING, 2, GN], F32R)
        fqT = sb("fqT", [P, T])
        fkT = sb("fkT", [P, T])
        after_a = q_parts[:, :, :, :].rearrange("p t h c -> p (t h c)").bitcast(F32)
        s_seq = after_a[0:PR, 0:T]
        tt = after_a[0:PR, T:T + GN]
        fv = after_a[:, T + GN:T + GN + NT * D].rearrange("p (t d) -> p t d", d=D)
        at_end = T + GN + NT * D
        fvT = after_a[:, at_end:at_end + GN]
        xs = after_a[:, at_end + GN:at_end + GN + XS_RING * GN].rearrange("p (r n) -> p r n", r=XS_RING)
        fm = sb("fm", [P, NT])
        f_shift = sb("f_shift", [P, NT])
        f_sum = sb("f_sum", [P, NT])
        f_inv = sb("f_inv", [P, NT])
        fp = probs[:, :, :].rearrange("p (a b) n -> p a (b n)", a=2)
        after_q = qT[:, :, :].rearrange("p r n -> p (r n)").bitcast(F32)
        pT = after_q[:, 0:PT_RING * GN].rearrange("p (r n) -> p r n", r=PT_RING)
        at_end = PT_RING * GN
        ao = after_q[:, at_end:at_end + 2 * D].rearrange("p (r d) -> p r d", r=2)
        out_sum = [after_q[:, at_end + 2 * D:at_end + 4 * D].rearrange("p (r d) -> p r d", r=2),
                   sb("out_sum1", [P, 2, D])]
        pair_sums = qkv[:, :, :].rearrange("p t w -> p (t w)")[:, 0:GN]
        scaled_out = [o_sb, v_ones[:, :, :].rearrange("p t d -> p (t d)")]
        tT = after_q[0:PR, at_end + 4 * D:at_end + 4 * D + GN]
        aoT = sb("aoT", [P, 2, P], F32R)
        raw = {"q": fqT, "k": fkT, "v": fqT, "o": fkT}
        w_tf = sb("w_tf", [P, P])
        w_u = sb("w_u", [P, PR, ALPHA])
        w_v = sb("w_v", [P, PR, ALPHA])
        w_uv = sb("w_uv", [P, PR])
        w_lam = sb("w_lam", [P, PR])
        w_b = sb("w_b", [PR, PR])
        w_c = sb("w_c", [PR, PR])
        w_p = sb("w_p", [PR, D])
        sigmoids = kT[:, :].bitcast(F32).rearrange("p (a n) -> p a n", a=2)
        fg, lam = sigmoids, sigmoids[0:PR, :, :]
        ident = sb("ident", [P, P])
        ident_b = sb("ident_b", [P, P], BF16)
        mask_b = sb("mask_b", [P, P], BF16)
        ones = sb("ones", [P, P])
        psum = ctx.enter_context(nc.psum_tensor("psum", [P, 8 * GN], F32))

        def bank(n):
            return psum[:, GN * n:GN * n + GN]

        def mx_bank(n):
            return bank(n % MX_RING)

        def st_bank(n):
            return bank(MX_RING + n % ST_RING)

        def pair_bank(key):
            return bank(4 + PAIR.slot(*key))

        misc = bank(7)
        misc_b = misc.bitcast(BF16)

        x_loaded = [sem(f"x_loaded{g}") for g in range(NG)]
        rot_loaded, tab_loaded, a_loaded, wo_loaded, b_loaded = (
            sem(n) for n in ("rot_loaded", "tab_loaded", "a_loaded", "wo_loaded", "b_loaded"))
        f_loaded = {w: sem(f"f_loaded_{w}") for w in "qkvo"}
        w_split = sem("w_split")
        consts = sem("consts")
        pool_step, dve_step, act_step = (
            sem(n) for n in ("pool_step", "dve_step", "act_step"))
        x_new = sem("x_new")
        var_ready, rstd_ready, xn_ready, xnT_ready = (
            sem(n) for n in ("var_ready", "rstd_ready", "xn_ready", "xnT_ready"))
        sq_ready, x_inv_ready = sem("sq_ready"), sem("x_inv_ready")
        misc_ready = sem("misc_ready")
        sim_sq_ready, sim_var, sim_pow, sim_ready = (
            sem(n) for n in ("sim_sq_ready", "sim_var", "sim_pow", "sim_ready"))
        gates_exp = sem("gates_exp")
        proj_copied, kparts_ready, kT_ready, qparts_ready, qT_ready = (
            sem(n) for n in ("proj_copied", "kparts_ready", "kT_ready", "qparts_ready", "qT_ready"))
        mx_ready, mx_free, m_ready = sem("mx_ready"), sem("mx_free"), sem("m_ready")
        shift_set = [sem(f"shift_set{half}") for half in range(2)]
        st_ready, probs_ready, pv_done, o_copied = (
            sem(n) for n in ("st_ready", "probs_ready", "pv_done", "o_copied"))
        att_ready, attT_ready, wo_copied = sem("att_ready"), sem("attT_ready"), sem("wo_copied")
        logit_copied, gate_arg, gate_exp, rparts_ready, rwT_ready = (
            sem(n) for n in ("logit_copied", "gate_arg", "gate_exp", "rparts_ready", "rwT_ready"))
        rb_ready, xs_ready, xs_used = sem("rb_ready"), sem("xs_ready"), sem("xs_used")
        xs_hi_ready, xs_lo_ready = sem("xs_hi_ready"), sem("xs_lo_ready")
        fqkv_copied, fv_ready = sem("fqkv_copied"), sem("fv_ready")
        fs_ready, fshift_ready, fprobs_ready = (
            sem(n) for n in ("fs_ready", "fshift_ready", "fprobs_ready"))
        pT_filled = sem("pT_filled")
        pT_copied = [sem(f"pT_copied{n}") for n in range(2)]
        pT_used = sem("pT_used")
        ao_ready, aoT_hi_ready, aoT_ready = sem("ao_ready"), sem("aoT_hi_ready"), sem("aoT_ready")
        out_filled, out_scaled = sem("out_filled"), sem("out_scaled")
        out_scaled_act, scaled_read, tile_summed = sem("out_scaled_act"), sem("scaled_read"), sem("tile_summed")
        wtf_ready, fg_exp, fg_ready, t_ready = (
            sem(n) for n in ("wtf_ready", "fg_exp", "fg_ready", "t_ready"))
        lam_read = sem("lam_read")
        lam_exp, s_ready, tt_ready = sem("lam_exp"), sem("s_ready"), sem("tt_ready")
        stored = sem("stored")

        def misc_copied(kind, *at):
            if kind == "sim":
                return sim_var, 1
            if kind == "xT":
                return xnT_ready, NORM.n(*at) + 1
            if kind == "proj":
                return proj_copied, 2 * at[0] + at[1] + 1
            if kind == "kT":
                return kT_ready, at[0] + 1
            if kind == "qT":
                return qT_ready, 2 * at[0] + at[1] + 1
            if kind == "shift":
                return shift_set[at[1]], at[0] + 1
            if kind == "oT":
                return att_ready, at[0] + 1
            if kind == "attT":
                return attT_ready, at[0] + 1
            if kind == "wo":
                return wo_copied, at[0] + 1
            if kind in ("tf", "lam", "u", "c"):
                return {"tf": t_ready, "lam": lam_read, "u": s_ready, "c": tt_ready}[kind], at[0] + 1
            if kind == "h":
                return x_new, x_new_n(STAGE_B, at[0])
            layer = int(at[0] == STAGE_F1)
            if kind == "aoT":
                return aoT_ready, NT * layer + at[1] + 1
            by_group = {"logit": logit_copied, "rT": rwT_ready, "v": fv_ready}
            return by_group[kind], NG * layer + at[1] + 1

        def pT_copies(key):
            own = PAIR.keys[PAIR.slot(*key)::2][:PAIR.n(*key) // 2 + 1]
            return sum(k[0] == "pT" for k in own)

        block = ctx.enter_context(nc.Block())

        @block.sync
        def _(sp):
            sp.dma_start(X[:, 0:GT, :], x.rearrange("b (n p) d -> p (b n) d", p=P)[:, 0:GT, :]).then_inc(x_loaded[0], 16)
            sp.dma_start(cos_t[:, :, :], cos).then_inc(rot_loaded, 16)
            sp.dma_start(sin_t[:, :, :], sin).then_inc(rot_loaded, 16)
            xv = x.rearrange("b (n p) d -> p (b n) d", p=P)
            ov = out.rearrange("b (n p) d -> p (b n) d", p=P)
            for g in range(1, NG):
                sp.dma_start(X[:, GT * g:GT * g + GT, :], xv[:, GT * g:GT * g + GT, :]).then_inc(x_loaded[g], 16)
            for w, src in (("q", q_proj), ("k", k_proj), ("v", v_proj), ("o", o_proj)):
                if w in "vo":
                    sp.wait_ge(w_split, GT * "vo".index(w) + GT)
                sp.dma_start(raw[w][:, :].rearrange("p (e d) -> p e d", e=E), src.rearrange("e c h -> c e h"))\
                    .then_inc(f_loaded[w], 16)
            for g in range(NG):
                sp.wait_ge(x_new, x_new_n(STAGE_F1, g))
                sp.dma_start(ov[:, GT * g:GT * g + GT, :], X[:, GT * g:GT * g + GT, :]).then_inc(stored, 16)
            sp.wait_ge(stored, 16 * NG)

        @block.gpsimd
        def _(pool):
            steps = [0]

            def after(ins):
                steps[0] += 1
                ins.then_inc(pool_step, 1)
                pool.wait_ge(pool_step, steps[0])

            after(pool.memset(ident[:, :], 0.0))
            after(pool.affine_select(out=ident[:, :], in_=ident[:, :], compare_op=ALU.not_equal, fill=1.0,
                                     base=0, pattern=[[-1, P]], channel_multiplier=1))
            pool.tensor_copy(ident_b[:, :], ident[:, :]).then_inc(consts, 1)
            after(pool.memset(minus_half[:, :], -0.5))

            def inverse_std(stage, g):
                a, b = GT * g, GT * g + GT
                pool.wait_ge(var_ready, NORM.n(stage, g) + 1)
                pool.tensor_tensor(rstd[:, a:b], var_eps[:, a:b], minus_half[:, 0:GT], ALU.pow).then_inc(rstd_ready, 1)

            def inverse_norm(layer, g):
                a, b = GT * g, GT * g + GT
                pool.wait_ge(sq_ready, NG * layer + g + 1)
                pool.tensor_tensor(x_inv[:, a:b], sq_sum[:, a:b], minus_half[:, 0:GT], ALU.pow).then_inc(x_inv_ready, 1)

            inverse_std(STAGE_A, 0)
            after(pool.memset(mask_b[:, :], 0.0))
            pool.affine_select(out=mask_b[:, :], in_=mask_b[:, :], compare_op=ALU.is_ge, fill=MASKED,
                               base=0, pattern=[[-1, P]], channel_multiplier=1).then_inc(consts, 1)
            pool.memset(ones[:, :], 1.0).then_inc(consts, 1)
            pool.dma_start(w_tf[:, 0:PR], W_toP).then_inc(b_loaded, 16)
            pool.dma_start(w_tf[:, PR:P], W_F).then_inc(b_loaded, 16)
            pool.dma_start(w_u[:, :, :], W_U).then_inc(b_loaded, 16)
            pool.dma_start(w_v[:, :, :], W_V.rearrange("(o p) a -> o p a", o=1).broadcast_to([P, PR, ALPHA])).then_inc(b_loaded, 16)
            pool.dma_start(w_lam[PR:P, :], W_lam).then_inc(b_loaded, 16)
            pool.dma_start(w_b[:, :], B_mat).then_inc(b_loaded, 16)
            pool.dma_start(w_c[:, :], C_mat).then_inc(b_loaded, 16)
            pool.dma_start(w_p[:, :], W_fromP).then_inc(b_loaded, 16)
            inverse_std(STAGE_A, 1)
            pool.wait_ge(sim_var, 1)
            pool.tensor_tensor(sim_sq[:, :], sim_sq[:, :], minus_half[:, :], ALU.pow).then_inc(sim_pow, 1)
            pool.iota(expert_no[:, :], pattern=[[1, E]], base=0, channel_multiplier=0,
                      allow_small_or_imprecise_dtypes=True).then_inc(consts, 1)
            after(pool.memset(spread[:, :, :], 0.0))
            for part in range(PARTS):
                after(pool.affine_select(out=spread[:, :, :], in_=spread[:, :, :], compare_op=ALU.not_equal,
                                         fill=1.0, base=-E * part, pattern=[[-1, E], [0, P]],
                                         channel_multiplier=1))

            def split_weights(w):
                pool.wait_ge(f_loaded[w], 16)
                for piece in range(GT):
                    hi, lo = (fw[w][:, half, OE * piece:OE * piece + OE, :].rearrange("p e d -> p (e d)")
                              for half in (HI, LO))
                    src = raw[w][:, GN * piece:GN * piece + GN]
                    after(pool.tensor_copy(hi, src))
                    pool.tensor_tensor(lo, src, hi.bitcast(F32), ALU.subtract).then_inc(w_split, 1)

            split_weights("q")
            def sum_tile(layer, i):
                n = NT * layer + i
                if n:
                    pool.wait_ge(tile_summed, n)
                pool.wait_ge(out_scaled_act, E // SHARES * (n + 1))
                o, half, sums = pair_sums, GN // 2, out_sum[i % 2]
                pool.tensor_tensor(o[:, :], scaled_out[0][:, :], scaled_out[1], ALU.add).then_inc(scaled_read, 1)
                pool.wait_ge(scaled_read, n + 1)
                after(pool.tensor_tensor(o[:, 0:half], o[:, 0:half], o[:, half:GN], ALU.add))
                after(pool.tensor_tensor(o[:, 0:D], o[:, 0:D], o[:, D:2 * D], ALU.add))
                pool.wait_ge(out_scaled, E // SHARES * (n + 1))
                after(pool.tensor_tensor(sums[:, 0, :], sums[:, 0, :], sums[:, 1, :], ALU.add))
                pool.tensor_tensor(sums[:, 0, :], sums[:, 0, :], o[:, 0:D], ALU.add).then_inc(tile_summed, 1)

            weights = list("kvo")
            for place in places():
                for chain, at, step in SIDE.get(place, ()):
                    if step == 0 and chain in ("prep", "gate", "scan") and (chain, at) != ("prep", (1,)):
                        inverse_std(FFN_STAGE[at[0]] if chain == "gate" else STAGE_B if chain == "scan" else STAGE_A, at[-1])
                        if chain == "prep":
                            split_weights(weights.pop(0))
                    elif chain == "gate" and step == 1:
                        inverse_norm(*at)
                        if weights:
                            split_weights(weights.pop(0))
                if place[0] == "T" and place[3] == 2 and place[2]:
                    sum_tile(place[1], place[2] - 1)
                elif place == ("ffn", place[1], NT - 1):
                    sum_tile(place[1], NT - 1)

        @block.scalar
        def _(act):
            act.dma_start(w_qkv[:, 0:D], Wq).then_inc(a_loaded, 16)
            act.dma_start(w_qkv[:, D:D + HD], Wk).then_inc(a_loaded, 16)
            act.dma_start(w_qkv[:, D + HD:D + 2 * HD], Wv).then_inc(a_loaded, 16)
            for lo, n, b in ((0, D, bq), (D, HD, bk), (D + HD, HD, bv)):
                act.dma_start(b_qkv[:, lo:lo + n], b.rearrange("(o n) -> o n", o=1).broadcast_to([P, n])).then_inc(rot_loaded, 16)
            act.dma_start(b_o[:, :], bo.rearrange("(o n) -> o n", o=1).broadcast_to([P, D])).then_inc(tab_loaded, 16)
            act.dma_start(sim_sb[:, :], sim).then_inc(tab_loaded, 16)
            act.dma_start(gate_sig[:, :], gates.rearrange("(o n) -> o n", o=1).broadcast_to([P, E])).then_inc(tab_loaded, 16)
            act.dma_start(w_o[:, :], Wo).then_inc(wo_loaded, 16)

            def take(*key):
                act.wait_ge(misc_ready, MISC.n(*key) + 1)

            def xT_copy(stage, g):
                take("xT", stage, g)
                act.activation(xnT[:, GN * g:GN * g + GN], misc, ACT.Copy).then_inc(xnT_ready, 1)

            def prep(g, step):
                if step == 2:
                    xT_copy(STAGE_A, g)
                elif step == 9:
                    kT_copy(g)

            def kT_copy(g):
                take("kT", g)
                act.activation(kT[0:ST_ROWS, GN * g:GN * g + GN], misc_b[0:ST_ROWS, 0:GN], ACT.Copy).then_inc(kT_ready, 1)

            def q_copy(i, half):
                if i >= Q_RING:
                    act.wait_ge(st_ready, st_n(i - Q_RING + 1, 0))
                take("qT", i, half)
                act.activation(qT[0:QK_PAD, i % Q_RING, 1024 * half:1024 * half + 1024], misc_b[0:QK_PAD, :],
                               ACT.Copy).then_inc(qT_ready, 1)

            def shift_copy(i):
                take("shift", i, 0)
                act.activation(qT[SHIFT_ROW:ST_ROWS, i % Q_RING, 0:1024], misc_b[SHIFT_ROW:ST_ROWS, :],
                               ACT.Copy).then_inc(shift_set[0], 1)

            def exp_a(i, slot):
                n = st_n(i, slot)
                act.wait_ge(st_ready, n + 1)
                if n >= P_RING:
                    act.wait_ge(pv_done, (n - P_RING) // HB + 1)
                act.activation(probs[:, n % P_RING, :], st_bank(n), ACT.Exp, scale=SCALE_A).then_inc(probs_ready, 1)

            def sums_copy(i):
                act.wait_ge(pv_done, BASE[i + 1])
                act.activation(o_sb[:, :], bank(6), ACT.Copy).then_inc(o_copied, 1)

            def attT_copy(i):
                take("attT", i)
                act.activation(attT[:, :], misc[:, 0:D], ACT.Copy).then_inc(attT_ready, 1)

            def finish(i, step):
                if step == 0:
                    sums_copy(i)
                elif step == 2:
                    attT_copy(i)

            def gate(layer, g, step):
                n = NG * layer + g
                if step == 2:
                    xT_copy(FFN_STAGE[layer], g)
                elif step == 3:
                    act.wait_ge(gate_arg, n + 1)
                    act.activation(gexp[:, :, :], gtmp[:, :, :], ACT.Exp).then_inc(gate_exp, 1)
                elif step == 5:
                    take("rT", FFN_STAGE[layer], g)
                    act.activation(rwT[:, GN * g:GN * g + GN], misc_b[0:PARTS * E, 0:GN], ACT.Copy).then_inc(rwT_ready, 1)

            def scan(g, step):
                if step == 2:
                    xT_copy(STAGE_B, g)
                elif step == 3:
                    take("tf", g)
                    act.activation(fg[PR:P, 0, :], misc[PR:P, :], ACT.Abs).then_inc(act_step, 1)
                    act.activation(fg[PR:P, 1, :], misc[PR:P, :], ACT.Relu, scale=-1.0).then_inc(act_step, 1)
                    act.activation(tT[:, :], misc[0:PR, :], ACT.Copy).then_inc(t_ready, 1)
                    act.wait_ge(act_step, 3 * g + 2)
                    act.activation(fg[PR:P, 0, :], fg[PR:P, 0, :], ACT.Tanh, scale=0.5)
                    act.activation(fg[PR:P, 1, :], fg[PR:P, 1, :], ACT.Exp, scale=-1.0).then_inc(fg_exp, 1)
                elif step == 5:
                    take("lam", g)
                    act.activation(lam[:, 0, :], misc[0:PR, :], ACT.Abs).then_inc(act_step, 1)
                    act.activation(lam[:, 1, :], misc[0:PR, :], ACT.Relu, scale=-1.0).then_inc(lam_read, 1)
                    act.wait_ge(act_step, 3 * g + 3)
                    act.activation(lam[:, 0, :], lam[:, 0, :], ACT.Tanh, scale=0.25)
                    act.wait_ge(lam_read, g + 1)
                    act.activation(lam[:, 1, :], lam[:, 1, :], ACT.Exp, scale=-0.5).then_inc(lam_exp, 1)

            def beside(*place):
                for chain, at, step in SIDE.get(place, ()):
                    if chain == "q":
                        q_copy(*at, step)
                    elif chain == "shift" and step == 0:
                        shift_copy(*at)
                    elif chain == "finish":
                        finish(*at, step)
                    elif chain == "prep":
                        prep(*at, step)
                    elif chain == "sim" and step == 1:
                        act.wait_ge(tab_loaded, 16 * 3)
                        act.activation(gate_sig[:, :], gate_sig[:, :], ACT.Exp, scale=-1.0).then_inc(gates_exp, 1)
                    elif chain == "gate":
                        gate(*at, step)
                    elif chain == "scan":
                        scan(*at, step)

            for step in range(PREP_STEPS):
                prep(0, step)
            q_copy(0, 0)
            q_copy(0, 1)
            shift_copy(0)
            for i in range(NT):
                for slot in range(HB * (i + 1)):
                    exp_a(i, slot)
                    beside("A", st_n(i, slot))

            def copy_qkv(layer, g):
                act.wait_ge(xs_used, xs_n(layer, g, E - 1) + 1)
                act.activation(fqT[:, GN * g:GN * g + GN], bank(3), ACT.Copy).then_inc(fqkv_copied, 1)
                act.activation(fkT[:, GN * g:GN * g + GN], bank(4), ACT.Copy).then_inc(fqkv_copied, 1)
                act.activation(fvT[:, :], bank(5), ACT.Copy).then_inc(fqkv_copied, 1)

            def copy_v(stage, g):
                take("v", stage, g)
                act.activation(fv[:, GT * g:GT * g + GT, :].rearrange("p a b -> p (a b)"), misc,
                               ACT.Copy).then_inc(fv_ready, 1)

            def project(stage, layer):
                for g in range(NG):
                    for e in range(E):
                        if g and e == LAG:
                            copy_qkv(layer, g - 1)
                        beside("P", layer, g, e)
                        k = xs_n(layer, g, e)
                        act.wait_ge(xs_ready, k + 1)
                        if k >= XS_HALVES_RING:
                            act.wait_ge(xs_used, k - XS_HALVES_RING + 1)
                        act.activation(xs_halves[:, k % XS_HALVES_RING, HI, :], xs[:, k % XS_RING, :],
                                       ACT.Copy).then_inc(xs_hi_ready, 1)
                        if g and e == V_TURN:
                            copy_v(stage, g - 1)
                copy_qkv(layer, NG - 1)
                copy_v(stage, NG - 1)

            def exp_f(layer, i):
                n = NT * layer + i
                act.wait_ge(fshift_ready, n + 1)
                if n >= 2:
                    act.wait_ge(pT_used, weighed((n - 2) // NT, (n - 2) % NT))
                act.activation(fp[:, i % 2, 0:P * (i + 1)], psum[:, 0:P * (i + 1)], ACT.Exp,
                               bias=f_shift[:, i:i + 1], scale=SCALE_F, accum_out=f_sum[:, i:i + 1])\
                    .then_inc(fprobs_ready, 1)

            def scale_outputs(stage, layer, i, c):
                n = NT * layer + i
                act.wait_ge(out_filled, n * GT + c + 1)
                if n and c == 1:
                    act.wait_ge(scaled_read, n)
                ps = pair_bank(("out", stage, i, c))
                for e in range(OE):
                    act.activation(scaled_out[c // SHARES][:, D * e:D * e + D], ps[:, D * e:D * e + D], ACT.Copy,
                                   scale=rw[:, i, OE * c + e:OE * c + e + 1]).then_inc(out_scaled_act, 1)

            def aoT_copy(stage, i):
                take("aoT", stage, i)
                n = NT * (stage == STAGE_F1) + i
                if n:
                    act.wait_ge(out_filled, GT * n)
                act.activation(aoT[:, HI, :], misc[:, 0:P], ACT.Copy).then_inc(aoT_hi_ready, 1)

            def pT_copy(stage, layer, i, c):
                n, key = pT_n(layer, i, c), ("pT", stage, i, c)
                w = P * min(GT, i + 1 - GT * c)
                act.wait_ge(pT_filled, n + 1)
                if n >= PT_RING:
                    act.wait_ge(pT_used, n - PT_RING + 1)
                act.activation(pT[:, n % PT_RING, 0:w], pair_bank(key)[:, 0:w], ACT.Copy)\
                    .then_inc(pT_copied[PAIR.slot(*key)], 1)

            def expert_attention(stage, layer):
                project(stage, layer)
                exp_f(layer, 0)
                for g in range(NG):
                    for i in range(GT * g, GT * g + GT):
                        beside("T", layer, i, 0)
                        if i:
                            aoT_copy(stage, i - 1)
                        for c in range(min(2, i // GT + 1)):
                            pT_copy(stage, layer, i, c)
                        beside("T", layer, i, 1)
                        if i + 1 < NT:
                            exp_f(layer, i + 1)
                        if i:
                            scale_outputs(stage, layer, i - 1, 1)
                        beside("T", layer, i, 2)
                        for c in range(2, i // GT + 1):
                            pT_copy(stage, layer, i, c)
                        if i:
                            scale_outputs(stage, layer, i - 1, 3)
                        beside("T", layer, i, 3)
                aoT_copy(stage, NT - 1)
                for c in range(1, GT, SHARES):
                    scale_outputs(stage, layer, NT - 1, c)

            expert_attention(STAGE_F0, 0)
            expert_attention(STAGE_F1, 1)

        @block.tensor
        def _(pe):
            def fill(*key):
                last = MISC.before(*key)
                if last:
                    pe.wait_ge(*misc_copied(*last))

            def transposes(key, into, pieces, identity):
                fill(*key)
                for o, src in zip(into, pieces):
                    last = pe.transpose(o, src, identity)
                last.then_inc(misc_ready, 1)

            def xT(stage, g):
                pe.wait_ge(xn_ready, NORM.n(stage, g) + 1)
                transposes(("xT", stage, g), [misc[:, P * a:P * a + P] for a in range(GT)],
                           [xn[:, GT * (NORM.n(stage, g) % 2) + a, :] for a in range(GT)], ident[:, :])

            def prep(g, step):
                if step == 2:
                    xT(STAGE_A, g)
                elif step in (3, 4):
                    qkv_of(g, step - 3)
                elif step == 9:
                    k_transposes(g)

            def qkv_of(g, half):
                pe.wait_ge(xnT_ready, NORM.n(STAGE_A, g) + 1)
                w = D + 2 * HD
                fill("proj", g, half)
                for a in range(2):
                    t = GT * g + 2 * half + a
                    last = pe.matmul(misc[:, w * a:w * a + w], xnT[:, P * t:P * t + P], w_qkv[:, :],
                                     start=True, stop=True)
                last.then_inc(misc_ready, 1)

            def k_transposes(g):
                pe.wait_ge(kparts_ready, g + 1)
                transposes(("kT", g), [misc_b[0:ST_ROWS, P * a:P * a + P] for a in range(GT)],
                           [k_parts[:, a, 0:ST_ROWS] for a in range(GT)], ident_b[:, :])

            def q_transposes(i, half):
                pe.wait_ge(qparts_ready, i // GT + 1)
                transposes(("qT", i, half), [misc_b[0:QK_PAD, P * a:P * a + P] for a in range(8)],
                           [q_parts[:, i % (2 * GT), 8 * half + a, :] for a in range(8)], ident_b[:, :])

            def max_scores(i, u):
                h0, nh, k0, nk = max_units(i)[u]
                n = MX_BASE[i] + u
                w = nk * P
                if u == 0:
                    pe.wait_ge(qT_ready, 2 * (i + 1))
                    pe.wait_ge(kT_ready, i // GT + 1)
                if n >= MX_RING:
                    pe.wait_ge(mx_free, n - MX_RING + 1)
                diagonal = k0 + nk == i + 1
                for a in range(nh):
                    h = h0 + a
                    last = pe.matmul(mx_bank(n)[:, w * a:w * a + w], qT[0:QK_PAD, i % Q_RING, P * h:P * h + P],
                                     kT[0:QK_PAD, P * k0:P * k0 + w], start=True, stop=True)
                    if diagonal:
                        last = pe.matmul(mx_bank(n)[:, w * a + w - P:w * a + w], ident_b[:, :], mask_b[:, :],
                                         start=False, stop=True, skip_group_check=True)
                last.then_inc(mx_ready, 1)

            def shift_rows(i, half):
                pe.wait_ge(m_ready, i + 1)
                fill("shift", i, half)
                for a in range(8):
                    last = pe.transpose(misc_b[SHIFT_ROW:ST_ROWS, P * a:P * a + P],
                                        m_parts[:, i % 2, 8 * half + a, 0:PARTS], ident_b[:, :],
                                        tile_position=(0, SHIFT_ROW))
                last.then_inc(misc_ready, 1)

            def scores(i, slot):
                j, c = slot // HB, slot % HB
                n = st_n(i, slot)
                w = HB * P
                if slot == 0:
                    for half in range(2):
                        pe.wait_ge(shift_set[half], i + 1)
                if n >= ST_RING:
                    pe.wait_ge(probs_ready, n - ST_RING + 1)
                last = pe.matmul(st_bank(n), kT[0:ST_ROWS, P * j:P * j + P],
                                 qT[0:ST_ROWS, i % Q_RING, w * c:w * c + w], start=True, stop=j < i)
                if j == i:
                    last = pe.matmul(st_bank(n).rearrange("p (a b) -> p a b", a=HB), mask_b[:, :],
                                     ident_b[:, :].rearrange("p (o b) -> p o b", o=1).broadcast_to([P, HB, P]),
                                     start=False, stop=True)
                last.then_inc(st_ready, 1)

            def weigh_values(i, j):
                n = st_n(i, HB * j)
                pe.wait_ge(probs_ready, n + HB)
                if j == 0 and i > 0:
                    pe.wait_ge(o_copied, i)
                for c in range(HB):
                    last = pe.matmul(bank(6)[32 * c:32 * c + 32, :], v_ones[:, j, :], probs[:, (n + c) % P_RING, :],
                                     start=j == 0, stop=j == i, tile_position=(0, 32 * c), skip_group_check=True)
                last.then_inc(pv_done, 1)

            def finish_a(i, step):
                if step == 0:
                    pe.wait_ge(o_copied, i + 1)
                    transposes(("oT", i), [misc[:, P * a:P * a + P] for a in range(HB)],
                               [o_sb[:, P * a:P * a + P] for a in range(HB)], ident[:, :])
                elif step == 1:
                    pe.wait_ge(att_ready, i + 1)
                    transposes(("attT", i), [misc[:, 0:P]], [att[:, i % 2, :]], ident[:, :])
                else:
                    pe.wait_ge(attT_ready, i + 1)
                    if i == 0:
                        pe.wait_ge(wo_loaded, 16)
                    fill("wo", i)
                    pe.matmul(misc[:, 0:D], attT[:, :], w_o[:, :], start=True, stop=True).then_inc(misc_ready, 1)

            def gate(layer, g, step):
                stage, n = FFN_STAGE[layer], NG * layer + g
                if step == 2:
                    xT(stage, g)
                elif step == 3:
                    pe.wait_ge(xnT_ready, NORM.n(stage, g) + 1)
                    if n == 0:
                        pe.wait_ge(sim_ready, 1)
                    fill("logit", stage, g)
                    for a in range(GT):
                        t = GT * g + a
                        last = pe.matmul(misc[:, E * a:E * a + E], xnT[:, P * t:P * t + P], sim_n[:, :],
                                         start=True, stop=True)
                    last.then_inc(misc_ready, 1)
                elif step == 5:
                    pe.wait_ge(rparts_ready, n + 1)
                    transposes(("rT", stage, g), [misc_b[0:PARTS * E, P * a:P * a + P] for a in range(GT)],
                               [rw_parts[:, a, :, :].rearrange("p a b -> p (a b)") for a in range(GT)], ident_b[:, :])

            def scan(g, step):
                if step == 2:
                    xT(STAGE_B, g)
                elif step == 3:
                    pe.wait_ge(xnT_ready, NORM.n(STAGE_B, g) + 1)
                    if g == 0:
                        pe.wait_ge(wtf_ready, 1)
                    fill("tf", g)
                    pe.matmul(misc, w_tf[:, :], xnT[:, GN * g:GN * g + GN], start=True, stop=True).then_inc(misc_ready, 1)
                elif step == 5:
                    pe.wait_ge(fg_ready, g + 1)
                    fill("lam", g)
                    pe.matmul(misc[0:PR, :], w_lam[PR:P, :], fg[PR:P, 0, :], start=True, stop=True,
                              tile_position=(PR, 0)).then_inc(misc_ready, 1)
                elif step == 7:
                    fill("u", g)
                    pe.matmul(misc[0:PR, :], w_b[:, :], tT[:, :], start=True, stop=True).then_inc(misc_ready, 1)
                elif step == 8:
                    fill("c", g)
                    pe.matmul(misc[0:PR, :], w_c[:, :], s_seq[:, GN * g:GN * g + GN], start=True,
                              stop=True).then_inc(misc_ready, 1)
                elif step == 9:
                    fill("h", g)
                    for a in range(GT):
                        last = pe.matmul(misc[:, P * a:P * a + P], tt[:, P * a:P * a + P], w_p[:, :],
                                         start=True, stop=True)
                    last.then_inc(misc_ready, 1)

            def beside(*place):
                for chain, at, step in SIDE.get(place, ()):
                    if chain == "q":
                        q_transposes(*at, step)
                    elif chain == "shift":
                        shift_rows(*at, step)
                    elif chain == "finish" and step > 0:
                        finish_a(*at, step - 1)
                    elif chain == "prep":
                        prep(*at, step)
                    elif chain == "sim" and step == 1:
                        pe.wait_ge(consts, 3)
                        pe.wait_ge(sim_sq_ready, 1)
                        fill("sim")
                        pe.matmul(misc[:, 0:E], ones[:, :], sim_sq[:, :], start=True, stop=True).then_inc(misc_ready, 1)
                    elif chain == "gate":
                        gate(*at, step)
                    elif chain == "scan":
                        scan(*at, step)

            pe.wait_ge(consts, 1)
            pe.wait_ge(a_loaded, 16 * 3)
            for step in range(PREP_STEPS):
                prep(0, step)
            q_transposes(0, 0)
            q_transposes(0, 1)
            pe.wait_ge(consts, 2)
            for u in range(len(max_units(0))):
                max_scores(0, u)
            shift_rows(0, 0)
            shift_rows(0, 1)
            for i in range(NT):
                for slot in range(HB * (i + 1)):
                    scores(i, slot)
                    if slot == HB - 1 and i > 0:
                        weigh_values(i - 1, i - 1)
                    beside("A", st_n(i, slot))
                    for unit in MAX_PLAN[st_n(i, slot)]:
                        max_scores(*unit)
                    if slot % HB == HB - 1 and slot >= HB:
                        weigh_values(i, slot // HB - 1)
            weigh_values(NT - 1, NT - 1)

            def spread_weight(ps, g, e):
                pe.matmul(ps, spread[:, e, :], rwT[:, GN * g:GN * g + GN], start=True, stop=True).then_inc(rb_ready, 1)

            def project_expert(layer, g, e):
                n, k = NG * layer + g, xs_n(layer, g, e)
                pe.wait_ge(xs_hi_ready, k + 1)
                pe.wait_ge(xs_lo_ready, k + 1)
                for at, (w, b) in enumerate(zip("qkv", (3, 4, 5))):
                    if e == 0 and n > 0:
                        pe.wait_ge(fqkv_copied, 3 * (n - 1) + at + 1)
                    for a, c in ((HI, HI), (HI, LO), (LO, HI)):
                        last = pe.matmul(bank(b), fw[w][:, a, e, :], xs_halves[:, k % XS_HALVES_RING, c, :],
                                         start=e == 0 and a == c, stop=e == E - 1 and a == LO)
                last.then_inc(xs_used, 1)

            def turn_v(stage, layer, g):
                pe.wait_ge(fqkv_copied, 3 * (NG * layer + g) + 3)
                transposes(("v", stage, g), [misc[:, P * a:P * a + P] for a in range(GT)],
                           [fvT[:, P * a:P * a + P] for a in range(GT)], ident[:, :])

            def project(stage, layer):
                if layer == 0:
                    pe.wait_ge(w_split, 4 * GT)
                for g in range(NG):
                    pe.wait_ge(rwT_ready, NG * layer + g + 1)
                    for e in range(E):
                        beside("P", layer, g, e)
                        k = xs_n(layer, g, e)
                        if k >= 3:
                            pe.wait_ge(xs_ready, k - 2)
                        spread_weight(bank(k % 3), g, e)
                        if g or e >= LAG:
                            project_expert(layer, *divmod(E * g + e - LAG, E))
                        if g and e == V_TURN:
                            turn_v(stage, layer, g - 1)
                for e in range(E - LAG, E):
                    project_expert(layer, NG - 1, e)
                turn_v(stage, layer, NG - 1)

            def scores_f(stage, layer, i):
                n, L = NT * layer + i, P * (i + 1)
                if i % GT == 0:
                    pe.wait_ge(fqkv_copied, 3 * (NG * layer + i // GT + 1))
                if i:
                    pe.wait_ge(fprobs_ready, n)
                for k0 in range(0, L, GN):
                    w = min(GN, L - k0)
                    pe.matmul(psum[:, k0:k0 + w], fqT[:, P * i:P * i + P], fkT[:, k0:k0 + w],
                              start=True, stop=True)
                    if k0 == GN * ((L - 1) // GN) and i > 1:
                        turn_output(stage, layer, i - 2)
                pe.matmul(psum[:, L - P:L], ident_b[:, :], mask_b[:, :], start=False, stop=True,
                          skip_group_check=True).then_inc(fs_ready, 1)

            def pair_fill(*key):
                last = PAIR.before(*key)
                if last and last[0] == "pT":
                    pe.wait_ge(pT_copied[PAIR.slot(*key)], pT_copies(last))
                elif last:
                    pe.wait_ge(out_scaled_act if last[3] % SHARES else out_scaled,
                               scaled_n(int(last[1] == STAGE_F1), last[2], OE * last[3] + OE - 1) + 1)

            def transpose_probs(stage, layer, i, c):
                key = ("pT", stage, i, c)
                if c == 0:
                    pe.wait_ge(fprobs_ready, NT * layer + i + 1)
                pair_fill(*key)
                for a in range(min(GT, i + 1 - GT * c)):
                    k0 = P * (GT * c + a)
                    last = pe.transpose(pair_bank(key)[:, P * a:P * a + P], fp[:, i % 2, k0:k0 + P], ident[:, :])
                last.then_inc(pT_filled, 1)

            def weigh_f(stage, layer, i, c):
                n, key = pT_n(layer, i, c), ("pT", stage, i, c)
                pe.wait_ge(pT_copied[PAIR.slot(*key)], pT_copies(key))
                if c == 0:
                    pe.wait_ge(fv_ready, NG * layer + i // GT + 1)
                    if i:
                        pe.wait_ge(ao_ready, NT * layer + i)
                for a in range(min(GT, i + 1 - GT * c)):
                    j = GT * c + a
                    last = pe.matmul(bank(6)[:, 0:D], pT[:, n % PT_RING, P * a:P * a + P], fv[:, j, :],
                                     start=j == 0, stop=j == i)
                last.then_inc(pT_used, 1)

            def expert_outputs(stage, layer, i, c):
                if c == 0:
                    pe.wait_ge(aoT_ready, NT * layer + i + 1)
                pair_fill("out", stage, i, c)
                for a, b in ((HI, HI), (HI, LO), (LO, HI)):
                    last = pe.matmul(pair_bank(("out", stage, i, c)), aoT[:, a, :],
                                     fw["o"][:, b, OE * c:OE * c + OE, :].rearrange("p e d -> p (e d)"),
                                     start=a == b, stop=a == LO)
                last.then_inc(out_filled, 1)

            def turn_output(stage, layer, i):
                pe.wait_ge(ao_ready, NT * layer + i + 1)
                transposes(("aoT", stage, i), [misc[:, 0:P]], [ao[:, i % 2, :]], ident[:, :])

            def row(stage, layer, i):
                if i == NT:
                    turn_output(stage, layer, i - 1)
                for kind, c in row_steps(i):
                    if kind == "pT":
                        transpose_probs(stage, layer, i, c)
                    elif kind == "av":
                        weigh_f(stage, layer, i, c)
                    elif kind == "out":
                        expert_outputs(stage, layer, i - 1, c)
                    else:
                        beside("T", layer, i, c)

            def expert_attention(stage, layer):
                project(stage, layer)
                scores_f(stage, layer, 0)
                for g in range(NG):
                    for i in range(GT * g, GT * g + GT):
                        beside("T", layer, i, 0)
                        if i + 1 < NT:
                            scores_f(stage, layer, i + 1)
                        else:
                            turn_output(stage, layer, i - 1)
                        row(stage, layer, i)
                row(stage, layer, NT)

            expert_attention(STAGE_F0, 0)
            expert_attention(STAGE_F1, 1)

        @block.vector
        def _(dve):
            steps = [0]

            def after(ins):
                steps[0] += 1
                ins.then_inc(dve_step, 1)
                dve.wait_ge(dve_step, steps[0])

            def take(*key):
                dve.wait_ge(misc_ready, MISC.n(*key) + 1)

            def wide(col, shape):
                return col.broadcast_to(shape)

            def moments(stage, g):
                tiles = range(GT * g, GT * g + GT)
                a, b = GT * g, GT * g + GT
                if stage == STAGE_A:
                    dve.wait_ge(x_loaded[g], 16)
                else:
                    dve.wait_ge(x_new, x_new_n(stage - 1, g))
                for t in tiles:
                    last = dve.bn_stats(stats[:, t - a, :], X[:, t, :])
                after(last)
                for t in tiles:
                    last = dve.bn_aggr(mean_var[:, t, :], stats[:, t - a, :])
                after(last)
                dve.tensor_scalar(var_eps[:, a:b], mean_var[:, a:b, 1], EPS, None, ALU.add).then_inc(var_ready, 1)

            def normalise(stage, g):
                n = NORM.n(stage, g)
                dve.wait_ge(rstd_ready, n + 1)
                if n >= 2:
                    dve.wait_ge(misc_ready, MISC.n("xT", *NORM.keys[n - 2]) + 1)
                for t in range(GT * g, GT * g + GT):
                    last = dve.tensor_scalar(xn[:, GT * (n % 2) + t - GT * g, :], X[:, t, :], mean_var[:, t, 0:1], rstd[:, t:t + 1],
                                             ALU.subtract, ALU.mult)
                last.then_inc(xn_ready, 1)

            def split_part(part, src, outs, rest_out=None, first=None):
                for o, v in outs:
                    last = dve.tensor_copy(o, v)
                if rest_out is None:
                    return last
                after(last)
                after(dve.tensor_tensor(rest_out, src, first, ALU.subtract))

            def prep(g, step):
                a, b = GT * g, GT * g + GT
                if step == 0:
                    moments(STAGE_A, g)
                elif step == 1:
                    normalise(STAGE_A, g)
                elif step in (3, 4):
                    add_bias(g, step - 3)
                    if step == 4:
                        dve.wait_ge(proj_copied, 2 * (g + 1))
                        rotate(g)
                elif step == 5:
                    for part in range(PARTS):
                        k_part(g, part)
                elif step in (6, 7, 8):
                    q_part(g, step - 6)

            def add_bias(g, half):
                if g == 0 and half == 0:
                    dve.wait_ge(rot_loaded, 16 * 5)
                take("proj", g, half)
                w = D + 2 * HD
                dve.tensor_tensor(qkv[:, 2 * half:2 * half + 2, :],
                                  misc[:, 0:2 * w].rearrange("p (a b) -> p a b", a=2),
                                  b_qkv[:, :].rearrange("p (o b) -> p o b", o=1).broadcast_to([P, 2, w]),
                                  ALU.add).then_inc(proj_copied, 1)

            def rotate(g):
                a, b = GT * g, GT * g + GT
                qk = qkv[:, :, 0:D + HD].rearrange("p t (h d) -> p t h d", d=HD)
                q2 = HH // 2
                hs = [P, GT, H + 1, q2]
                c = cos_t[:, a:b, :].rearrange("p t (o d) -> p t o d", o=1)
                sn = sin_t[:, a:b, :].rearrange("p t (o d) -> p t o d", o=1)
                dve.tensor_tensor(turn_c[:, :, :, :], qk[:, :, :, 0:HH], c.broadcast_to([P, GT, H + 1, HH]), ALU.mult)
                dve.tensor_tensor(turn_s[:, :, :, 0:q2], qk[:, :, :, q2:HH], sn[:, :, :, 0:q2].broadcast_to(hs), ALU.mult)
                after(dve.tensor_tensor(turn_s[:, :, :, q2:HH], qk[:, :, :, 0:q2], sn[:, :, :, q2:HH].broadcast_to(hs), ALU.mult))
                dve.tensor_copy(v_ones[:, a:b, 0:HD], qkv[:, :, D + HD:D + 2 * HD])
                after(dve.tensor_tensor(qk[:, :, :, 0:HH], turn_c[:, :, :, :], turn_s[:, :, :, :], ALU.add))

            def k_part(g, part):
                if part == 0 and g:
                    dve.wait_ge(misc_ready, MISC.n("kT", g - 1) + 1)
                kp = k_parts[:, :, 0:QK_ROWS].rearrange("p t (a b d) -> p t a b d", a=PARTS, b=PARTS)
                src = rest[:, :, H, :] if part else qkv[:, :, D:D + HD]
                outs = [(kp[:, :, :, part, :],
                         src.rearrange("p t (o d) -> p t o d", o=1).broadcast_to([P, GT, PARTS, HD]))]
                if part < PARTS - 1:
                    split_part(part, src, outs, rest[:, :, H, :], kp[:, :, 0, part, :])
                else:
                    split_part(part, src, outs).then_inc(kparts_ready, 1)

            def q_part(g, part):
                if part == 0 and g >= 2:
                    dve.wait_ge(misc_ready, MISC.n("qT", GT * (g - 1) - 1, 1) + 1)
                s = GT * g % (2 * GT)
                qp = q_parts[:, s:s + GT, :, 0:QK_ROWS].rearrange("p t h (a b d) -> p t h a b d", a=PARTS, b=PARTS)
                src = rest[:, :, 0:H, :] if part else qkv[:, :, 0:D].rearrange("p t (h d) -> p t h d", d=HD)
                outs = [(qp[:, t, :, part, :, :],
                         src[:, t, :, :].rearrange("p h (o d) -> p h o d", o=1).broadcast_to([P, H, PARTS, HD]))
                        for t in range(GT)]
                if part < PARTS - 1:
                    split_part(part, src, outs, rest[:, :, 0:H, :], qp[:, :, :, part, 0, :])
                else:
                    split_part(part, src, outs).then_inc(qparts_ready, 1)

            def max_reduce(i, u):
                h0, nh, k0, nk = max_units(i)[u]
                n, pieces = MX_BASE[i] + u, max_pieces(i)
                o = m[:, h0:h0 + nh] if pieces == 1 else m_part[:, h0, u % pieces:u % pieces + 1]
                dve.wait_ge(mx_ready, n + 1)
                dve.tensor_reduce(o, mx_bank(n)[:, 0:nh * nk * P].rearrange("p (a b) -> p a b", a=nh),
                                  AX_X, ALU.max).then_inc(mx_free, 1)

            def shift_parts(i):
                dve.wait_ge(mx_free, MX_BASE[i + 1])
                if max_pieces(i) > 1:
                    after(dve.tensor_reduce(m[:, :], m_part[:, :, 0:max_pieces(i)], AX_X, ALU.max))
                mp = m_parts[:, i % 2, :, :]
                after(dve.tensor_scalar(mp[:, :, 0], m[:, :], -1.0, None, ALU.mult))
                after(dve.scalar_tensor_tensor(out=m_rest[:, 0, :], in0=m[:, :], scalar=-1.0, in1=mp[:, :, 0],
                                               op0=ALU.mult, op1=ALU.subtract))
                after(dve.tensor_copy(mp[:, :, 1], m_rest[:, 0, :]))
                after(dve.tensor_tensor(m_rest[:, 1, :], m_rest[:, 0, :], mp[:, :, 1], ALU.subtract))
                dve.tensor_copy(mp[:, :, 2], m_rest[:, 1, :]).then_inc(m_ready, 1)

            def shift_copy(i):
                take("shift", i, 1)
                dve.tensor_copy(qT[SHIFT_ROW:ST_ROWS, i % Q_RING, 1024:2048], misc_b[SHIFT_ROW:ST_ROWS, :])\
                    .then_inc(shift_set[1], 1)

            def finish_a(i, step):
                if step == 0:
                    take("oT", i)
                    o = misc.rearrange("p (a c d) -> p a c d", a=HB, c=HB)
                    after(dve.reciprocal(den[:, :, :], o[:, :, :, HD]))
                    dve.tensor_tensor(att[:, i % 2, :].rearrange("p (c a d) -> p a c d", c=HB, a=HB),
                                      o[:, :, :, 0:HD],
                                      den[:, :, :].rearrange("p a (c o) -> p a c o", o=1).broadcast_to([P, HB, HB, HD]),
                                      ALU.mult).then_inc(att_ready, 1)
                elif step == 2:
                    take("wo", i)
                    dve.tensor_tensor(wo_out[:, :], misc[:, 0:D], b_o[:, :], ALU.add).then_inc(wo_copied, 1)
                    dve.wait_ge(wo_copied, i + 1)
                    dve.tensor_tensor(X[:, i, :], X[:, i, :], wo_out[:, :], ALU.add).then_inc(x_new, 1)

            dve.memset(q_parts[:, :, :, QK_ROWS:QK_PAD], 0.0)
            dve.memset(k_parts[:, :, QK_ROWS:QK_PAD], 0.0)
            dve.memset(k_parts[:, :, SHIFT_ROW:ST_ROWS], 1.0)
            dve.memset(v_ones[:, :, HD:HD + 1], 1.0)
            after(dve.memset(v_ones[:, :, HD + 1:32], 0.0))
            def sim_step(step):
                if step == 0:
                    dve.wait_ge(tab_loaded, 16 * 3)
                    dve.tensor_tensor(sim_sq[:, :], sim_sb[:, :], sim_sb[:, :], ALU.mult).then_inc(sim_sq_ready, 1)
                elif step == 1:
                    take("sim")
                    dve.tensor_scalar(sim_sq[:, :], misc[:, 0:E], NORM_EPS, None, ALU.add).then_inc(sim_var, 1)
                elif step == 2:
                    dve.wait_ge(gates_exp, 1)
                    after(dve.tensor_scalar(gate_sig[:, :], gate_sig[:, :], 1.0, None, ALU.add))
                    after(dve.reciprocal(gate_sig[:, :], gate_sig[:, :]))
                    dve.wait_ge(sim_pow, 1)
                    dve.tensor_tensor(sim_n[:, :], sim_sb[:, :], sim_sq[:, :], ALU.mult).then_inc(sim_ready, 1)
                elif step == 3:
                    dve.wait_ge(b_loaded, 16 * 8)
                    after(dve.tensor_tensor(w_u[:, :, :], w_u[:, :, :], w_v[:, :, :], ALU.mult))
                    after(dve.tensor_reduce(w_uv[:, :], w_u[:, :, :], AX_X, ALU.add))
                    dve.tensor_tensor(w_tf[:, 0:PR], w_tf[:, 0:PR], w_uv[:, :], ALU.add).then_inc(wtf_ready, 1)

            def gates_of(layer, g):
                n = NG * layer + g
                eg = [P, GT, E]
                stage = FFN_STAGE[layer]
                if n == 0:
                    dve.wait_ge(consts, 4)
                a, b = GT * g, GT * g + GT
                take("logit", stage, g)
                dve.wait_ge(x_inv_ready, n + 1)
                dve.tensor_tensor(logits[:, :, :], misc[:, 0:GT * E].rearrange("p (t e) -> p t e", t=GT),
                                  x_inv[:, a:b].rearrange("p (t o) -> p t o", o=1).broadcast_to(eg),
                                  ALU.mult).then_inc(logit_copied, 1)
                dve.wait_ge(logit_copied, n + 1)
                after(dve.tensor_tensor(logits[:, :, :], logits[:, :, :],
                                        gate_sig[:, :].rearrange("p (o e) -> p o e", o=1).broadcast_to(eg), ALU.subtract))
                for t in range(GT):
                    last = dve.max(top[:, t, :], logits[:, t, :])
                after(last)
                for t in range(GT):
                    last = dve.max_index(top_no[:, t, :], top[:, t, :], logits[:, t, :])
                after(last)
                after(dve.tensor_copy(top_nof[:, :, :], top_no[:, :, 0:2]))
                numbers = expert_no[:, :].rearrange("p (o e) -> p o e", o=1).broadcast_to(eg)
                dve.tensor_tensor(pick[:, 0, :, :], numbers, top_nof[:, :, 0:1].broadcast_to(eg), ALU.is_equal)
                after(dve.tensor_tensor(pick[:, 1, :, :], numbers, top_nof[:, :, 1:2].broadcast_to(eg), ALU.is_equal))
                dve.tensor_tensor(pick[:, 0, :, :], pick[:, 0, :, :], pick[:, 1, :, :], ALU.add)
                dve.tensor_scalar(gcol[:, 0, :], top[:, :, 0], 0.0, None, ALU.is_le)
                after(dve.tensor_scalar(gcol[:, 1, :], top[:, :, 0], 0.0, None, ALU.max))
                dve.tensor_scalar(on[:, :, :], logits[:, :, :], 0.0, None, ALU.is_gt)
                dve.tensor_scalar(gtmp[:, :, :], logits[:, :, :], 0.0, None, ALU.max)
                col = lambda c: gcol[:, c, :].rearrange("p (t o) -> p t o", o=1).broadcast_to(eg)
                after(dve.tensor_tensor(pick[:, 0, :, :], pick[:, 0, :, :], col(0), ALU.mult))
                after(dve.tensor_tensor(on[:, :, :], on[:, :, :], pick[:, 0, :, :], ALU.add))
                dve.tensor_tensor(gtmp[:, :, :], gtmp[:, :, :], col(1), ALU.subtract).then_inc(gate_arg, 1)

            def gate_softmax(layer, g):
                n = NG * layer + g
                col = lambda c: gcol[:, c, :].rearrange("p (t o) -> p t o", o=1).broadcast_to([P, GT, E])
                dve.wait_ge(gate_exp, n + 1)
                w = rw[:, GT * g:GT * g + GT, :]
                after(dve.tensor_tensor(w, gexp[:, :, :], on[:, :, :], ALU.mult))
                after(dve.tensor_reduce(gcol[:, 2, :], w, AX_X, ALU.add))
                after(dve.reciprocal(gcol[:, 0, :], gcol[:, 2, :]))
                after(dve.tensor_tensor(w, w, col(0), ALU.mult))
                if n:
                    dve.wait_ge(misc_ready, MISC.n("rT", FFN_STAGE[(n - 1) // NG], (n - 1) % NG) + 1)
                for part in range(PARTS):
                    src = rw_rest[:, :, :] if part else w
                    o = rw_parts[:, :, part, :]
                    if part < PARTS - 1:
                        split_part(part, src, [(o, src)], rw_rest[:, :, :], o)
                    else:
                        split_part(part, src, [(o, src)]).then_inc(rparts_ready, 1)

            def scale_tile(k, weights, src):
                dve.wait_ge(rb_ready, k + 1)
                if k >= XS_RING:
                    dve.wait_ge(xs_lo_ready, k - XS_RING + 1)
                dve.tensor_tensor(xs[:, k % XS_RING, :], weights, src, ALU.mult).then_inc(xs_ready, 1)

            def scaled_low(k):
                dve.wait_ge(xs_hi_ready, k + 1)
                if k >= XS_HALVES_RING:
                    dve.wait_ge(xs_used, k - XS_HALVES_RING + 1)
                halves = xs_halves[:, k % XS_HALVES_RING, :, :]
                dve.tensor_tensor(halves[:, LO, :], xs[:, k % XS_RING, :], halves[:, HI, :].bitcast(F32),
                                  ALU.subtract).then_inc(xs_lo_ready, 1)

            def gate(layer, g, step):
                a, b = GT * g, GT * g + GT
                stage = FFN_STAGE[layer]
                if step == 0:
                    moments(stage, g)
                elif step == 1:
                    normalise(stage, g)
                    dve.wait_ge(xn_ready, NORM.n(stage, g) + 1)
                    for t in range(a, b):
                        row = xn[:, GT * (NORM.n(stage, g) % 2) + t - a, :]
                        last = dve.tensor_tensor_reduce(sq_junk[:, t - a, :], row, row, 1.0, 0.0,
                                                        ALU.mult, ALU.add, sq_sum[:, t:t + 1])
                    after(last)
                    dve.tensor_scalar(sq_sum[:, a:b], sq_sum[:, a:b], NORM_EPS, None, ALU.add).then_inc(sq_ready, 1)
                elif step == 3:
                    gates_of(layer, g)
                elif step == 4:
                    gate_softmax(layer, g)

            def add_to_x(g):
                a, b = GT * g, GT * g + GT
                dve.tensor_tensor(X[:, a:b, :], X[:, a:b, :], misc.rearrange("p (t d) -> p t d", t=GT),
                                  ALU.add).then_inc(x_new, 1)

            def scan(g, step):
                if step == 0:
                    moments(STAGE_B, g)
                elif step == 1:
                    normalise(STAGE_B, g)
                elif step == 4:
                    dve.wait_ge(fg_exp, g + 1)
                    dve.scalar_tensor_tensor(out=fg[PR:P, 0, :], in0=fg[PR:P, 0, :], scalar=1.0, in1=fg[PR:P, 1, :],
                                             op0=ALU.add, op1=ALU.mult).then_inc(fg_ready, 1)
                elif step == 6:
                    dve.wait_ge(lam_exp, g + 1)
                    after(dve.tensor_scalar(lam[:, 0, :], lam[:, 0, :], 0.5, 0.5, ALU.mult, ALU.add))
                    after(dve.tensor_tensor(lam[:, 0, :], lam[:, 0, :], lam[:, 1, :], ALU.mult))
                elif step == 7:
                    take("u", g)
                    if g:
                        dve.wait_ge(s_ready, g)
                    dve.tensor_tensor_scan(s_seq[:, GN * g:GN * g + GN], lam[:, 0, :], misc[0:PR, :],
                                           s_seq[:, GN * g - 1:GN * g] if g else 0.0, ALU.mult, ALU.add)\
                        .then_inc(s_ready, 1)
                elif step == 8:
                    take("c", g)
                    dve.tensor_tensor(tt[:, :], misc[0:PR, :], tT[:, :], ALU.add).then_inc(tt_ready, 1)
                elif step == 9:
                    take("h", g)
                    add_to_x(g)

            def beside(*place):
                for chain, at, step in SIDE.get(place, ()):
                    if chain == "shift" and step == 1:
                        shift_copy(*at)
                    elif chain == "finish" and step > 0:
                        finish_a(*at, step - 1)
                    elif chain == "prep":
                        prep(*at, step)
                    elif chain == "sim":
                        sim_step(step)
                    elif chain == "gate":
                        gate(*at, step)
                    elif chain == "scan":
                        scan(*at, step)

            for step in range(PREP_STEPS):
                prep(0, step)
            for u in range(len(max_units(0))):
                max_reduce(0, u)
            shift_parts(0)
            shift_copy(0)
            for slot in range(first_slot(NT)):
                beside("A", slot)
                for unit in MAX_PLAN[slot]:
                    max_reduce(*unit)
                for i in range(1, NT):
                    if slot == max_window(i)[1] - 1:
                        shift_parts(i)

            def project(stage, layer):
                for g in range(NG):
                    dve.wait_ge(xnT_ready, NORM.n(stage, g) + 1)
                    for e in range(E):
                        if (layer, g, e) == (1, 0, 4):
                            add_tile(0, NT - 1)
                        beside("P", layer, g, e)
                        k = xs_n(layer, g, e)
                        scale_tile(k, bank(k % 3), xnT[:, GN * g:GN * g + GN])
                        if g or e:
                            scaled_low(k - 1)
                scaled_low(xs_n(layer, NG - 1, E - 1))

            def max_f(layer, i):
                dve.wait_ge(fs_ready, NT * layer + i + 1)
                after(dve.tensor_reduce(fm[:, i:i + 1], psum[:, 0:P * (i + 1)], AX_X, ALU.max))
                dve.tensor_scalar(f_shift[:, i:i + 1], fm[:, i:i + 1], -SCALE_F, None, ALU.mult).then_inc(fshift_ready, 1)

            def sum_experts(stage, layer, i, c):
                dve.wait_ge(out_filled, (NT * layer + i) * GT + c + 1)
                if c == 0 and NT * layer + i > 1:
                    before = (layer, i - 2) if i > 1 else (layer - 1, NT + i - 2)
                    dve.wait_ge(x_new, NT + UPDATE.n(FFN_STAGE[before[0]], before[1]) + 1)
                ps = pair_bank(("out", stage, i, c))
                for e in range(OE * c, OE * c + OE):
                    n = scaled_n(layer, i, e)
                    o, src = out_sum[i % 2][:, e % 2, :], ps[:, D * (e % OE):D * (e % OE) + D]
                    if e < 2:
                        dve.tensor_scalar(o, src, rw[:, i, e:e + 1], None, ALU.mult).then_inc(out_scaled, 1)
                    else:
                        dve.wait_ge(out_scaled, n - 1)
                        dve.scalar_tensor_tensor(out=o, in0=src, scalar=rw[:, i, e:e + 1], in1=o,
                                                 op0=ALU.mult, op1=ALU.add).then_inc(out_scaled, 1)

            def add_tile(layer, i):
                dve.wait_ge(tile_summed, NT * layer + i + 1)
                dve.tensor_tensor(X[:, i, :], X[:, i, :], out_sum[i % 2][:, 0, :], ALU.add).then_inc(x_new, 1)

            def aoT_low(stage, layer, i):
                dve.wait_ge(aoT_hi_ready, NT * layer + i + 1)
                dve.tensor_tensor(aoT[:, LO, :], misc[:, 0:P], aoT[:, HI, :].bitcast(F32), ALU.subtract)\
                    .then_inc(aoT_ready, 1)

            def attend_f(layer, i):
                n = NT * layer + i
                dve.wait_ge(fprobs_ready, n + 1)
                after(dve.reciprocal(f_inv[:, i:i + 1], f_sum[:, i:i + 1]))
                dve.wait_ge(pT_used, weighed(layer, i))
                dve.tensor_scalar(ao[:, i % 2, :], bank(6)[:, 0:D], f_inv[:, i:i + 1], None, ALU.mult).then_inc(ao_ready, 1)

            def expert_attention(stage, layer):
                project(stage, layer)
                max_f(layer, 0)
                for g in range(NG):
                    for i in range(GT * g, GT * g + GT):
                        beside("T", layer, i, 0)
                        if i:
                            aoT_low(stage, layer, i - 1)
                        if i + 1 < NT:
                            max_f(layer, i + 1)
                        if i:
                            sum_experts(stage, layer, i - 1, 0)
                        if i > 1:
                            add_tile(layer, i - 2)
                        beside("T", layer, i, 1)
                        beside("T", layer, i, 2)
                        if i:
                            sum_experts(stage, layer, i - 1, 2)
                        attend_f(layer, i)
                        beside("T", layer, i, 3)
                aoT_low(stage, layer, NT - 1)
                for c in range(0, GT, SHARES):
                    sum_experts(stage, layer, NT - 1, c)
                add_tile(layer, NT - 2)
                if layer == 1:
                    add_tile(layer, NT - 1)

            expert_attention(STAGE_F0, 0)
            expert_attention(STAGE_F1, 1)


_INS = ["L0_attn_a_x", "L0_attn_a_Wq", "L0_attn_a_bq", "L0_attn_a_Wk", "L0_attn_a_bk", "L0_attn_a_Wv",
        "L0_attn_a_bv", "L0_attn_a_Wo", "L0_attn_a_bo", "L0_attn_b_W_toP", "L0_attn_b_W_U", "L0_attn_b_W_F",
        "L0_attn_b_W_V", "L0_attn_b_W_lam", "L0_attn_b_B_mat", "L0_attn_b_C_mat", "L0_attn_b_W_fromP",
        "L0_ffn_sim_matrix", "L0_ffn_gates", "L0_ffn_q_proj", "L0_ffn_k_proj", "L0_ffn_v_proj",
        "L0_ffn_o_proj"]
_OUTS = [((1, 2048, 128), "float32")]


def _rotation_tables():
    import numpy as np
    theta = np.float32(10000.0) ** (-np.arange(HH, dtype=np.float32) / np.float32(HH))
    angle = np.arange(T, dtype=np.float32)[:, None] * theta[None, :].astype(np.float32)
    sign = np.where(np.arange(HH) < HH // 2, -1.0, 1.0).astype(np.float32)
    tables = np.cos(angle).astype(np.float32), (np.sin(angle) * sign).astype(np.float32)
    return [np.ascontiguousarray(a.reshape(NT, P, HH).transpose(1, 0, 2)) for a in tables]


def kernel(**inputs):
    import numpy as _np
    import concourse.bacc as _bacc
    from concourse import mybir as _mybir
    from concourse.bass_utils import run_bass_kernel_spmd as _run

    nc = _bacc.Bacc("TRN2", target_bir_lowering=False, num_devices=1)
    cos, sin = _rotation_tables()
    named = [(name, inputs[name]) for name in _INS] + [("cos", cos), ("sin", sin)]
    arrays, args = {}, []
    for name, value in named:
        a = _np.ascontiguousarray(value)
        arrays[f"in_{name}_dram"] = a
        args.append(nc.dram_tensor(f"in_{name}_dram", a.shape, _mybir.dt.from_np(a.dtype), kind="ExternalInput").ap())
    for i, (shape, dtype) in enumerate(_OUTS):
        dt = _mybir.dt.from_np(_np.dtype(dtype))
        args.append(nc.dram_tensor(f"out_{i}_dram", shape, dt, kind="ExternalOutput").ap())
    hybrid_block_kernel(nc, *args)
    r = _run(nc, [arrays], core_ids=[0])
    return r.results[0]["out_0_dram"]
```
